# Optimizing a Trainium2 kernel written in Bass

```python
import numpy as np
import jax
import jax.numpy as jnp

def _softmax(x, axis=-1):
    return jax.nn.softmax(x, axis=axis)

def _gelu(x):
    return jax.nn.gelu(x, approximate=True)

def _silu(x):
    return jax.nn.silu(x)

def _sigmoid(x):
    return jax.nn.sigmoid(x)

def _layernorm(x, axis=-1, eps=1e-05):
    m = jnp.mean(x, axis=axis, keepdims=True)
    v = jnp.var(x, axis=axis, keepdims=True)
    return (x - m) / jnp.sqrt(v + eps)

def _scatter_add(tgt, idx, src, axis=0):
    return tgt.at[idx].add(src)

def _segment_sum(src, seg, n):
    return jax.ops.segment_sum(src, seg, n)
kernel_name = 'mk_adaln_d1_jaxref_r8_50706b'

def setup_inputs(seed: int=0):
    np.random.seed(seed)
    _w = jnp.asarray

    def _L0_attn_setup():
        import jax, jax.numpy as jnp
        import numpy as np
        D_STATE = 16
        DT_RANK = 6
        EPS = 1e-05

        def layer_norm(x, w, b):
            mu = jnp.mean(x, axis=-1, keepdims=True)
            var = jnp.mean((x - mu) ** 2, axis=-1, keepdims=True)
            return (x - mu) * jax.lax.rsqrt(var + EPS) * w + b

        def selective_scan(u, delta, A, Bp, Cp, Dp):
            delta_A = jnp.exp(jnp.einsum('bld,dn->bldn', delta, A))
            delta_B_u = jnp.einsum('bld,bln,bld->bldn', delta, Bp, u)
            Bsz, L, D = u.shape

            def step(x, inp):
                dA_t, dBu_t, C_t = inp
                x = dA_t * x + dBu_t
                y = jnp.einsum('bdn,bn->bd', x, C_t)
                return (x, y)
            x0 = jnp.zeros((Bsz, D, D_STATE), dtype=u.dtype)
            xs = (jnp.swapaxes(delta_A, 0, 1), jnp.swapaxes(delta_B_u, 0, 1), jnp.swapaxes(Cp, 0, 1))
            _, ys = jax.lax.scan(step, x0, xs)
            y = jnp.swapaxes(ys, 0, 1)
            return y + u * Dp

        def ssm(x, x_proj_W, dt_proj_W, dt_proj_b, A_log, D_param):
            A = -jnp.exp(A_log.astype(jnp.float32))
            dbc = x @ x_proj_W.T
            delta_r = dbc[..., :DT_RANK]
            Bp = dbc[..., DT_RANK:DT_RANK + D_STATE]
            Cp = dbc[..., DT_RANK + D_STATE:]
            delta = jax.nn.softplus(delta_r @ dt_proj_W.T + dt_proj_b) * 0.001
            return selective_scan(x, delta, A, Bp, Cp, D_param.astype(jnp.float32))
        key = jax.random.key(seed)
        ks = jax.random.split(key, 10)
        B, L, C, Din = (16, 256, 256, 96)
        A = jnp.tile(jnp.arange(1, D_STATE + 1, dtype=jnp.float32)[None, :], (Din, 1))
        return {'feat_patch': jax.random.normal(ks[0], (B, L, C), dtype=jnp.float32), 'ln_w': jnp.ones((C,), jnp.float32), 'ln_b': jnp.zeros((C,), jnp.float32), 'in_proj_W': jax.random.normal(ks[1], (Din, C), jnp.float32) * (1.0 / np.sqrt(C)), 'conv_w': jax.random.normal(ks[2], (Din, 1, 3), jnp.float32) * 0.3, 'conv_b': jnp.zeros((Din,), jnp.float32), 'x_proj_W': jax.random.normal(ks[3], (DT_RANK + 2 * D_STATE, Din), jnp.float32) * (1.0 / np.sqrt(Din)), 'dt_proj_W': jax.random.normal(ks[4], (Din, DT_RANK), jnp.float32) * (1.0 / np.sqrt(DT_RANK)), 'dt_proj_b': jnp.zeros((Din,), jnp.float32), 'A_log': jnp.log(A), 'D_param': jnp.ones((Din,), jnp.float32), 'out_proj_W': jax.random.normal(ks[5], (C, Din), jnp.float32) * (1.0 / np.sqrt(Din))}
    _L0_attn_in = _L0_attn_setup()

    def _L0_ffn_setup():
        import jax, jax.numpy as jnp
        import numpy as np
        E, H, I = (8, 256, 512)
        TOP_K = 1
        B, S = (1, 256)
        key = jax.random.key(seed)
        ks = jax.random.split(key, 7)
        std = 0.02
        return {'hidden_states': jax.random.normal(ks[0], (B, S, H), dtype=jnp.float32), 'router_w': jax.random.normal(ks[1], (E, H), dtype=jnp.float32) * std, 'gate_up_proj': jax.random.normal(ks[2], (E, H, 2 * I), dtype=jnp.float32) * std, 'down_proj': jax.random.normal(ks[3], (E, I, H), dtype=jnp.float32) * std, 'shared_gate_w': jax.random.normal(ks[4], (H, I), dtype=jnp.float32) * std, 'shared_up_w': jax.random.normal(ks[5], (H, I), dtype=jnp.float32) * std, 'shared_down_w': jax.random.normal(ks[6], (I, H), dtype=jnp.float32) * std}
    _L0_ffn_in = _L0_ffn_setup()
    _L0_c = _w((lambda *s: np.random.randn(*s).astype(np.float32) * 0.05)(2, 256))
    _L0_wmod = _w((lambda *s: np.random.randn(*s).astype(np.float32) * 0.05)(256, 6 * 256) * 256 ** (-0.5))
    _d = {'L0_attn_feat_patch': _L0_attn_in['feat_patch'], 'L0_attn_ln_w': _L0_attn_in['ln_w'], 'L0_attn_ln_b': _L0_attn_in['ln_b'], 'L0_attn_in_proj_W': _L0_attn_in['in_proj_W'], 'L0_attn_conv_w': _L0_attn_in['conv_w'], 'L0_attn_conv_b': _L0_attn_in['conv_b'], 'L0_attn_x_proj_W': _L0_attn_in['x_proj_W'], 'L0_attn_dt_proj_W': _L0_attn_in['dt_proj_W'], 'L0_attn_dt_proj_b': _L0_attn_in['dt_proj_b'], 'L0_attn_A_log': _L0_attn_in['A_log'], 'L0_attn_D_param': _L0_attn_in['D_param'], 'L0_attn_out_proj_W': _L0_attn_in['out_proj_W'], 'L0_ffn_router_w': _L0_ffn_in['router_w'], 'L0_ffn_gate_up_proj': _L0_ffn_in['gate_up_proj'], 'L0_ffn_down_proj': _L0_ffn_in['down_proj'], 'L0_ffn_shared_gate_w': _L0_ffn_in['shared_gate_w'], 'L0_ffn_shared_up_w': _L0_ffn_in['shared_up_w'], 'L0_ffn_shared_down_w': _L0_ffn_in['shared_down_w'], 'L0_c': _L0_c, 'L0_wmod': _L0_wmod}
    _x0 = _d['L0_attn_feat_patch']
    _d['L0_attn_feat_patch'] = jax.random.normal(jax.random.fold_in(jax.random.key(seed), 1), (2, 2048, 256), dtype=_x0.dtype)
    del _x0
    return _d

def reference(L0_attn_feat_patch, L0_attn_ln_w, L0_attn_ln_b, L0_attn_in_proj_W, L0_attn_conv_w, L0_attn_conv_b, L0_attn_x_proj_W, L0_attn_dt_proj_W, L0_attn_dt_proj_b, L0_attn_A_log, L0_attn_D_param, L0_attn_out_proj_W, L0_ffn_router_w, L0_ffn_gate_up_proj, L0_ffn_down_proj, L0_ffn_shared_gate_w, L0_ffn_shared_up_w, L0_ffn_shared_down_w, L0_c, L0_wmod):

    def _L0_attn_ref(feat_patch, ln_w, ln_b, in_proj_W, conv_w, conv_b, x_proj_W, dt_proj_W, dt_proj_b, A_log, D_param, out_proj_W):
        import jax, jax.numpy as jnp
        import numpy as np
        D_STATE = 16
        DT_RANK = 6
        EPS = 1e-05

        def layer_norm(x, w, b):
            mu = jnp.mean(x, axis=-1, keepdims=True)
            var = jnp.mean((x - mu) ** 2, axis=-1, keepdims=True)
            return (x - mu) * jax.lax.rsqrt(var + EPS) * w + b

        def selective_scan(u, delta, A, Bp, Cp, Dp):
            delta_A = jnp.exp(jnp.einsum('bld,dn->bldn', delta, A))
            delta_B_u = jnp.einsum('bld,bln,bld->bldn', delta, Bp, u)
            Bsz, L, D = u.shape

            def step(x, inp):
                dA_t, dBu_t, C_t = inp
                x = dA_t * x + dBu_t
                y = jnp.einsum('bdn,bn->bd', x, C_t)
                return (x, y)
            x0 = jnp.zeros((Bsz, D, D_STATE), dtype=u.dtype)
            xs = (jnp.swapaxes(delta_A, 0, 1), jnp.swapaxes(delta_B_u, 0, 1), jnp.swapaxes(Cp, 0, 1))
            _, ys = jax.lax.scan(step, x0, xs)
            y = jnp.swapaxes(ys, 0, 1)
            return y + u * Dp

        def ssm(x, x_proj_W, dt_proj_W, dt_proj_b, A_log, D_param):
            A = -jnp.exp(A_log.astype(jnp.float32))
            dbc = x @ x_proj_W.T
            delta_r = dbc[..., :DT_RANK]
            Bp = dbc[..., DT_RANK:DT_RANK + D_STATE]
            Cp = dbc[..., DT_RANK + D_STATE:]
            delta = jax.nn.softplus(delta_r @ dt_proj_W.T + dt_proj_b) * 0.001
            return selective_scan(x, delta, A, Bp, Cp, D_param.astype(jnp.float32))
        residual = feat_patch
        x = layer_norm(feat_patch, ln_w, ln_b)
        x = x @ in_proj_W.T
        x_ncl = jnp.swapaxes(x, 1, 2)
        x_ncl = jax.lax.conv_general_dilated(x_ncl, conv_w, window_strides=(1,), padding=((1, 1),), dimension_numbers=('NCH', 'OIH', 'NCH'), feature_group_count=96)
        x_ncl = x_ncl + conv_b[None, :, None]
        x = jnp.swapaxes(x_ncl, 1, 2)
        x = jax.nn.silu(x)
        y = ssm(x, x_proj_W, dt_proj_W, dt_proj_b, A_log, D_param)
        out = y @ out_proj_W.T
        return out + residual

    def _L0_ffn_ref(hidden_states, router_w, gate_up_proj, down_proj, shared_gate_w, shared_up_w, shared_down_w):
        import jax, jax.numpy as jnp
        import numpy as np
        E, H, I = (8, 256, 512)
        TOP_K = 1
        B, S = (1, 256)
        orig_shape = hidden_states.shape
        x = hidden_states.reshape(-1, H)
        T = x.shape[0]
        logits = x @ router_w.T
        top_vals, top_idx = jax.lax.top_k(logits, TOP_K)
        scores = jnp.full_like(logits, -jnp.inf)
        scores = scores.at[jnp.arange(T)[:, None], top_idx].set(top_vals)
        scores = jax.nn.sigmoid(scores.astype(jnp.float32)).astype(logits.dtype)
        xr = x[None, :, :] * scores.T[:, :, None]
        gate_up = jnp.einsum('eth,ehf->etf', xr, gate_up_proj)
        gate, up = jnp.split(gate_up, 2, axis=-1)
        routed = jnp.einsum('etf,efh->eth', up * jax.nn.silu(gate), down_proj)
        routed_sum = routed.sum(axis=0)
        shared = jax.nn.silu(x @ shared_gate_w) * (x @ shared_up_w) @ shared_down_w
        return (shared + routed_sum).reshape(orig_shape)
    x = L0_attn_feat_patch
    mod = (_silu(L0_c) @ L0_wmod).reshape(L0_c.shape[0], 6, 1, -1)
    sa, ca, ga, sb, cb, gb = (mod[:, 0], mod[:, 1], mod[:, 2], mod[:, 3], mod[:, 4], mod[:, 5])
    ga = (2 * (ga >= 0) - 1) * jnp.maximum(jnp.abs(ga), 0.25)
    gb = (2 * (gb >= 0) - 1) * jnp.maximum(jnp.abs(gb), 0.25)
    h = _layernorm(x, axis=-1) * (1 + ca) + sa
    x = x + ga * _L0_attn_ref(h, L0_attn_ln_w, L0_attn_ln_b, L0_attn_in_proj_W, L0_attn_conv_w, L0_attn_conv_b, L0_attn_x_proj_W, L0_attn_dt_proj_W, L0_attn_dt_proj_b, L0_attn_A_log, L0_attn_D_param, L0_attn_out_proj_W)
    h = _layernorm(x, axis=-1) * (1 + cb) + sb
    x = x + gb * _L0_ffn_ref(h, L0_ffn_router_w, L0_ffn_gate_up_proj, L0_ffn_down_proj, L0_ffn_shared_gate_w, L0_ffn_shared_up_w, L0_ffn_shared_down_w)
    return x

_drawn_inputs = setup_inputs


def setup_inputs(seed=0):
    import zlib

    import numpy as np

    out = dict(_drawn_inputs(seed))
    spreads = {'L0_attn_ln_w': (1.0, 0.6),
     'L0_attn_ln_b': (0.0, 0.617),
     'L0_attn_conv_b': (0.0, 0.531),
     'L0_attn_dt_proj_b': (0.0, 0.8),
     'L0_attn_D_param': (1.0, 0.6)}
    factors = {'L0_attn_x_proj_W': 8.0,
     'L0_attn_dt_proj_W': 8.0,
     'L0_attn_A_log': 8.0,
     'L0_ffn_router_w': 8.0,
     'L0_ffn_gate_up_proj': 8.0,
     'L0_ffn_down_proj': 8.0,
     'L0_ffn_shared_gate_w': 8.0,
     'L0_ffn_shared_up_w': 8.0,
     'L0_ffn_shared_down_w': 8.0}
    for name, (base, spread) in spreads.items():
        noise = np.random.default_rng([zlib.crc32(name.encode()), seed]).standard_normal(out[name].shape)
        drawn = base * np.exp(spread * noise) if base else spread * noise
        out[name] = jnp.asarray(drawn.astype(out[name].dtype))
    for name, factor in factors.items():
        out[name] = (out[name] * factor).astype(out[name].dtype)
    return out
```

```python
import concourse.bass as bass
from concourse import mybir
from contextlib import ExitStack

F32 = mybir.dt.float32
BF16 = mybir.dt.bfloat16
I32 = mybir.dt.int32
ALU = mybir.AluOpType
ACT = mybir.ActivationFunctionType
AX = mybir.AxisListType

P = 128
B, L, D = 2, 2048, 256
DI, NS, RK = 96, 16, 6
E, FF = 8, 512
KD, KF = D // P, FF // P
CH = 512
NC = L // CH
TPC = CH // P
U = B * TPC
NT = B * L // P
D1A = P - DI
D1B = DI - D1A
NA, NB = NS, NS // 2
NTILE = NA + NB
RT = NT + E - 1
SR = 3 * B * NS
EW = KD * 2 * FF + KF * D
EPS = 1e-5
GS = 8
SA, CA, GA, SB, CB, GB = range(6)


class Chain:

    def __init__(self, eng, sem):
        self.eng, self.sem, self.off, self.n = eng, sem, 0, 0
        self.met = None

    def inc(self, ins):
        ins.then_inc(self.sem, 1)
        self.n += 1
        return self.n

    def wait(self, n=None):
        self.eng.wait_ge(self.sem, self.off + (self.n if n is None else n))
        if self.met is not None:
            self.eng.sem_inc(self.met, 1)

    def link(self, ins):
        self.inc(ins)
        self.wait()

    def loop(self, base, it, per):
        self.off, self.n = base + it * per, 0

    def end(self, base, per, times):
        assert self.n == per, ("steps of the loop", self.n, per)
        self.off, self.n = 0, base + per * times


def flat(ap):
    return ap.rearrange("p a n -> p (a n)")


def adaln_block(nc, x, lnw, lnb, inW, convw, convb, xW, dtW, dtb, alog, dpar, outW, rW, guW, dnW,
                sgW, suW, sdW, cond, wmod, consts, selc, out):
    ctx = ExitStack()
    with ctx:
        def sb(name, shape, dt=F32):
            return ctx.enter_context(nc.sbuf_tensor(name, shape, dt))

        def sem(name):
            return ctx.enter_context(nc.semaphore(name))

        xs = nc.dram_tensor("xs_sorted", [RT * P, D], F32, kind="Internal").ap()
        ys = nc.dram_tensor("ys_sorted", [RT * P, D], F32, kind="Internal").ap()

        R = sb("R", [P, NT, D])
        H = sb("H", [P, NT, D])
        WR = sb("WR", [P, E * EW])
        WS = sb("WS", [P, EW])
        MODB = sb("MODB", [P, B, 3, D])
        CST = sb("CST", [P, 2 * P + E * NT + RT])
        ident = CST[:, 0:P]
        ltri = CST[:, P:2 * P]
        jrow = CST[:, 2 * P:2 * P + E * NT].rearrange("p (e j) -> p e j", e=E)
        jtile = CST[:, 2 * P + E * NT:2 * P + E * NT + RT]
        hT = sb("hT", [P, 2, KD, P])
        sg = sb("sg", [P, 2, FF])
        av = sb("av", [P, 2, FF])
        aT = sb("aT", [P, 2, KF, P])
        tmp = sb("tmp", [P, 2, D])
        yb = sb("yb", [P, 2, D])
        h2s = sb("h2s", [P, 2, D])
        st = sb("st", [P, U, 6])
        mv = sb("mv", [P, 2, U, 2])
        rs = sb("rs", [P, 2, U])
        nm = sb("nm", [P, 2, U])
        LG = sb("LG", [P, NT, E])
        wrT = sb("wrT", [P, KD, E])
        posi = sb("posi", [P, NT], I32)
        eidi = sb("eidi", [P, RT], I32)
        S1 = sb("S1", [P, NT])
        zero = sb("zero", [P, D])
        one = sb("one", [P, P])

        at = [0]

        def carve(*shape):
            n = 1
            for s in shape:
                n *= s
            ap = WR[:, at[0]:at[0] + n]
            at[0] += n
            if len(shape) == 1:
                return ap
            names = "abcd"[:len(shape)]
            return ap.rearrange(f"p ({' '.join(names)}) -> p {' '.join(names)}",
                                **{k: v for k, v in zip(names, shape)})

        XIN = carve(2, L + 2)
        MODA = carve(B, 3, D)
        winT = carve(3, KD, P)
        wxBT, wxCT = carve(2, SR), carve(2, SR)
        wxDT = carve(2, B * RK)
        wdtT = carve(2, P)
        woutT = carve(3, D)
        par = carve(2, 6)
        Apar = carve(NTILE)
        state = carve(NTILE)
        lnwc, lnbc = carve(KD), carve(KD)
        bia = carve(2)
        uu = carve(2, CH)
        dl = carve(2, CH)
        ww = carve(2, CH)
        cv = carve(2, CH)
        ysb = carve(2, CH)
        dr = carve(CH)
        spl = carve(3, CH)
        sel = carve(NTILE * P // 2).bitcast(BF16).rearrange("p (t c) -> p t c", t=NTILE)
        BsCs = carve(CH).bitcast(BF16).rearrange("p (a c) -> p a c", a=2)
        mid = carve(CH // 2).bitcast(BF16)
        base_dyn = at[0]
        dA = carve(2, CH)
        cs = carve(2, CH)
        hs = carve(2, CH)
        g = carve(2, CH)
        et = carve(2, CH)
        assert at[0] <= E * EW
        at[0] = base_dyn
        z = carve(U, D)
        zT = carve(B, KD, CH)
        assert at[0] <= E * EW

        HF = H[:, :, :].rearrange("p t d -> p (t d)")
        inR = HF[:, 0:3 * D].rearrange("p (k d) -> p k d", k=3)
        xR = HF[:, 768:768 + 6 * P].rearrange("p (m x d) -> p m x d", m=3, x=2)
        dtR = HF[:, 1536:1536 + 2 * B * RK].rearrange("p (x r) -> p x r", x=2)
        outR = HF[:, 1600:1600 + 3 * KD * P].rearrange("p (k m d) -> p k m d", k=KD, m=3)
        rR = HF[:, 2368:2368 + D]
        cT = HF[:, 2624:2624 + KD * B].rearrange("p (k b) -> p k b", k=KD)
        scT = HF[:, 2628:2628 + KD * B].rearrange("p (k b) -> p k b", k=KD)
        cB = HF[:, 2632:2632 + KD * B * P].rearrange("p (k b n) -> p k b n", k=KD, b=B)

        PS = ctx.enter_context(nc.psum_tensor("PS", [P, 8, CH], F32))

        names = ("z0 ab rt holda holdv holdp x sm wt wm cst ws wr xsz "
                 "d0 dch ach pch a0 t0 e0 w0 b0 m0 m1 "
                 "rv1 sq1 nm1 n1 h1 rv2 sq2 nm2 z1 zt zev xin xev "
                 "cv u dbc drr zz sp r1 dlt bs bb cb da cs sc g st y ye o x1 r0 "
                 "rv3 sq3 nm3 n3 h2 h3 ht htv gu sgs a atp atv y3 r3 lgc "
                 "oh rk pos s1 xr scd xt0 xt1 ht5 htv5 gu5 sg5 a5 at5 atv5 y5 yb5 ysd0 ysd1 fin od").split() + [f"gt{i}" for i in range(GS)]
        S = {n: sem("s_" + n) for n in names}
        WM = HF[:, NT * D - KD * 3 * D * 2:NT * D].rearrange("p (k n) -> p k n", k=KD)
        SELF = WR[:, base_dyn:base_dyn + NTILE * P]

        block = ctx.enter_context(nc.Block())

        def tok(c, u):
            return (u // TPC) * (NT // B) + c * TPC + u % TPC

        def Rt(c, u):
            return flat(R[:, bass.ds(tok(c, u), 1), :])

        def Ht(c, u):
            return flat(H[:, bass.ds(tok(c, u), 1), :])

        def wgu(W, k, half):
            return W[:, k * 2 * FF + half * FF:k * 2 * FF + (half + 1) * FF]

        def wdn(W, k):
            return W[:, KD * 2 * FF + k * D:KD * 2 * FF + (k + 1) * D]

        SMALL = [0]

        @block.sync
        def _(sp):
            def small(dst, src):
                sp.dma_start(dst, src).then_inc(S["sm"], 16)
                SMALL[0] += 16

            xv = x.rearrange("b (j p) d -> p b j d", p=P)
            for b in range(B):
                sp.dma_start(R[:, b * NT // B:(b + 1) * NT // B, :], xv[:, b]).then_inc(S["x"], 16)
            sp.dma_start(CST[:, :], consts).then_inc(S["cst"], 16)
            sp.dma_start(SELF[0:SR, :], selc).then_inc(S["cst"], 16)
            sp.dma_start(WM, wmod.rearrange("(k p) n -> p k n", p=P)).then_inc(S["wm"], 16)
            for k in range(KD):
                for b in range(B):
                    sp.dma_start(cT[:, k, b:b + 1], cond[b, k * P:(k + 1) * P].rearrange("(p a) -> p a", a=1)) \
                        .then_inc(S["wm"], 16)
            sp.wait_ge(S["z0"], 1)
            small(inR[0:DI, 0, :], inW)
            small(inR[DI:P, 1, :], inW[0:D1A, :])
            small(inR[0:D1B, 2, :], inW[D1A:DI, :])
            small(inR[D1B:P, 2, :], inW[D1A:DI, :])
            for m in range(2):
                r0 = RK + m * NS
                for rep in range(3):
                    q = rep * B * NS
                    small(xR[q:q + NS, m, 0, 0:DI], xW[r0:r0 + NS, :])
                    small(xR[q + NS:q + 2 * NS, m, 0, DI:P], xW[r0:r0 + NS, 0:D1A])
                    small(xR[q + NS:q + 2 * NS, m, 1, 0:D1B], xW[r0:r0 + NS, D1A:DI])
            small(xR[0:RK, 2, 0, 0:DI], xW[0:RK, :])
            small(xR[RK:2 * RK, 2, 0, DI:P], xW[0:RK, 0:D1A])
            small(xR[RK:2 * RK, 2, 1, 0:D1B], xW[0:RK, D1A:DI])
            small(dtR[0:DI, 0, 0:RK], dtW)
            small(dtR[DI:P, 0, RK:2 * RK], dtW[0:D1A, :])
            small(dtR[0:D1B, 1, RK:2 * RK], dtW[D1A:DI, :])
            small(dtR[D1B:P, 1, RK:2 * RK], dtW[D1A:DI, :])
            ov = outW.rearrange("(k p) d -> p k d", p=P)
            small(outR[:, :, 0, 0:DI], ov)
            small(outR[:, :, 1, DI:P], ov[:, :, 0:D1A])
            small(outR[:, :, 2, 0:D1B], ov[:, :, D1A:DI])
            small(outR[:, :, 2, D1B:P], ov[:, :, D1A:DI])
            small(rR[0:E, :], rW)
            for k in range(KD):
                small(lnwc[:, k:k + 1], lnw[k * P:(k + 1) * P].rearrange("(p a) -> p a", a=1))
                small(lnbc[:, k:k + 1], lnb[k * P:(k + 1) * P].rearrange("(p a) -> p a", a=1))

            def rows(x_, p0, p1, d0):
                n = p1 - p0
                small(par[p0:p1, x_, 0:3], convw[d0:d0 + n, 0, :])
                small(par[p0:p1, x_, 3:4], convb[d0:d0 + n].rearrange("(p a) -> p a", a=1))
                small(par[p0:p1, x_, 4:5], dtb[d0:d0 + n].rearrange("(p a) -> p a", a=1))
                if not (x_ == 1 and p0 > 0):
                    small(par[p0:p1, x_, 5:6], dpar[d0:d0 + n].rearrange("(p a) -> p a", a=1))

            rows(0, 0, DI, 0)
            rows(0, DI, P, 0)
            rows(1, 0, D1B, D1A)
            rows(1, D1B, P, D1A)
            small(Apar[0:DI, 0:NA], alog)
            small(Apar[DI:P, 0:NA], alog[0:D1A, :])
            small(Apar[0:D1B, NA:NTILE], alog[D1A:DI, 0:NB])
            small(Apar[D1B:P, NA:NTILE], alog[D1A:DI, NB:NS])

            for k in range(KD):
                sp.dma_start(wgu(WS, k, 0), sgW[k * P:(k + 1) * P, :]).then_inc(S["ws"], 16)
                sp.dma_start(wgu(WS, k, 1), suW[k * P:(k + 1) * P, :]).then_inc(S["ws"], 16)
            sp.dma_start(WS[:, KD * 2 * FF:EW].rearrange("p (k n) -> p k n", k=KF),
                         sdW.rearrange("(k p) n -> p k n", p=P)).then_inc(S["ws"], 16)
            for t in range(RT):
                sp.dma_start(xs[t * P:(t + 1) * P, :], zero[:, :]).then_inc(S["xsz"], 16)
            sp.wait_ge(S["x1"], NT)
            sp.wait_ge(S["st"], NC * NTILE)
            for e in range(E):
                We = WR[:, e * EW:(e + 1) * EW]
                sp.dma_start(We[:, 0:KD * 2 * FF].rearrange("p (k n) -> p k n", k=KD),
                             guW[e].rearrange("(k p) n -> p k n", p=P)).then_inc(S["wr"], 16)
                sp.dma_start(We[:, KD * 2 * FF:EW].rearrange("p (k n) -> p k n", k=KF),
                             dnW[e].rearrange("(k p) n -> p k n", p=P)).then_inc(S["wr"], 16)
            sp.wait_ge(S["scd"], 16 * NT)

            def load(t, slot):
                sp.dma_start(tmp[:, slot, :], xs[bass.ds(t * P, P), :]).then_inc(S[f"xt{slot}"], 16)

            def store(t, slot):
                sp.wait_ge(S["yb5"], t + 1)
                sp.dma_start(ys[bass.ds(t * P, P), :], yb[:, slot, :]).then_inc(S[f"ysd{slot}"], 16)

            for t in range(5):
                if t >= 2:
                    sp.wait_ge(S["ht5"], t - 1)
                load(t, t % 2)
            with sp.Fori(0, (RT - 5) // 2) as k:
                for s in range(2):
                    sp.wait_ge(S["ht5"], k * 2 + (4 + s))
                    load(k * 2 + (5 + s), (5 + s) % 2)
                    store(k * 2 + s, s)
            for t in range(RT - 5, RT):
                store(t, t % 2)

        @block.gpsimd
        def _(gp):
            ch = Chain(gp, S["pch"])
            gp.wait_ge(S["m1"], 1)
            ch.met = S["holdp"]
            b0 = ch.n
            with gp.Fori(0, NC) as c:
                ch.loop(b0, c, 2 * U)
                for u in range(U):
                    gp.wait_ge(S["h1"], c * U + u + 1)
                    gp.sem_inc(S["holdp"], 1)
                    ch.link(nc.gpsimd.tensor_tensor(tmp[:, u % 2, :], Ht(c, u),
                                                    MODA[:, u // TPC, GA, :], ALU.mult))
                    ch.link(nc.gpsimd.tensor_tensor(Rt(c, u), Rt(c, u), tmp[:, u % 2, :], ALU.add))
            ch.end(b0, 2 * U, NC)
            gp.sem_inc(S["r0"], 1)
            with gp.Fori(0, NC) as c:
                for i in range(NTILE):
                    gp.wait_ge(S["sc"], c * NTILE + i + 1)
                    gp.wait_ge(S["cs"], c * NTILE + i + 1)
                    if i >= 2:
                        gp.wait_ge(S["y"], c * NTILE + i - 1)
                    nc.gpsimd.tensor_tensor(g[:, i % 2, :], hs[:, i % 2, :], cs[:, i % 2, :], ALU.mult) \
                        .then_inc(S["g"], 1)
                    nc.gpsimd.tensor_copy(state[:, i:i + 1], hs[:, i % 2, CH - 1:CH]).then_inc(S["st"], 1)
            b0 = ch.n
            with gp.Fori(0, NC) as c:
                ch.loop(b0, c, U)
                for u in range(U):
                    gp.wait_ge(S["n3"], c * U + u + 1)
                    gp.sem_inc(S["holdp"], 1)
                    ch.link(nc.gpsimd.tensor_tensor(Ht(c, u), Ht(c, u), MODB[:, u // TPC, CB - 3, :], ALU.mult))
                    if u >= 2:
                        gp.wait_ge(S["ht"], c * U + u - 1)
                        gp.sem_inc(S["holdp"], 1)
                    nc.gpsimd.tensor_tensor(h2s[:, u % 2, :], Ht(c, u), MODB[:, u // TPC, SB - 3, :], ALU.add) \
                        .then_inc(S["h2"], 1)
                    gp.wait_ge(S["h2"], c * U + u + 1)
                    gp.sem_inc(S["holdp"], 1)
                    nc.gpsimd.tensor_tensor(Ht(c, u), Ht(c, u), MODB[:, u // TPC, SB - 3, :], ALU.add) \
                        .then_inc(S["h3"], 1)
            ch.end(b0, U, NC)
            gp.wait_ge(S["pos"], 1)
            gp.wait_ge(S["xsz"], 16 * RT)
            for t in range(NT):
                gp.wait_ge(S["xr"], t + 1)
                gp.indirect_dma_start(out=xs[:, :], out_offset=bass.IndirectOffsetOnAxis(ap=posi[:, t:t + 1], axis=0),
                                      in_=H[:, t, :], in_offset=None).then_inc(S["scd"], 16)
            gp.wait_ge(S["ysd0"], 16 * ((RT + 1) // 2))
            gp.wait_ge(S["ysd1"], 16 * (RT // 2))
            for t in range(NT):
                if t >= GS:
                    gp.wait_ge(S[f"gt{t % GS}"], 16 * (t // GS))
                gp.indirect_dma_start(out=H[:, t, :], out_offset=None, in_=ys[:, :],
                                      in_offset=bass.IndirectOffsetOnAxis(ap=posi[:, t:t + 1], axis=0)) \
                    .then_inc(S[f"gt{t % GS}"], 16)

        @block.scalar
        def _(act):
            ch = Chain(act, S["ach"])
            act.wait_ge(S["wm"], 16 * 5)
            nc.scalar.activation(scT[:, :, :], cT[:, :, :], ACT.Silu).then_inc(S["a0"], 1)
            act.wait_ge(S["sm"], SMALL[0])
            nc.scalar.activation(Apar[:, :], Apar[:, :], ACT.Exp).then_inc(S["a0"], 1)

            def norm(c, which, rvs, sqs, nms):
                act.wait_ge(S[rvs], c + 1)
                nc.scalar.activation(rs[:, which, :], rs[:, which, :], ACT.Sqrt).then_inc(S[sqs], 1)
                act.wait_ge(S[nms], c + 1)
                act.sem_inc(S["holda"], 1)

            with act.Fori(0, NC) as c:
                norm(c, 0, "rv1", "sq1", "nm1")
                for u in range(U):
                    nc.scalar.activation(Ht(c, u), Rt(c, u), ACT.Identity, bias=nm[:, 0, u:u + 1],
                                         scale=rs[:, 0, u:u + 1]).then_inc(S["n1"], 1)
                norm(c, 1, "rv2", "sq2", "nm2")
                for u in range(U):
                    nc.scalar.activation(z[:, u, :], Ht(c, u), ACT.Identity, bias=nm[:, 1, u:u + 1],
                                         scale=rs[:, 1, u:u + 1]).then_inc(S["z1"], 1)
                for b in range(B):
                    act.wait_ge(S["zt"], c * U + (b + 1) * TPC)
                    nc.scalar.activation(flat(zT[:, b, :, :]), flat(PS[:, KD * b:KD * b + KD, :]), ACT.Copy) \
                        .then_inc(S["zev"], 1)
                act.wait_ge(S["xin"], c + 1)
                act.sem_inc(S["holda"], 1)
                for X in range(2):
                    nc.scalar.activation(XIN[:, X, bass.ds(c * CH + 1, CH)], PS[:, 4 + X, :], ACT.Identity,
                                         bias=bia[:, X:X + 1]).then_inc(S["xev"], 1)
            b0 = ch.n
            with act.Fori(0, NC) as c:
                ch.loop(b0, c, 2)
                for X in range(2):
                    act.wait_ge(S["cv"], c * 2 + X + 1)
                    nc.scalar.activation(uu[:, X, :], cv[:, X, :], ACT.Silu, bias=par[:, X, 3:4]).then_inc(S["u"], 1)
                act.wait_ge(S["dbc"], c * 3 + 1)
                nc.scalar.activation(dr[0:B * RK, :], PS[0:B * RK, 4, :], ACT.Copy).then_inc(S["drr"], 1)
                act.wait_ge(S["zz"], c + 1)
                for X in range(2):
                    nc.scalar.activation(et[:, X, :], PS[:, X, :], ACT.Abs, bias=par[:, X, 4:5]).then_inc(S["ab"], 1)
                for X in range(2):
                    act.wait_ge(S["ab"], c * 2 + X + 1)
                    ch.inc(nc.scalar.activation(et[:, X, :], et[:, X, :], ACT.Exp, scale=-1.0))
                for X in range(2):
                    ch.wait(X + 1)
                    nc.scalar.activation(et[:, X, :], et[:, X, :], ACT.Ln, bias=1.0).then_inc(S["sp"], 1)
                for i in range(NTILE):
                    X = int(i >= NA)
                    if i == 0 or i == NA:
                        act.wait_ge(S["dlt"], c * 2 + X + 1)
                    if i >= 2:
                        act.wait_ge(S["sc"], c * NTILE + i - 1)
                    nc.scalar.activation(dA[:, i % 2, :], dl[:, X, :], ACT.Exp, scale=Apar[:, i:i + 1]) \
                        .then_inc(S["da"], 1)
                    act.wait_ge(S["cb"], c * NTILE + i + 1)
                    if i >= 2:
                        act.wait_ge(S["g"], c * NTILE + i - 1)
                    nc.scalar.activation(cs[:, i % 2, :], PS[:, 2, :], ACT.Copy).then_inc(S["cs"], 1)
            ch.end(b0, 2, NC)

            def silu(p, gus, ns, sgs, avs, n):
                act.wait_ge(S[gus], n + 1)
                nc.scalar.activation(sg[:, p, :], PS[:, 2 * p, :], ACT.Silu).then_inc(S[sgs], 1)

            with act.Fori(0, NC) as c:
                norm(c, 0, "rv3", "sq3", "nm3")
                for u in range(U):
                    nc.scalar.activation(Ht(c, u), Rt(c, u), ACT.Identity, bias=nm[:, 0, u:u + 1],
                                         scale=rs[:, 0, u:u + 1]).then_inc(S["n3"], 1)
                for s in range(U + 2):
                    if s < U:
                        if s >= 2:
                            act.wait_ge(S["rt"], c * U + s - 1)
                        act.wait_ge(S["ht"], c * U + s + 1)
                        nc.scalar.activation(flat(hT[:, s % 2, :, :]), PS[:, 6, 0:D], ACT.Copy).then_inc(S["htv"], 1)
                    if s >= 1 and s - 1 < U:
                        silu((s - 1) % 2, "gu", None, "sgs", None, c * U + s - 1)
                    if s >= 2:
                        act.wait_ge(S["atp"], c * U + s - 1)
                        nc.scalar.activation(flat(aT[:, s % 2, :, :]), PS[:, 4, :], ACT.Copy).then_inc(S["atv"], 1)
            act.wait_ge(S["s1"], 1)
            nc.scalar.activation(S1[:, :], S1[:, :], ACT.Sigmoid).then_inc(S["a0"], 1)
            act.wait_ge(S["a0"], 3)
            act.wait_ge(S["h3"], NT)
            for t in range(NT):
                nc.scalar.activation(H[:, t, :], H[:, t, :], ACT.Copy, scale=S1[:, t:t + 1]).then_inc(S["xr"], 1)

            def step5(s, par_):
                if not isinstance(s, int) or s < RT:
                    act.wait_ge(S["ht5"], s + 1)
                    nc.scalar.activation(flat(hT[:, par_, :, :]), PS[:, 6, 0:D], ACT.Copy).then_inc(S["htv5"], 1)
                if not isinstance(s, int) or 1 <= s <= RT:
                    silu(1 - par_, "gu5", None, "sg5", None, s - 1)
                if not isinstance(s, int) or 2 <= s <= RT + 1:
                    act.wait_ge(S["at5"], s - 1)
                    nc.scalar.activation(flat(aT[:, par_, :, :]), PS[:, 4, :], ACT.Copy).then_inc(S["atv5"], 1)

            for s in range(3):
                step5(s, s % 2)
            with act.Fori(0, (RT - 3) // 2) as k:
                for s in range(2):
                    step5(k * 2 + (3 + s), (3 + s) % 2)
            for s in range(RT, RT + 3):
                step5(s, s % 2)
            for t in range(NT):
                act.wait_ge(S["fin"], t + 1)
                act.dma_start(out[t // (NT // B), (t % (NT // B)) * P:(t % (NT // B) + 1) * P, :], R[:, t, :]) \
                    .then_inc(S["od"], 16)
            act.wait_ge(S["od"], 16 * NT)

        @block.vector
        def _(v):
            V = nc.vector
            ch = Chain(v, S["dch"])
            ch.link(V.memset(HF[:, 0:2624], 0.0))
            ch.link(V.memset(XIN[:, :, :], 0.0))
            ch.inc(V.memset(state[:, :], 0.0))
            ch.inc(V.memset(one[:, :], 1.0))
            ch.link(V.memset(par[:, :, :], 0.0))
            V.memset(zero[:, :], 0.0).then_inc(S["z0"], 1)
            v.wait_ge(S["cst"], 32)
            ch.link(V.tensor_copy(sel[0:SR, :, :].rearrange("p t c -> p (t c)"), SELF[0:SR, :]))
            v.wait_ge(S["a0"], 1)
            V.tensor_copy(cB[:, :, :, :], scT[:, :, :].unsqueeze(3).to_broadcast([P, KD, B, P])).then_inc(S["b0"], 1)
            v.wait_ge(S["t0"], 1)
            for m in range(3):
                for k in range(KD):
                    ch.inc(V.tensor_copy(winT[:, m, k, :], PS[:, m // 2, ((m % 2) * KD + k) * P:((m % 2) * KD + k + 1) * P]))
            for m, dst, n in ((0, wxBT, SR), (1, wxCT, SR), (2, wxDT, B * RK)):
                for X in range(2):
                    ch.inc(V.tensor_copy(dst[:, X, :], PS[:, 2 + (2 * m + X) // 4, ((2 * m + X) % 4) * P:((2 * m + X) % 4) * P + n]))
            for X in range(2):
                ch.inc(V.tensor_copy(wdtT[0:B * RK, X, :], PS[0:B * RK, 3, (2 + X) * P:(3 + X) * P]))
            for m in range(3):
                for k in range(KD):
                    ch.inc(V.tensor_copy(woutT[:, m, k * P:(k + 1) * P], PS[:, 4 + m // 2, ((m % 2) * KD + k) * P:((m % 2) * KD + k + 1) * P]))
            for k in range(KD):
                ch.inc(V.tensor_copy(wrT[:, k, :], PS[:, 5, (2 + k) * P:(2 + k) * P + E]))
            ch.wait()
            v.sem_inc(S["e0"], 1)
            v.wait_ge(S["w0"], 1)
            ch.inc(V.tensor_copy(bia[:, :], PS[:, 7, 0:2]))
            for m in range(3):
                for k in range(KD):
                    ch.inc(V.tensor_scalar(winT[:, m, k, :], winT[:, m, k, :], lnwc[:, k:k + 1], None, ALU.mult))
            v.wait_ge(S["m0"], 1)
            for b in range(B):
                for j in range(3):
                    for hf in range(2):
                        m = 2 * j + hf
                        dst = (MODA if m < 3 else MODB)[:, b, m % 3, :]
                        src = PS[:, 3 * b + j, hf * D:(hf + 1) * D]
                        if m in (CA, CB):
                            ch.inc(V.tensor_scalar(dst, src, 1.0, None, ALU.add))
                        else:
                            ch.inc(V.tensor_copy(dst, src))
            ch.wait()
            for gate in (MODA[:, :, GA, :], MODB[:, :, GB - 3, :]):
                sgn = tmp[:, :, :]
                mag = yb[:, :, :]
                ch.inc(V.tensor_scalar(sgn, gate, 0.0, None, ALU.is_ge))
                ch.link(V.tensor_scalar(mag, gate, -1.0, None, ALU.mult))
                ch.inc(V.tensor_scalar(sgn, sgn, 2.0, -1.0, ALU.mult, ALU.add))
                ch.link(V.tensor_tensor(mag, mag, gate, ALU.max))
                ch.link(V.tensor_scalar(mag, mag, 0.25, None, ALU.max))
                ch.link(V.tensor_tensor(gate, sgn, mag, ALU.mult))
            v.wait_ge(S["a0"], 2)
            ch.link(V.tensor_scalar(Apar[:, :], Apar[:, :], -0.001, None, ALU.mult))
            v.sem_inc(S["m1"], 1)

            def stats(src, which, c, rvs, sqs, nms):
                n0 = ch.n
                for u in range(U):
                    ch.inc(V.bn_stats(st[:, u, :], src(c, u)))
                for u in range(U):
                    ch.wait(n0 + u + 1)
                    ch.inc(V.bn_aggr(mv[:, which, u, :], st[:, u, :]))
                ch.wait()
                ch.link(V.tensor_scalar(rs[:, which, :], mv[:, which, :, 1], EPS, None, ALU.add))
                V.reciprocal(rs[:, which, :], rs[:, which, :]).then_inc(S[rvs], 1)
                v.wait_ge(S[sqs], c + 1)
                V.scalar_tensor_tensor(nm[:, which, :], mv[:, which, :, 0], -1.0, rs[:, which, :], ALU.mult, ALU.mult) \
                    .then_inc(S[nms], 1)

            v.wait_ge(S["x"], 16 * B)
            ch.met = S["holdv"]
            b0, per = ch.n, 4 * U + 2 + U
            with v.Fori(0, NC) as c:
                ch.loop(b0, c, per)
                stats(Rt, 0, c, "rv1", "sq1", "nm1")
                n0 = ch.n
                for u in range(U):
                    v.wait_ge(S["n1"], c * U + u + 1)
                    ch.inc(V.tensor_tensor(Ht(c, u), Ht(c, u), MODA[:, u // TPC, CA, :], ALU.mult))
                for u in range(U):
                    ch.wait(n0 + u + 1)
                    V.tensor_tensor(Ht(c, u), Ht(c, u), MODA[:, u // TPC, SA, :], ALU.add).then_inc(S["h1"], 1)
                v.wait_ge(S["h1"], c * U + U)
                v.sem_inc(S["holdv"], 1)
                stats(Ht, 1, c, "rv2", "sq2", "nm2")
            ch.end(b0, per, NC)
            ch.met = None

            v.wait_ge(S["xev"], 2 * NC)
            v.wait_ge(S["r0"], 1)
            b0, per = ch.n, 4 + 8 + 2 + 2 + NTILE + U
            with v.Fori(0, NC) as c:
                ch.loop(b0, c, per)
                for X in range(2):
                    ch.link(V.tensor_scalar(cv[:, X, :], XIN[:, X, bass.ds(c * CH, CH)], par[:, X, 0:1], None, ALU.mult))
                    ch.link(V.scalar_tensor_tensor(cv[:, X, :], XIN[:, X, bass.ds(c * CH + 1, CH)], par[:, X, 1:2],
                                                   cv[:, X, :], ALU.mult, ALU.add))
                    V.scalar_tensor_tensor(cv[:, X, :], XIN[:, X, bass.ds(c * CH + 2, CH)], par[:, X, 2:3],
                                           cv[:, X, :], ALU.mult, ALU.add).then_inc(S["cv"], 1)
                for m in range(2):
                    q = B * NS
                    v.wait_ge(S["dbc"], c * 3 + 2 + m)
                    src = PS[0:SR, 5 + m, :]
                    ch.link(V.tensor_copy(BsCs[0:SR, m, :], src))
                    ch.link(V.tensor_tensor(spl[0:SR, 0, :], src, BsCs[0:SR, m, :], ALU.subtract))
                    ch.link(V.tensor_copy(mid[0:SR, :], spl[0:SR, 0, :]))
                    ch.link(V.tensor_tensor(spl[0:SR, 1, :], spl[0:SR, 0, :], mid[0:SR, :], ALU.subtract))
                    V.tensor_copy(BsCs[q:2 * q, m, :], mid[q:2 * q, :])
                    V.tensor_copy(BsCs[2 * q:3 * q, m, :], spl[2 * q:3 * q, 1, :]).then_inc(S["bs"], 1)
                v.wait_ge(S["zz"], c + 1)
                for X in range(2):
                    v.wait_ge(S["ab"], c * 2 + X + 1)
                    ch.inc(V.tensor_scalar(dl[:, X, :], PS[:, X, :], par[:, X, 4:5], 0.0, ALU.add, ALU.max))
                for X in range(2):
                    v.wait_ge(S["sp"], c * 2 + X + 1)
                    ch.wait(12 + X + 1)
                    V.tensor_tensor(dl[:, X, :], dl[:, X, :], et[:, X, :], ALU.add).then_inc(S["dlt"], 1)
                for X in range(2):
                    v.wait_ge(S["dlt"], c * 2 + X + 1)
                    ch.inc(V.scalar_tensor_tensor(ww[:, X, :], dl[:, X, :], 0.001, uu[:, X, :], ALU.mult, ALU.mult))
                ch.wait()

                def y_out(X):
                    v.wait_ge(S["y"], c * NTILE + (NA if X == 0 else NTILE))
                    V.scalar_tensor_tensor(ysb[:, X, :], uu[:, X, :], par[:, X, 5:6], PS[:, 3 if X == 0 else 7, :],
                                           ALU.mult, ALU.add).then_inc(S["ye"], 1)

                for i in range(NTILE):
                    X = int(i >= NA)
                    v.wait_ge(S["bb"], c * NTILE + i + 1)
                    ch.link(V.tensor_tensor(PS[:, i % 2, :], ww[:, X, :], PS[:, i % 2, :], ALU.mult))
                    v.wait_ge(S["da"], c * NTILE + i + 1)
                    if i >= 2:
                        v.wait_ge(S["g"], c * NTILE + i - 1)
                        v.wait_ge(S["st"], c * NTILE + i - 1)
                    V.tensor_tensor_scan(hs[:, i % 2, :], dA[:, i % 2, :], PS[:, i % 2, :], state[:, i:i + 1],
                                         ALU.mult, ALU.add).then_inc(S["sc"], 1)
                    if i == NA + 2:
                        y_out(0)
                y_out(1)
                for u in range(U):
                    if u % 2 == 0:
                        v.wait_ge(S["o"], c * U + u + 2)
                    ch.link(V.tensor_tensor(tmp[:, u % 2, :], PS[:, (4, 5, 6, 2)[u // 2], (u % 2) * D:(u % 2 + 1) * D],
                                            MODA[:, u // TPC, GA, :], ALU.mult))
                    V.tensor_tensor(Rt(c, u), Rt(c, u), tmp[:, u % 2, :], ALU.add).then_inc(S["x1"], 1)
                v.wait_ge(S["st"], c * NTILE + NTILE)
            ch.end(b0, per, NC)

            v.wait_ge(S["x1"], NT)
            ch.met = S["holdv"]
            b0, per = ch.n, 2 * U + 1 + U
            with v.Fori(0, NC) as c:
                ch.loop(b0, c, per)
                stats(Rt, 0, c, "rv3", "sq3", "nm3")
                for s in range(U + 3):
                    if s >= 1 and s - 1 < U:
                        u = s - 1
                        v.wait_ge(S["rt"], c * U + u + 1)
                        V.tensor_copy(flat(LG[:, bass.ds(tok(c, u), 1), :]), PS[:, 7, 0:E]).then_inc(S["lgc"], 1)
                        v.wait_ge(S["sgs"], c * U + u + 1)
                        V.tensor_tensor(av[:, u % 2, :], sg[:, u % 2, :], PS[:, 2 * (u % 2) + 1, :], ALU.mult) \
                            .then_inc(S["a"], 1)
                    if s >= 3:
                        u = s - 3
                        v.wait_ge(S["y3"], c * U + u + 1)
                        ch.link(V.tensor_tensor(tmp[:, u % 2, :], PS[:, 5, 0:D], MODB[:, u // TPC, GB - 3, :], ALU.mult))
                        V.tensor_tensor(Rt(c, u), Rt(c, u), tmp[:, u % 2, :], ALU.add).then_inc(S["r3"], 1)
            ch.end(b0, per, NC)

            ch.met = None
            v.wait_ge(S["a"], NT)
            v.wait_ge(S["r3"], NT)
            oh = flat(sg[:, :, :])[:, 0:NT * E].rearrange("p (t e) -> p t e", e=E)
            eq = flat(sg[:, :, :])[:, NT * E:2 * NT * E].rearrange("p (t e) -> p t e", e=E)
            rk = flat(av[:, :, :])[:, 0:NT * E].rearrange("p (t e) -> p t e", e=E)
            cum = flat(av[:, :, :])[:, NT * E:2 * NT * E].rearrange("p (e t) -> p e t", e=E)
            seen = tmp[:, 0, 0:NT]
            nots = tmp[:, 1, 0:NT]
            ch.link(V.tensor_reduce(S1[:, :], LG[:, :, :], axis=AX.X, op=ALU.max))
            v.sem_inc(S["s1"], 1)
            mx = yb[:, 0, 0:NT]
            ch.link(V.tensor_reduce(mx, LG[:, :, :], axis=AX.X, op=ALU.max))
            ch.link(V.tensor_tensor(eq, LG[:, :, :], mx.unsqueeze(2).to_broadcast([P, NT, E]), ALU.is_ge))
            ch.link(V.memset(seen, 0.0))
            for e in range(E):
                ch.link(V.tensor_scalar(nots, seen, -1.0, 1.0, ALU.mult, ALU.add))
                ch.inc(V.tensor_tensor(oh[:, :, e], eq[:, :, e], nots, ALU.mult))
                ch.link(V.tensor_tensor(seen, seen, eq[:, :, e], ALU.max))
            ch.wait()
            v.sem_inc(S["oh"], 1)
            v.wait_ge(S["rk"], 1)
            ch.inc(V.tensor_copy(rk.rearrange("p t e -> p (t e)"), PS[:, 0, 0:NT * E]))
            ch.link(V.tensor_copy(cum, PS[:, 1, 0:NT * E].rearrange("p (t e) -> p e t", e=E)))
            inc_ = flat(aT[:, 0, :, :])[:, 0:NT * E].rearrange("p (e t) -> p e t", e=E)
            ones_row = one[:, 0:NT]
            for e in range(E):
                ch.inc(V.tensor_tensor_scan(inc_[:, e, :], ones_row, cum[:, e, :], 0.0, ALU.mult, ALU.add))
            ch.wait()
            cmp_ = flat(aT[:, 1, :, :])[:, 0:NT * E].rearrange("p (e t) -> p e t", e=E)
            nti = yb[:, 0, 64:64 + E]
            ends = yb[:, 0, 80:80 + E]
            offs = yb[:, 0, 96:96 + E]
            ch.link(V.tensor_tensor(cmp_, inc_[:, :, NT - 1:NT].to_broadcast([P, E, NT]), jrow, ALU.is_gt))
            ch.link(V.tensor_reduce(nti, cmp_, axis=AX.X, op=ALU.add))
            ch.link(V.tensor_tensor_scan(ends, one[:, 0:E], nti, 0.0, ALU.mult, ALU.add))
            ch.link(V.tensor_tensor(offs, ends, nti, ALU.subtract))
            ch.link(V.tensor_scalar(offs, offs, float(P), None, ALU.mult))
            ch.link(V.tensor_tensor(inc_, inc_, cum, ALU.subtract))
            ch.link(V.tensor_tensor(inc_, inc_, offs.unsqueeze(2).to_broadcast([P, E, NT]), ALU.add))
            ch.link(V.tensor_tensor(rk, rk, inc_.rearrange("p e t -> p t e"), ALU.add))
            ch.link(V.tensor_tensor(rk, rk, oh, ALU.mult))
            ch.link(V.tensor_reduce(mx, rk, axis=AX.X, op=ALU.add))
            ch.link(V.tensor_copy(posi[:, :], mx))
            ef = yb[:, 1, 0:RT]
            et_ = yb[:, 1, 64:64 + RT]
            ch.link(V.tensor_scalar(ef, jtile, ends[:, 0:1], None, ALU.is_ge))
            for e in range(1, E - 1):
                ch.link(V.tensor_scalar(et_, jtile, ends[:, e:e + 1], None, ALU.is_ge))
                ch.link(V.tensor_tensor(ef, ef, et_, ALU.add))
            ch.link(V.tensor_copy(eidi[:, :], ef))
            v.sem_inc(S["pos"], 1)

            def step5(s, par_):
                if not isinstance(s, int) or 1 <= s <= RT:
                    v.wait_ge(S["gu5"], s)
                    v.wait_ge(S["sg5"], s)
                    V.tensor_tensor(av[:, 1 - par_, :], sg[:, 1 - par_, :], PS[:, 2 * (1 - par_) + 1, :], ALU.mult) \
                        .then_inc(S["a5"], 1)
                if not isinstance(s, int) or s >= 3:
                    q = 1 - par_
                    v.wait_ge(S["y5"], s - 2)
                    if not isinstance(s, int) or s >= 5:
                        v.wait_ge(S[f"ysd{q}"], (s - 3) // 2 * 16 if isinstance(s, int) else ysw[0])
                    V.tensor_copy(yb[:, q, :], PS[:, 5, 0:D]).then_inc(S["yb5"], 1)

            ysw = [None]
            for s in range(5):
                step5(s, s % 2)
            with v.Fori(0, (RT - 5) // 2) as k:
                for s in range(2):
                    ysw[0] = k * 16 + 16
                    step5(k * 2 + (5 + s), (5 + s) % 2)
            for s in range(RT, RT + 3):
                step5(s, s % 2)
            b0 = ch.n
            for t in range(NT):
                v.wait_ge(S[f"gt{t % GS}"], 16 * (t // GS + 1))
                ch.link(V.tensor_tensor(H[:, t, :], H[:, t, :], MODB[:, t // (NT // B), GB - 3, :], ALU.mult))
                V.tensor_tensor(R[:, t, :], R[:, t, :], H[:, t, :], ALU.add).then_inc(S["fin"], 1)

        @block.tensor
        def _(pe):
            T = nc.tensor
            pe.wait_ge(S["cst"], 32)
            pe.wait_ge(S["sm"], SMALL[0])
            pe.wait_ge(S["z0"], 1)
            for m in range(3):
                for k in range(KD):
                    T.transpose(PS[:, m // 2, ((m % 2) * KD + k) * P:((m % 2) * KD + k + 1) * P],
                                inR[:, m, k * P:(k + 1) * P], ident)
            for m, n in ((0, SR), (1, SR), (2, B * RK)):
                for X in range(2):
                    j = 2 * m + X
                    T.transpose(PS[:, 2 + j // 4, (j % 4) * P:(j % 4) * P + n], xR[0:n, m, X, :], ident[0:n, 0:n])
            for X in range(2):
                T.transpose(PS[0:B * RK, 3, (2 + X) * P:(3 + X) * P], dtR[:, X, :], ident)
            for m in range(3):
                for k in range(KD):
                    T.transpose(PS[:, 4 + m // 2, ((m % 2) * KD + k) * P:((m % 2) * KD + k + 1) * P],
                                outR[:, k, m, :], ident)
            for k in range(KD):
                last = T.transpose(PS[:, 5, (2 + k) * P:(2 + k) * P + E], rR[0:E, k * P:(k + 1) * P], ident[0:E, 0:E])
            last.then_inc(S["t0"], 1)
            pe.wait_ge(S["e0"], 1)
            for X, ms in ((0, (0, 1)), (1, (2,))):
                j, n = 0, len(ms) * KD
                for m in ms:
                    for k in range(KD):
                        last = T.matmul(PS[:, 7, X:X + 1], winT[:, m, k, :], lnbc[:, k:k + 1],
                                        start=(j == 0), stop=(j == n - 1))
                        j += 1
            last.then_inc(S["w0"], 1)
            pe.wait_ge(S["b0"], 1)
            for b in range(B):
                for j in range(3):
                    for k in range(KD):
                        last = T.matmul(PS[:, 3 * b + j, :], cB[:, k, b, :], WM[:, k, j * CH:(j + 1) * CH],
                                        start=(k == 0), stop=(k == KD - 1))
            last.then_inc(S["m0"], 1)
            pe.wait_ge(S["m1"], 1)
            with pe.Fori(0, NC) as c:
                for u in range(U):
                    b, i = u // TPC, u % TPC
                    pe.wait_ge(S["z1"], c * U + u + 1)
                    for k in range(KD):
                        last = T.transpose(PS[:, KD * b + k, i * P:(i + 1) * P], z[:, u, k * P:(k + 1) * P], ident)
                    last.then_inc(S["zt"], 1)
                pe.wait_ge(S["zev"], c * B + B)
                for X, ops in ((0, ((0, 0), (1, 1))), (1, ((2, 1),))):
                    j, n = 0, len(ops) * KD
                    for m, b in ops:
                        for k in range(KD):
                            last = T.matmul(PS[:, 4 + X, :], winT[:, m, k, :], zT[:, b, k, :],
                                            start=(j == 0), stop=(j == n - 1))
                            j += 1
                last.then_inc(S["xin"], 1)
            with pe.Fori(0, NC) as c:
                pe.wait_ge(S["u"], c * 2 + 2)
                for bank, w, n in ((4, wxDT, B * RK), (5, wxBT, SR), (6, wxCT, SR)):
                    for X in range(2):
                        last = T.matmul(PS[0:n, bank, :], w[:, X, :], uu[:, X, :], start=(X == 0), stop=(X == 1))
                    last.then_inc(S["dbc"], 1)
                pe.wait_ge(S["drr"], c + 1)
                for X in range(2):
                    last = T.matmul(PS[:, X, :], wdtT[0:B * RK, X, :], dr[0:B * RK, :], start=True, stop=True)
                last.then_inc(S["zz"], 1)
                pe.wait_ge(S["bs"], c * 2 + 2)
                pe.wait_ge(S["dlt"], c * 2 + 2)

                def bcast(i):
                    if i >= 2:
                        pe.wait_ge(S["sc"], c * NTILE + i - 1)
                    T.matmul(PS[:, i % 2, :], sel[0:SR, i, :], BsCs[0:SR, 0, :], start=True, stop=True) \
                        .then_inc(S["bb"], 1)
                    if i >= 1:
                        pe.wait_ge(S["cs"], c * NTILE + i)
                    T.matmul(PS[:, 2, :], sel[0:SR, i, :], BsCs[0:SR, 1, :], start=True, stop=True) \
                        .then_inc(S["cb"], 1)

                bcast(0)
                bcast(1)
                for i in range(NTILE):
                    if i + 2 < NTILE:
                        bcast(i + 2)
                    pe.wait_ge(S["g"], c * NTILE + i + 1)
                    T.matmul(PS[:, 3 if i < NA else 7, :], ident, g[:, i % 2, :],
                             start=(i in (0, NA)), stop=(i in (NA - 1, NTILE - 1))).then_inc(S["y"], 1)
                pe.wait_ge(S["ye"], c * 2 + 2)
                for u in range(U):
                    b, i = u // TPC, u % TPC
                    o = PS[:, (4, 5, 6, 2)[u // 2], (u % 2) * D:(u % 2 + 1) * D]
                    if b == 0:
                        last = T.matmul(o, ysb[:, 0, i * P:(i + 1) * P], woutT[:, 0, :], start=True, stop=True)
                    else:
                        T.matmul(o, ysb[:, 0, i * P:(i + 1) * P], woutT[:, 1, :], start=True, stop=False)
                        last = T.matmul(o, ysb[:, 1, i * P:(i + 1) * P], woutT[:, 2, :], start=False, stop=True)
                    last.then_inc(S["o"], 1)

            def transposes(src, p, n, sname):
                for k in range(KD):
                    last = T.transpose(PS[:, 6, k * P:(k + 1) * P], src[:, k * P:(k + 1) * P], ident)
                last.then_inc(S[sname], 1)

            def gate_up(W, p, sname):
                for half in range(2):
                    for k in range(KD):
                        last = T.matmul(PS[:, 2 * p + half, :], hT[:, p, k, :], W(k, half),
                                        start=(k == 0), stop=(k == KD - 1))
                last.then_inc(S[sname], 1)

            def a_transposes(p, sname):
                for k in range(KF):
                    last = T.transpose(PS[:, 4, k * P:(k + 1) * P], av[:, p, k * P:(k + 1) * P], ident)
                last.then_inc(S[sname], 1)

            def down(W, p, sname):
                for k in range(KF):
                    last = T.matmul(PS[:, 5, 0:D], aT[:, p, k, :], W(k), start=(k == 0), stop=(k == KF - 1))
                last.then_inc(S[sname], 1)

            pe.wait_ge(S["ws"], 16 * (2 * KD + 1))
            with pe.Fori(0, NC) as c:
                q = c * U
                for s in range(U + 3):
                    if s < U:
                        pe.wait_ge(S["h2"], q + s + 1)
                        if s >= 1:
                            pe.wait_ge(S["htv"], q + s)
                        transposes(h2s[:, s % 2, :], s % 2, s, "ht")
                    if s >= 1 and s - 1 < U:
                        u = s - 1
                        pe.wait_ge(S["htv"], q + u + 1)
                        if u >= 2:
                            pe.wait_ge(S["a"], q + u - 1)
                        gate_up(lambda k, half: wgu(WS, k, half), u % 2, "gu")
                        if u >= 1:
                            pe.wait_ge(S["lgc"], q + u)
                        for k in range(KD):
                            last = T.matmul(PS[:, 7, 0:E], hT[:, u % 2, k, :], wrT[:, k, :],
                                            start=(k == 0), stop=(k == KD - 1))
                        last.then_inc(S["rt"], 1)
                    if s >= 2 and s - 2 < U:
                        u = s - 2
                        pe.wait_ge(S["a"], q + u + 1)
                        if u >= 1:
                            pe.wait_ge(S["atv"], q + u)
                        a_transposes(u % 2, "atp")
                    if s >= 3:
                        u = s - 3
                        pe.wait_ge(S["atv"], q + u + 1)
                        if u >= 1:
                            pe.wait_ge(S["r3"], q + u)
                        down(lambda k: wdn(WS, k), u % 2, "y3")
            pe.wait_ge(S["oh"], 1)
            oh = flat(sg[:, :, :])[:, 0:NT * E]
            T.matmul(PS[:, 0, 0:NT * E], ltri, oh, start=True, stop=True)
            T.matmul(PS[:, 1, 0:NT * E], one[:, :], oh, start=True, stop=True).then_inc(S["rk"], 1)
            pe.wait_ge(S["pos"], 1)
            pe.wait_ge(S["wr"], 16 * 2 * E)

            def WRe(e, lo, n):
                return WR[:, bass.ds(e * EW + lo, n)]

            def step5(s, par_, k2):
                if not isinstance(s, int) or s < RT:
                    pe.wait_ge(S[f"xt{par_}"], k2 * 16 + 16)
                    if not isinstance(s, int) or s >= 1:
                        pe.wait_ge(S["htv5"], s)
                    transposes(tmp[:, par_, :], par_, s, "ht5")
                if not isinstance(s, int) or 1 <= s <= RT:
                    p = 1 - par_
                    e = pe.value_load(eidi[0:1, bass.ds(s - 1, 1)], min_val=0, max_val=E - 1)
                    pe.wait_ge(S["htv5"], s)
                    if not isinstance(s, int) or s >= 3:
                        pe.wait_ge(S["a5"], s - 2)
                    gate_up(lambda k, half: WRe(e, k * 2 * FF + half * FF, FF), p, "gu5")
                if not isinstance(s, int) or 2 <= s <= RT + 1:
                    pe.wait_ge(S["a5"], s - 1)
                    if not isinstance(s, int) or s >= 3:
                        pe.wait_ge(S["atv5"], s - 2)
                    a_transposes(par_, "at5")
                if not isinstance(s, int) or s >= 3:
                    e = pe.value_load(eidi[0:1, bass.ds(s - 3, 1)], min_val=0, max_val=E - 1)
                    pe.wait_ge(S["atv5"], s - 2)
                    if not isinstance(s, int) or s >= 4:
                        pe.wait_ge(S["yb5"], s - 3)
                    down(lambda k: WRe(e, KD * 2 * FF + k * D, D), 1 - par_, "y5")

            for s in range(4):
                step5(s, s % 2, s // 2)
            with pe.Fori(0, (RT - 5) // 2) as k:
                for s in range(2):
                    step5(k * 2 + (4 + s), s, k + 2)
            for s in range(RT - 1, RT + 3):
                step5(s, s % 2, s // 2)


_INS = ["L0_attn_feat_patch", "L0_attn_ln_w", "L0_attn_ln_b", "L0_attn_in_proj_W", "L0_attn_conv_w", "L0_attn_conv_b",
        "L0_attn_x_proj_W", "L0_attn_dt_proj_W", "L0_attn_dt_proj_b", "L0_attn_A_log", "L0_attn_D_param",
        "L0_attn_out_proj_W", "L0_ffn_router_w", "L0_ffn_gate_up_proj", "L0_ffn_down_proj", "L0_ffn_shared_gate_w",
        "L0_ffn_shared_up_w", "L0_ffn_shared_down_w", "L0_c", "L0_wmod"]


def _consts():
    import numpy as np
    ident = np.eye(P, dtype=np.float32)
    ltri = np.triu(np.ones((P, P), np.float32), 1)
    jrow = np.broadcast_to(np.tile(np.arange(NT, dtype=np.float32) * P, E), (P, E * NT))
    jtile = np.broadcast_to(np.arange(RT, dtype=np.float32), (P, RT))
    cst = np.concatenate([ident, ltri, jrow, jtile], 1)
    sel = np.zeros((3, B, NS, NTILE, P), np.float32)
    for n in range(NA):
        sel[:, 0, n, n, 0:DI] = 1
        sel[:, 1, n, n, DI:P] = 1
    for m in range(NB):
        sel[:, 1, m, NA + m, 0:D1B] = 1
        sel[:, 1, m + NB, NA + m, D1B:P] = 1
    return np.ascontiguousarray(cst), sel.reshape(SR, NTILE * P)


def kernel(**inputs):
    import numpy as np
    import concourse.bacc as bacc
    from concourse.bass_utils import run_bass_kernel_spmd
    nc = bacc.Bacc("TRN2", target_bir_lowering=False, num_devices=1)
    arrays = {f"in_{n}": np.ascontiguousarray(inputs[n]) for n in _INS}
    arrays["in_consts"], arrays["in_sel"] = _consts()
    args = [nc.dram_tensor(n, a.shape, mybir.dt.from_np(a.dtype), kind="ExternalInput").ap() for n, a in arrays.items()]
    o = nc.dram_tensor("out_0", (B, L, D), F32, kind="ExternalOutput").ap()
    adaln_block(nc, *args, o)
    r = run_bass_kernel_spmd(nc, [arrays], core_ids=[0])
    return r.results[0]["out_0"]
```

```python
import concourse.bass as bass
from concourse import mybir
from contextlib import ExitStack

F32 = mybir.dt.float32
BF16 = mybir.dt.bfloat16
I32 = mybir.dt.int32
ALU = mybir.AluOpType
ACT = mybir.ActivationFunctionType
AX = mybir.AxisListType

P = 128
B, L, D = 2, 2048, 256
DI, NS, RK = 96, 16, 6
E, FF = 8, 512
KD, KF = D // P, FF // P
CH = 512
NC = L // CH
TPC = CH // P
U = B * TPC
NT = B * L // P
D1A = P - DI
D1B = DI - D1A
NA, NB = NS, NS // 2
NTILE = NA + NB
RT = NT + E - 1
SR = 3 * B * NS
EW = KD * 2 * FF + KF * D
EPS = 1e-5
IN_T, IN_HI, GATE, UP, TANH, HID, HID_T, HID_HI, DOWN, RES = 0, 1, 2, 3, 3, 4, 5, 6, 7, 8
FIRST = 15
LAST_SLOTS = FIRST + 3 * (U - 1) + RES + 1
PROJ = {1 + 3 * k: k for k in range(U // 2)}
STATS = 12
CONV, SILU, SPLIT, ABS, LOG_IN, LOG, STEP, STEP_U = 0, 1, 4, 16, 17, 18, 19, 20
ITEM = {2 + 3 * k: k for k in range(5)}
ITEMS = 5
SPLIT_OPS = 7
PRO_SLOTS = STEP_U + 1
assert NTILE == 3 * U
EXPERTS_FROM, EXPERTS_EVERY = 5, 3
GS = 8
SA, CA, GA, SB, CB, GB = range(6)


class Chain:

    def __init__(self, eng, sem):
        self.eng, self.sem, self.off, self.n = eng, sem, 0, 0
        self.met = None

    def inc(self, ins):
        ins.then_inc(self.sem, 1)
        self.n += 1
        return self.n

    def wait(self, n=None):
        self.eng.wait_ge(self.sem, self.off + (self.n if n is None else n))
        if self.met is not None:
            self.eng.sem_inc(self.met, 1)

    def link(self, ins):
        self.inc(ins)
        self.wait()

    def loop(self, base, it, per):
        self.off, self.n = base + it * per, 0

    def end(self, base, per, times):
        assert self.n == per, ("steps of the loop", self.n, per)
        self.off, self.n = 0, base + per * times


def flat(ap):
    return ap.rearrange("p a n -> p (a n)")


def adaln_block(nc, x, lnw, lnb, inW, convw, convb, xW, dtW, dtb, alog, dpar, outW, rW, guW, dnW,
                sgW, suW, sdW, cond, wmod, consts, selc, out):
    ctx = ExitStack()
    with ctx:
        def sb(name, shape, dt=F32):
            return ctx.enter_context(nc.sbuf_tensor(name, shape, dt))

        def sem(name):
            return ctx.enter_context(nc.semaphore(name))

        xs = nc.dram_tensor("xs_sorted", [RT * P, D], F32, kind="Internal").ap()
        ys = nc.dram_tensor("ys_sorted", [RT * P, D], F32, kind="Internal").ap()

        R = sb("R", [P, NT, D])
        H = sb("H", [P, NT, D])
        WR = sb("WR", [P, E * EW])
        WRh = WR[:, 0:E * EW // 2].bitcast(BF16)
        WRl = WR[:, E * EW // 2:E * EW].bitcast(BF16)
        WSh = sb("WSh", [P, EW], BF16)
        WSl = sb("WSl", [P, EW], BF16)
        MODB = sb("MODB", [P, B, 3, D])
        CST = sb("CST", [P, 2 * P + E * NT + RT])
        ident = CST[:, 0:P]
        ltri = CST[:, P:2 * P]
        jrow = CST[:, 2 * P:2 * P + E * NT].rearrange("p (e j) -> p e j", e=E)
        jtile = CST[:, 2 * P + E * NT:2 * P + E * NT + RT]
        hT = sb("hT", [P, 2, 2, KD, P], BF16)
        sg = sb("sg", [P, 2, FF])
        av = sb("av", [P, 2, FF])
        aT = sb("aT", [P, 2, 2, KF, P], BF16)
        tmp = sb("tmp", [P, 2, D])
        yb = sb("yb", [P, 2, D])
        h2s = sb("h2s", [P, 2, D])
        st = sb("st", [P, U, 6])
        mv = sb("mv", [P, 2, U, 2])
        rs = sb("rs", [P, 2, U])
        nm = sb("nm", [P, 2, U])
        LG = sb("LG", [P, NT, E])
        wrT = sb("wrT", [P, KD, E])
        wrp = sb("wrp", [P, 2, KD, E], BF16)
        posi = sb("posi", [P, NT], I32)
        eidi = sb("eidi", [P, RT], I32)
        S1 = sb("S1", [P, NT])
        zero = sb("zero", [P, D])
        one = sb("one", [P, P])

        at = [0]

        def carve(*shape):
            n = 1
            for s in shape:
                n *= s
            ap = WR[:, at[0]:at[0] + n]
            at[0] += n
            if len(shape) == 1:
                return ap
            names = "abcd"[:len(shape)]
            return ap.rearrange(f"p ({' '.join(names)}) -> p {' '.join(names)}",
                                **{k: v for k, v in zip(names, shape)})

        XIN = carve(2, L + 2)
        MODA = carve(B, 3, D)
        winT = carve(3, KD, P)
        wxBT, wxCT = carve(2, SR), carve(2, SR)
        wxDT = carve(2, B * RK)
        wdtT = carve(2, P)
        woutT = carve(3, D)
        par = carve(2, 6)
        Apar = carve(NTILE)
        state = carve(NTILE)
        lnwc, lnbc = carve(KD), carve(KD)
        bia = carve(2)
        ysb = carve(2, CH)
        stx = carve(NT, 6)
        mvx = carve(NT, 2)
        rsx = carve(NT)
        nmx = carve(NT)
        sel = carve(NTILE * P // 2).bitcast(BF16).rearrange("p (t c) -> p t c", t=NTILE)
        BsCs = carve(NC * CH).bitcast(BF16).rearrange("p (m a c) -> p m a c", m=NC, a=2)
        cv = carve(2, CH)
        bc = carve(2, CH)
        vz = carve(2, CH)
        et = carve(2, CH)
        dr = carve(CH)
        spl = carve(2, CH)
        mid = carve(CH // 2).bitcast(BF16)
        base_dyn = at[0]
        dA = carve(2, CH)
        cs = carve(2, CH)
        hs = carve(2, CH)
        g = carve(2, CH)
        assert at[0] <= E * EW
        at[0] = base_dyn
        STG = carve(EW)
        assert at[0] <= E * EW
        at[0] = base_dyn
        z = carve(U, D)
        zT = carve(B, KD, CH)
        cT, scT = carve(KD, B), carve(KD, B)
        cB = carve(KD, B, P)
        assert at[0] <= E * EW

        HF = H[:, TPC:NT // B, :].rearrange("p t d -> p (t d)")
        inR = HF[:, 0:3 * D].rearrange("p (k d) -> p k d", k=3)
        xR = HF[:, 768:768 + 6 * P].rearrange("p (m x d) -> p m x d", m=3, x=2)
        dtR = HF[:, 1536:1536 + 2 * B * RK].rearrange("p (x r) -> p x r", x=2)
        outR = HF[:, 1600:1600 + 3 * KD * P].rearrange("p (k m d) -> p k m d", k=KD, m=3)
        rR = HF[:, 2368:2368 + D]
        ROWS_END = 2368 + D

        PS = ctx.enter_context(nc.psum_tensor("PS", [P, 8, CH], F32))

        names = ("z0 r0l mev gates ex wl ab rt holda holdv holdp x sm wt wm cst ws wr xsz "
                 "d0 dch ach pch a0 t0 e0 w0 b0 m0 m1 "
                 "rv1 sq1 nm1 n1 h1 rv2 sq2 nm2 z1 zt zev xin xev "
                 "cv u dbc drr zz sp r1 dlt bs bb cb da cs sc g st y ye o x1 r0 "
                 "rv3 sq3 nm3 n3 h2 h3 ht htv gu sgs a atp atv y3 r3 lgc "
                 "oh rk pos s1 xr scd xt0 xt1 ht5 htv5 gu5 sg5 a5 at5 atv5 y5 yb5 ysd0 ysd1 fin od").split() + [f"gt{i}" for i in range(GS)] + "pi pv mx gg atl htl atl5 htl5 st00 st01 st10 st11 st20 st21 wh wlg wld wsh wsl spl rld".split()
        S = {n: sem("s_" + n) for n in names}
        WM = H[:, NT - KD * 3 * 2:NT, :].rearrange("p (k t) d -> p k (t d)", k=KD)
        SELF = WR[:, base_dyn:base_dyn + NTILE * P]

        block = ctx.enter_context(nc.Block())

        def tok(c, u):
            if u < 0:
                c, u = c - 1, u + U
            return (u // TPC) * (NT // B) + c * TPC + u % TPC

        def batch(u):
            return u % U // TPC

        def Rt(c, u):
            return flat(R[:, bass.ds(tok(c, u), 1), :])

        def Ht(c, u):
            return flat(H[:, bass.ds(tok(c, u), 1), :])


        def uu(c, X):
            return XIN[:, X, bass.ds(c * CH, CH)]

        def dl(c, X):
            return flat(H[:, bass.ds(c * TPC + X * TPC // 2, TPC // 2), :])

        def ww(c, X):
            return flat(H[:, bass.ds(NT // B + c * TPC + X * TPC // 2, TPC // 2), :])

        SLOT = [R[:, b * NT // B:b * NT // B + 2 * TPC, :].rearrange("p t d -> p (t d)") for b in range(B)]
        spill = [nc.dram_tensor(f"spill{b}", [P, 2 * TPC * D], F32, kind="Internal").ap() for b in range(B)]

        LATE = (E - 2) * EW // 2
        STAGES = ((SLOT[0], SLOT[1]),
                  (WR[:, LATE:LATE + KD * 2 * FF], WR[:, LATE + KD * 2 * FF:LATE + EW]),
                  (WR[:, E * EW // 2 + LATE:E * EW // 2 + LATE + KD * 2 * FF],
                   WR[:, E * EW // 2 + LATE + KD * 2 * FF:E * EW]))
        STAGE = [e % 3 for e in range(E - 2)] + [0, 0]

        def raw(e):
            return STAGES[STAGE[e]]

        def landed(e, part):
            return S[f"st{STAGE[e]}{part}"], 16 * STAGE[:e + 1].count(STAGE[e])

        def wgu(W, k, half):
            return W[:, k * 2 * FF + half * FF:k * 2 * FF + (half + 1) * FF]

        def wdn(W, k):
            return W[:, KD * 2 * FF + k * D:KD * 2 * FF + (k + 1) * D]

        SMALL = [0]

        def walk(slot, c, n, slots=NTILE):
            for j in range(slots):
                slot(c, n, j)

        def lead(pro_slot, part):
            for j in range(*((0, 8), (8, 14), (14, PRO_SLOTS))[part]):
                pro_slot(None, 0, j)

        def item_bank(c):
            return 5 if c is not None else 6

        def tile_at(f, j, after):
            u, r = divmod(j - FIRST - after, 3)
            if r != 0 or u >= U or not there(f, u):
                return None
            return u

        def reused(c, i):
            return not isinstance(c, int) or c >= 1 or i >= 2

        def scanned(c):
            return not isinstance(c, int) or c < NC

        def expert_at(c, j):
            e, r = divmod(j - EXPERTS_FROM, EXPERTS_EVERY)
            return e if isinstance(c, int) and c == NC and r == 0 and 0 <= e < E else None

        def proj_in(c, j):
            if scanned(c):
                return PROJ.get(j - 1)
            return j if j < U // 2 else None

        def proj_bank(c, k):
            return 5 if scanned(c) else k

        def there(f, u):
            return not isinstance(f, int) or 0 <= f * U + u < NT

        @block.sync
        def _(sp):
            def small(dst, src):
                sp.dma_start(dst, src).then_inc(S["sm"], 16)
                SMALL[0] += 16

            xv = x.rearrange("b (j p) d -> p b j d", p=P)
            for b in range(B):
                sp.dma_start(R[:, b * NT // B:(b + 1) * NT // B, :], xv[:, b]).then_inc(S["x"], 16)
            sp.dma_start(CST[:, :], consts).then_inc(S["cst"], 16)
            sp.dma_start(SELF[0:SR, :], selc).then_inc(S["cst"], 16)
            sp.dma_start(WM, wmod.rearrange("(k p) n -> p k n", p=P)).then_inc(S["wm"], 16)
            for k in range(KD):
                for b in range(B):
                    sp.dma_start(cT[:, k, b:b + 1], cond[b, k * P:(k + 1) * P].rearrange("(p a) -> p a", a=1)) \
                        .then_inc(S["wm"], 16)
            sp.wait_ge(S["z0"], 1)
            small(inR[0:DI, 0, :], inW)
            small(inR[DI:P, 1, :], inW[0:D1A, :])
            small(inR[0:D1B, 2, :], inW[D1A:DI, :])
            small(inR[D1B:P, 2, :], inW[D1A:DI, :])
            for m in range(2):
                r0 = RK + m * NS
                for rep in range(3):
                    q = rep * B * NS
                    small(xR[q:q + NS, m, 0, 0:DI], xW[r0:r0 + NS, :])
                    small(xR[q + NS:q + 2 * NS, m, 0, DI:P], xW[r0:r0 + NS, 0:D1A])
                    small(xR[q + NS:q + 2 * NS, m, 1, 0:D1B], xW[r0:r0 + NS, D1A:DI])
            small(xR[0:RK, 2, 0, 0:DI], xW[0:RK, :])
            small(xR[RK:2 * RK, 2, 0, DI:P], xW[0:RK, 0:D1A])
            small(xR[RK:2 * RK, 2, 1, 0:D1B], xW[0:RK, D1A:DI])
            small(dtR[0:DI, 0, 0:RK], dtW)
            small(dtR[DI:P, 0, RK:2 * RK], dtW[0:D1A, :])
            small(dtR[0:D1B, 1, RK:2 * RK], dtW[D1A:DI, :])
            small(dtR[D1B:P, 1, RK:2 * RK], dtW[D1A:DI, :])
            ov = outW.rearrange("(k p) d -> p k d", p=P)
            small(outR[:, :, 0, 0:DI], ov)
            small(outR[:, :, 1, DI:P], ov[:, :, 0:D1A])
            small(outR[:, :, 2, 0:D1B], ov[:, :, D1A:DI])
            small(outR[:, :, 2, D1B:P], ov[:, :, D1A:DI])
            small(rR[0:E, :], rW)
            for k in range(KD):
                small(lnwc[:, k:k + 1], lnw[k * P:(k + 1) * P].rearrange("(p a) -> p a", a=1))
                small(lnbc[:, k:k + 1], lnb[k * P:(k + 1) * P].rearrange("(p a) -> p a", a=1))

            def rows(x_, p0, p1, d0):
                n = p1 - p0
                small(par[p0:p1, x_, 0:3], convw[d0:d0 + n, 0, :])
                small(par[p0:p1, x_, 3:4], convb[d0:d0 + n].rearrange("(p a) -> p a", a=1))
                small(par[p0:p1, x_, 4:5], dtb[d0:d0 + n].rearrange("(p a) -> p a", a=1))
                if not (x_ == 1 and p0 > 0):
                    small(par[p0:p1, x_, 5:6], dpar[d0:d0 + n].rearrange("(p a) -> p a", a=1))

            rows(0, 0, DI, 0)
            rows(0, DI, P, 0)
            rows(1, 0, D1B, D1A)
            rows(1, D1B, P, D1A)
            small(Apar[0:DI, 0:NA], alog)
            small(Apar[DI:P, 0:NA], alog[0:D1A, :])
            small(Apar[0:D1B, NA:NTILE], alog[D1A:DI, 0:NB])
            small(Apar[D1B:P, NA:NTILE], alog[D1A:DI, NB:NS])

            for t in range(RT):
                sp.dma_start(xs[t * P:(t + 1) * P, :], zero[:, :]).then_inc(S["xsz"], 16)
            sp.wait_ge(S["xev"], 2 * NC)
            for k in range(KD):
                sp.dma_start(wgu(STG, k, 0), sgW[k * P:(k + 1) * P, :]).then_inc(S["ws"], 16)
                sp.dma_start(wgu(STG, k, 1), suW[k * P:(k + 1) * P, :]).then_inc(S["ws"], 16)
            sp.dma_start(STG[:, KD * 2 * FF:EW].rearrange("p (k n) -> p k n", k=KF),
                         sdW.rearrange("(k p) n -> p k n", p=P)).then_inc(S["ws"], 16)
            sp.wait_ge(S["r3"], 2 * U)
            for b in range(B):
                sp.dma_start(spill[b], SLOT[b]).then_inc(S["spl"], 16)
            sp.wait_ge(S["spl"], 16 * B)
            sp.wait_ge(S["x1"], NT)
            sp.wait_ge(S["st"], NC * NTILE)
            for e in range(E):
                before = [d for d in range(e) if STAGE[d] == STAGE[e]]
                if before:
                    sp.wait_ge(S["wlg"], before[-1] + 1)
                sp.dma_start(raw(e)[0][:, 0:KD * 2 * FF].rearrange("p (k n) -> p k n", k=KD),
                             guW[e].rearrange("(k p) n -> p k n", p=P)).then_inc(landed(e, 0)[0], 16)
                if before:
                    sp.wait_ge(S["wld"], before[-1] + 1)
                sp.dma_start(raw(e)[1][:, 0:KF * D].rearrange("p (k n) -> p k n", k=KF),
                             dnW[e].rearrange("(k p) n -> p k n", p=P)).then_inc(landed(e, 1)[0], 16)
            sp.wait_ge(S["wlg"], E)
            sp.wait_ge(S["wld"], E)
            for b in range(B):
                sp.dma_start(SLOT[b], spill[b]).then_inc(S["rld"], 16)
            sp.wait_ge(S["scd"], 16 * NT)

            def load(t, slot):
                sp.dma_start(tmp[:, slot, :], xs[bass.ds(t * P, P), :]).then_inc(S[f"xt{slot}"], 16)

            def store(t, slot):
                sp.wait_ge(S["yb5"], t + 1)
                sp.dma_start(ys[bass.ds(t * P, P), :], yb[:, slot, :]).then_inc(S[f"ysd{slot}"], 16)

            for t in range(5):
                if t >= 2:
                    sp.wait_ge(S["ht5"], t - 1)
                load(t, t % 2)
            with sp.Fori(0, (RT - 5) // 2) as k:
                for s in range(2):
                    sp.wait_ge(S["ht5"], k * 2 + (4 + s))
                    load(k * 2 + (5 + s), (5 + s) % 2)
                    store(k * 2 + s, s)
            for t in range(RT - 5, RT):
                store(t, t % 2)

        @block.gpsimd
        def _(gp):
            ch = Chain(gp, S["pch"])
            gp.wait_ge(S["gates"], 1)
            ch.met = S["holdp"]
            b0 = ch.n
            with gp.Fori(0, NC // 2) as c:
                ch.loop(b0, c, 2 * U)
                for u in range(U):
                    gp.wait_ge(S["h1"], c * U + u + 1)
                    gp.sem_inc(S["holdp"], 1)
                    ch.link(nc.gpsimd.tensor_tensor(tmp[:, u % 2, :], Ht(c, u),
                                                    MODA[:, u // TPC, GA, :], ALU.mult))
                    ch.link(nc.gpsimd.tensor_tensor(Rt(c, u), Rt(c, u), tmp[:, u % 2, :], ALU.add))
            ch.end(b0, 2 * U, NC // 2)
            gp.sem_inc(S["r0"], 1)

            def pro_slot(c, n, j):
                a, k = divmod(j - SPLIT, SPLIT_OPS)
                if a not in (0, 1):
                    return
                q, T_ = B * NS, nc.gpsimd
                if k >= 5 and c is not None:
                    gp.wait_ge(S["st"], c * NTILE + j + 1)
                    gp.sem_inc(S["holdp"], 1)
                src, dst = bc[0:SR, a, :], flat(BsCs[0:SR, bass.ds(n, 1), a, :])
                if k == 0:
                    gp.wait_ge(S["pv"], n * ITEMS + 1 + a)
                    gp.sem_inc(S["holdp"], 1)
                    ch.link(T_.tensor_copy(mid[0:SR, :], src))
                elif k == 1:
                    ch.link(T_.tensor_copy(dst, mid[0:SR, :]))
                elif k == 2:
                    ch.link(T_.tensor_tensor(spl[0:SR, 0, :], src, mid[0:SR, :], ALU.subtract))
                elif k == 3:
                    ch.link(T_.tensor_copy(mid[0:SR, :], spl[0:SR, 0, :]))
                elif k == 4:
                    ch.link(T_.tensor_tensor(spl[0:SR, 1, :], spl[0:SR, 0, :], mid[0:SR, :], ALU.subtract))
                elif k == 5:
                    ch.link(T_.tensor_copy(flat(BsCs[q:2 * q, bass.ds(n, 1), a, :]), mid[q:2 * q, :]))
                else:
                    T_.tensor_copy(flat(BsCs[2 * q:3 * q, bass.ds(n, 1), a, :]), spl[2 * q:3 * q, 1, :]) \
                        .then_inc(S["bs"], 1)
                    gp.wait_ge(S["bs"], n * 2 + a + 1)
                    gp.sem_inc(S["holdp"], 1)

            def scan_tile(c, i):
                gp.wait_ge(S["sc"], c * NTILE + i + 1)
                gp.wait_ge(S["cs"], c * NTILE + i + 1)
                if reused(c, i):
                    gp.wait_ge(S["y"], c * NTILE + i - 1)
                nc.gpsimd.tensor_tensor(g[:, i % 2, :], hs[:, i % 2, :], cs[:, i % 2, :], ALU.mult) \
                    .then_inc(S["g"], 1)
                nc.gpsimd.tensor_copy(state[:, i:i + 1], hs[:, i % 2, CH - 1:CH]).then_inc(S["st"], 1)

            def ffn_input(f, u):
                q = f * U
                gp.wait_ge(S["n3"], q + u + 1)
                gp.sem_inc(S["holdp"], 1)
                ch.link(nc.gpsimd.tensor_tensor(Ht(f, u), Ht(f, u), MODB[:, batch(u), CB - 3, :], ALU.mult))
                if there(f, u - 2):
                    gp.wait_ge(S["ht"], q + u - 1)
                    gp.sem_inc(S["holdp"], 1)
                nc.gpsimd.tensor_tensor(h2s[:, u % 2, :], Ht(f, u), MODB[:, batch(u), SB - 3, :], ALU.add) \
                    .then_inc(S["h2"], 1)
                gp.wait_ge(S["h2"], q + u + 1)
                gp.sem_inc(S["holdp"], 1)
                nc.gpsimd.tensor_tensor(Ht(f, u), Ht(f, u), MODB[:, batch(u), SB - 3, :], ALU.add) \
                    .then_inc(S["h3"], 1)

            def slot(c, n, j):
                if scanned(c):
                    scan_tile(c, j)
                if n is not None:
                    pro_slot(c, n, j)
                if (u := tile_at(c - 1, j, IN_T - 2)) is not None:
                    ffn_input(c - 1, u)
                if (e := expert_at(c, j)) is not None:
                    gp.wait_ge(S["wh"], 2 * e + 1)
                    if e >= E - 2:
                        gp.wait_ge(S["wld"], E - 2)
                    lo, hi = e * EW, e * EW + KD * 2 * FF
                    nc.gpsimd.tensor_tensor(WRl[:, lo:hi], raw(e)[0][:, 0:KD * 2 * FF], WRh[:, lo:hi], ALU.subtract) \
                        .then_inc(S["wlg"], 1)

            for part in range(3):
                lead(pro_slot, part)
            walk(slot, 0, 1)
            walk(slot, 1, 2)
            b0, per = ch.n, U + 2 * (SPLIT_OPS - 1)
            with gp.Fori(2, NC - 1) as c:
                ch.loop(b0, c - 2, per)
                walk(slot, c, c + 1)
            ch.end(b0, per, NC - 3)
            walk(slot, NC - 1, None)
            walk(slot, NC, None, LAST_SLOTS)
            gp.wait_ge(S["pos"], 1)
            gp.wait_ge(S["xsz"], 16 * RT)
            for t in range(NT):
                gp.wait_ge(S["xr"], t + 1)
                gp.indirect_dma_start(out=xs[:, :], out_offset=bass.IndirectOffsetOnAxis(ap=posi[:, t:t + 1], axis=0),
                                      in_=H[:, t, :], in_offset=None).then_inc(S["scd"], 16)
            gp.wait_ge(S["ysd0"], 16 * ((RT + 1) // 2))
            gp.wait_ge(S["ysd1"], 16 * (RT // 2))
            for t in range(NT):
                if t >= GS:
                    gp.wait_ge(S[f"gt{t % GS}"], 16 * (t // GS))
                gp.indirect_dma_start(out=H[:, t, :], out_offset=None, in_=ys[:, :],
                                      in_offset=bass.IndirectOffsetOnAxis(ap=posi[:, t:t + 1], axis=0)) \
                    .then_inc(S[f"gt{t % GS}"], 16)

        @block.scalar
        def _(act):
            act.wait_ge(S["wm"], 16 * 5)
            nc.scalar.activation(scT[:, :, :], cT[:, :, :], ACT.Silu).then_inc(S["a0"], 1)
            def root(c, which, rvs, sqs):
                act.wait_ge(S[rvs], c + 1)
                nc.scalar.activation(rs[:, which, :], rs[:, which, :], ACT.Sqrt).then_inc(S[sqs], 1)

            def normed(c, nms):
                act.wait_ge(S[nms], c + 1)
                act.sem_inc(S["holda"], 1)

            def normalise_x(c):
                act.wait_ge(S["nm1"], c * 2 + 2)
                act.sem_inc(S["holda"], 1)
                for u in range(U):
                    nc.scalar.activation(Ht(c, u), Rt(c, u), ACT.Identity, bias=nm[:, 0, u:u + 1],
                                         scale=rs[:, 0, u:u + 1]).then_inc(S["n1"], 1)

            def normalise_h(c):
                root(c, 1, "rv2", "sq2")
                normed(c, "nm2")
                for u in range(U):
                    nc.scalar.activation(z[:, u, :], Ht(c, u), ACT.Identity, bias=nm[:, 1, u:u + 1],
                                         scale=rs[:, 1, u:u + 1]).then_inc(S["z1"], 1)

            def front(c):
                normalise_h(c)
                for b in range(B):
                    act.wait_ge(S["zt"], c * U + (b + 1) * TPC)
                    nc.scalar.activation(flat(zT[:, b, :, :]), flat(PS[:, KD * b:KD * b + KD, :]), ACT.Copy) \
                        .then_inc(S["zev"], 1)
                if not isinstance(c, int) or c + 2 < NC:
                    normalise_x(c + 2)
                act.wait_ge(S["xin"], c + 1)
                act.sem_inc(S["holda"], 1)
                for X in range(2):
                    nc.scalar.activation(XIN[:, X, bass.ds(c * CH + 1, CH)], PS[:, 4 + X, :], ACT.Identity,
                                         bias=bia[:, X:X + 1]).then_inc(S["xev"], 1)

            act.wait_ge(S["rv1"], 1)
            nc.scalar.activation(rsx[:, :], rsx[:, :], ACT.Sqrt).then_inc(S["sq1"], 1)
            normalise_x(0)
            act.wait_ge(S["sm"], SMALL[0])
            nc.scalar.activation(Apar[:, :], Apar[:, :], ACT.Exp).then_inc(S["a0"], 1)
            act.wait_ge(S["m0"], 1)
            act.wait_ge(S["t0"], 1)
            normalise_x(1)
            act.wait_ge(S["m1"], 1)
            with act.Fori(0, NC - 2) as c:
                front(c)
            front(NC - 2)

            def pro_slot(c, n, j):
                if j == SILU:
                    for X in range(2):
                        act.wait_ge(S["cv"], n * 2 + X + 1)
                        act.sem_inc(S["holda"], 1)
                        nc.scalar.activation(uu(n, X), cv[:, X, :], ACT.Silu, bias=par[:, X, 3:4]).then_inc(S["u"], 1)
                if (k := ITEM.get(j - 1)) is not None:
                    act.wait_ge(S["pi"], n * ITEMS + k + 1)
                    if k < 2:
                        nc.scalar.activation(bc[0:SR, k, :], PS[0:SR, item_bank(c), :], ACT.Copy).then_inc(S["pv"], 1)
                    elif k == 2:
                        nc.scalar.activation(dr[0:B * RK, :], PS[0:B * RK, item_bank(c), :], ACT.Copy).then_inc(S["pv"], 1)
                    else:
                        nc.scalar.activation(vz[:, k - 3, :], PS[:, item_bank(c), :], ACT.Identity, bias=par[:, k - 3, 4:5]) \
                            .then_inc(S["pv"], 1)
                if j == ABS:
                    act.wait_ge(S["pv"], n * ITEMS + ITEMS)
                    for X in range(2):
                        nc.scalar.activation(et[:, X, :], vz[:, X, :], ACT.Abs).then_inc(S["ab"], 1)
                    for X in range(2):
                        act.wait_ge(S["ab"], n * 2 + X + 1)
                        nc.scalar.activation(et[:, X, :], et[:, X, :], ACT.Exp, scale=-1.0).then_inc(S["ex"], 1)
                if j == LOG:
                    for X in range(2):
                        act.wait_ge(S["wl"], n * 2 + X + 1)
                        nc.scalar.activation(cv[:, X, :], cv[:, X, :], ACT.Ln).then_inc(S["sp"], 1)

            def scan_tile(c, i):
                X = int(i >= NA)
                if i == 0 or i == NA:
                    act.wait_ge(S["dlt"], c * 2 + X + 1)
                if reused(c, i):
                    act.wait_ge(S["sc"], c * NTILE + i - 1)
                act.sem_inc(S["holda"], 1)
                nc.scalar.activation(dA[:, i % 2, :], dl(c, X), ACT.Exp, scale=Apar[:, i:i + 1]) \
                    .then_inc(S["da"], 1)
                act.wait_ge(S["cb"], c * NTILE + i + 1)
                if reused(c, i):
                    act.wait_ge(S["g"], c * NTILE + i - 1)
                nc.scalar.activation(cs[:, i % 2, :], PS[:, 2, :], ACT.Copy).then_inc(S["cs"], 1)

            def rows_in(f, u):
                nc.scalar.activation(Ht(f, u), Rt(f, u), ACT.Identity, bias=nm[:, 0, u % U:u % U + 1],
                                     scale=rs[:, 0, u % U:u % U + 1]).then_inc(S["n3"], 1)

            def ffn_slot(f, j):
                q = f * U
                if (u := tile_at(f, j, HID_HI)) is not None:
                    act.wait_ge(S["atp"], q + u + 1)
                    nc.scalar.activation(flat(aT[:, u % 2, 0, :, :]), PS[:, 6, :], ACT.Copy).then_inc(S["atv"], 1)
                if (u := tile_at(f, j, IN_HI)) is not None:
                    act.wait_ge(S["ht"], q + u + 1)
                    nc.scalar.activation(flat(hT[:, u % 2, 0, :, :]), PS[:, 6, 0:D], ACT.Copy).then_inc(S["htv"], 1)
                if (u := tile_at(f, j, TANH)) is not None:
                    act.wait_ge(S["gg"], q + u + 1)
                    nc.scalar.activation(sg[:, u % 2, :], PS[:, 4, :], ACT.Tanh, scale=0.5).then_inc(S["sgs"], 1)
                if there(f, 0) and j == STATS:
                    root(f, 0, "rv3", "sq3")
                if there(f, 0) and j == STATS + 1:
                    normed(f, "nm3")
                    rows_in(f, 0)
                    rows_in(f, 1)
                if (u := tile_at(f, j, IN_T - 4)) is not None and not 0 <= u < 2:
                    rows_in(f, u)

            def high_parts(hi, src, n, half):
                nc.scalar.activation(hi, src, ACT.Copy, scale=0.5 if half else 1.0).then_inc(S[n], 1)

            def split_expert(e):
                if e >= E - 2:
                    act.wait_ge(S["wlg"], E - 2)
                    act.wait_ge(S["wld"], E - 2)
                for m, (lo, n) in enumerate(((0, KD * 2 * FF), (KD * 2 * FF, KF * D))):
                    act.wait_ge(*landed(e, m))
                    high_parts(WRh[:, e * EW + lo:e * EW + lo + n], raw(e)[m][:, 0:n], "wh", m == 1)

            def slot(c, n, j):
                if scanned(c):
                    scan_tile(c, j)
                if n is not None:
                    pro_slot(c, n, j)
                ffn_slot(c - 1, j)
                if (e := expert_at(c, j)) is not None:
                    split_expert(e)

            lead(pro_slot, 0)
            front(NC - 1)
            lead(pro_slot, 1)
            act.wait_ge(S["ws"], 16 * (2 * KD + 1))
            high_parts(WSh[:, 0:KD * 2 * FF], STG[:, 0:KD * 2 * FF], "wsh", False)
            high_parts(WSh[:, KD * 2 * FF:EW], STG[:, KD * 2 * FF:EW], "wsh", True)
            lead(pro_slot, 2)
            act.wait_ge(S["wsl"], 2)
            walk(slot, 0, 1)
            walk(slot, 1, 2)
            with act.Fori(2, NC - 1) as c:
                walk(slot, c, c + 1)
            walk(slot, NC - 1, None)
            walk(slot, NC, None, LAST_SLOTS)
            act.wait_ge(S["s1"], 1)
            nc.scalar.activation(S1[:, :], S1[:, :], ACT.Sigmoid).then_inc(S["a0"], 1)
            act.wait_ge(S["a0"], 3)
            act.wait_ge(S["h3"], NT)
            for t in range(NT):
                nc.scalar.activation(H[:, t, :], H[:, t, :], ACT.Copy, scale=S1[:, t:t + 1]).then_inc(S["xr"], 1)

            def step5(s, par_):
                if not isinstance(s, int) or s < RT:
                    act.wait_ge(S["ht5"], s + 1)
                    nc.scalar.activation(flat(hT[:, par_, 0, :, :]), PS[:, 2, 0:D], ACT.Copy).then_inc(S["htv5"], 1)
                if not isinstance(s, int) or 1 <= s <= RT:
                    act.wait_ge(S["gu5"], s)
                    nc.scalar.activation(sg[:, 1 - par_, :], PS[:, 4 * (1 - par_), :], ACT.Tanh, scale=0.5) \
                        .then_inc(S["sg5"], 1)
                if not isinstance(s, int) or 2 <= s <= RT + 1:
                    act.wait_ge(S["at5"], s - 1)
                    nc.scalar.activation(flat(aT[:, par_, 0, :, :]), PS[:, 6, :], ACT.Copy).then_inc(S["atv5"], 1)

            for s in range(3):
                step5(s, s % 2)
            with act.Fori(0, (RT - 3) // 2) as k:
                for s in range(2):
                    step5(k * 2 + (3 + s), (3 + s) % 2)
            for s in range(RT, RT + 3):
                step5(s, s % 2)
            for t in range(NT):
                act.wait_ge(S["fin"], t + 1)
                act.dma_start(out[t // (NT // B), (t % (NT // B)) * P:(t % (NT // B) + 1) * P, :], R[:, t, :]) \
                    .then_inc(S["od"], 16)
            act.wait_ge(S["od"], 16 * NT)

        @block.vector
        def _(v):
            V = nc.vector
            ch = Chain(v, S["dch"])
            ch.link(V.memset(HF[:, 0:ROWS_END], 0.0))
            ch.link(V.memset(XIN[:, :, :], 0.0))
            ch.inc(V.memset(state[:, :], 0.0))
            ch.inc(V.memset(one[:, :], 1.0))
            ch.link(V.memset(par[:, :, :], 0.0))
            V.memset(zero[:, :], 0.0).then_inc(S["z0"], 1)
            v.wait_ge(S["x"], 16 * B)
            n0 = ch.n
            for t in range(NT):
                ch.inc(V.bn_stats(stx[:, t, :], R[:, tok(t // U, t % U), :]))
            v.wait_ge(S["a0"], 1)
            V.tensor_copy(cB[:, :, :, :], scT[:, :, :].unsqueeze(3).to_broadcast([P, KD, B, P])).then_inc(S["b0"], 1)
            for t in range(NT):
                ch.wait(n0 + t + 1)
                ch.inc(V.bn_aggr(mvx[:, t, :], stx[:, t, :]))
            ch.wait()
            ch.link(V.tensor_scalar(rsx[:, :], mvx[:, :, 1], EPS, None, ALU.add))
            V.reciprocal(rsx[:, :], rsx[:, :]).then_inc(S["rv1"], 1)
            v.wait_ge(S["cst"], 32)
            ch.link(V.tensor_copy(sel[0:SR, :, :].rearrange("p t c -> p (t c)"), SELF[0:SR, :]))
            v.wait_ge(S["sq1"], 1)
            ch.link(V.scalar_tensor_tensor(nmx[:, :], mvx[:, :, 0], -1.0, rsx[:, :], ALU.mult, ALU.mult))
            def stats(src, which, c, rvs):
                n0 = ch.n
                for u in range(U):
                    ch.inc(V.bn_stats(st[:, u, :], src(c, u)))
                for u in range(U):
                    ch.wait(n0 + u + 1)
                    ch.inc(V.bn_aggr(mv[:, which, u, :], st[:, u, :]))
                ch.wait()
                ch.link(V.tensor_scalar(rs[:, which, :], mv[:, which, :, 1], EPS, None, ALU.add))
                V.reciprocal(rs[:, which, :], rs[:, which, :]).then_inc(S[rvs], 1)

            def mean_term(which, c, sqs, nms):
                v.wait_ge(S[sqs], c + 1)
                V.scalar_tensor_tensor(nm[:, which, :], mv[:, which, :, 0], -1.0, rs[:, which, :], ALU.mult, ALU.mult) \
                    .then_inc(S[nms], 1)

            def norm_in(c):
                V.tensor_copy(rs[:, 0, :], rsx[:, bass.ds(c * U, U)]).then_inc(S["nm1"], 1)
                V.tensor_copy(nm[:, 0, :], nmx[:, bass.ds(c * U, U)]).then_inc(S["nm1"], 1)

            def modulate(c):
                n0 = ch.n
                for u in range(U):
                    v.wait_ge(S["n1"], c * U + u + 1)
                    ch.inc(V.tensor_tensor(Ht(c, u), Ht(c, u), MODA[:, u // TPC, CA, :], ALU.mult))
                for u in range(U):
                    ch.wait(n0 + u + 1)
                    V.tensor_tensor(Ht(c, u), Ht(c, u), MODA[:, u // TPC, SA, :], ALU.add).then_inc(S["h1"], 1)

            def stats_h(c):
                if not isinstance(c, int) or c >= 1:
                    v.wait_ge(S["z1"], c * U)
                v.wait_ge(S["h1"], c * U + U)
                if ch.met is not None:
                    v.sem_inc(S["holdv"], 1)
                stats(Ht, 1, c, "rv2")

            def front(c):
                mean_term(1, c, "sq2", "nm2")
                if not isinstance(c, int) or c + 1 < NC:
                    modulate(c + 1)
                if not isinstance(c, int) or c + 2 < NC:
                    norm_in(c + 2)
                if not isinstance(c, int) or c + 1 < NC:
                    stats_h(c + 1)

            norm_in(0)
            v.wait_ge(S["m0"], 1)
            for b in range(B):
                for j in range(3):
                    for hf in range(2):
                        m = 2 * j + hf
                        dst = (MODA if m < 3 else MODB)[:, b, m % 3, :]
                        src = PS[:, 3 * b + j, hf * D:(hf + 1) * D]
                        if m in (CA, CB):
                            ch.inc(V.tensor_scalar(dst, src, 1.0, None, ALU.add))
                        else:
                            ch.inc(V.tensor_copy(dst, src))
            ch.wait()
            v.sem_inc(S["mev"], 1)
            modulate(0)
            norm_in(1)
            v.wait_ge(S["t0"], 1)
            for m in range(3):
                for k in range(KD):
                    ch.inc(V.tensor_copy(winT[:, m, k, :], PS[:, m // 2, ((m % 2) * KD + k) * P:((m % 2) * KD + k + 1) * P]))
            for m, dst, n in ((0, wxBT, SR), (1, wxCT, SR), (2, wxDT, B * RK)):
                for X in range(2):
                    ch.inc(V.tensor_copy(dst[:, X, :], PS[:, 2 + (2 * m + X) // 4, ((2 * m + X) % 4) * P:((2 * m + X) % 4) * P + n]))
            for X in range(2):
                ch.inc(V.tensor_copy(wdtT[0:B * RK, X, :], PS[0:B * RK, 3, (2 + X) * P:(3 + X) * P]))
            for m in range(3):
                for k in range(KD):
                    ch.inc(V.tensor_copy(woutT[:, m, k * P:(k + 1) * P], PS[:, 4 + m // 2, ((m % 2) * KD + k) * P:((m % 2) * KD + k + 1) * P]))
            for k in range(KD):
                ch.inc(V.tensor_copy(wrT[:, k, :], PS[:, 5, (2 + k) * P:(2 + k) * P + E]))
            ch.wait()
            ch.link(V.tensor_copy(wrp[:, 0, :, :], wrT[:, :, :]))
            ch.link(V.tensor_tensor(wrp[:, 1, :, :], wrT[:, :, :], wrp[:, 0, :, :], ALU.subtract))
            v.sem_inc(S["e0"], 1)
            v.wait_ge(S["w0"], 1)
            ch.inc(V.tensor_copy(bia[:, :], PS[:, 7, 0:2]))
            for m in range(3):
                for k in range(KD):
                    ch.inc(V.tensor_scalar(winT[:, m, k, :], winT[:, m, k, :], lnwc[:, k:k + 1], None, ALU.mult))
            ch.wait()
            v.sem_inc(S["m1"], 1)
            def bound_gate(gate):
                sgn = h2s[:, :, :]
                mag = yb[:, :, :]
                ch.inc(V.tensor_scalar(sgn, gate, 0.0, None, ALU.is_ge))
                ch.link(V.tensor_scalar(mag, gate, -1.0, None, ALU.mult))
                ch.inc(V.tensor_scalar(sgn, sgn, 2.0, -1.0, ALU.mult, ALU.add))
                ch.link(V.tensor_tensor(mag, mag, gate, ALU.max))
                ch.link(V.tensor_scalar(mag, mag, 0.25, None, ALU.max))
                ch.link(V.tensor_tensor(gate, sgn, mag, ALU.mult))

            bound_gate(MODA[:, :, GA, :])
            v.sem_inc(S["gates"], 1)
            stats_h(0)
            ch.met = S["holdv"]
            b0, per = ch.n, 2 * U + 1 + U
            with v.Fori(0, NC - 2) as c:
                ch.loop(b0, c, per)
                front(c)
            ch.end(b0, per, NC - 2)
            ch.met = None
            front(NC - 2)
            v.wait_ge(S["xev"], 4)

            def pro_slot(c, n, j):
                if j in (CONV, CONV + 1):
                    X = j - CONV
                    ch.link(V.tensor_scalar(cv[:, X, :], XIN[:, X, bass.ds(n * CH, CH)], par[:, X, 0:1], None, ALU.mult))
                    ch.link(V.scalar_tensor_tensor(cv[:, X, :], XIN[:, X, bass.ds(n * CH + 1, CH)], par[:, X, 1:2],
                                                   cv[:, X, :], ALU.mult, ALU.add))
                    V.scalar_tensor_tensor(cv[:, X, :], XIN[:, X, bass.ds(n * CH + 2, CH)], par[:, X, 2:3],
                                           cv[:, X, :], ALU.mult, ALU.add).then_inc(S["cv"], 1)
                if j == ABS:
                    v.wait_ge(S["pv"], n * ITEMS + ITEMS)
                    for X in range(2):
                        V.tensor_scalar(dl(n, X), vz[:, X, :], 0.0, None, ALU.max).then_inc(S["mx"], 1)
                if j == LOG_IN:
                    for X in range(2):
                        v.wait_ge(S["ex"], n * 2 + X + 1)
                        ch.link(V.tensor_scalar(cv[:, X, :], et[:, X, :], 1.0, None, ALU.add))
                        V.scalar_tensor_tensor(et[:, X, :], cv[:, X, :], -1.0, et[:, X, :], ALU.add, ALU.subtract) \
                            .then_inc(S["wl"], 1)
                if j == STEP:
                    for X in range(2):
                        v.wait_ge(S["mx"], n * 2 + X + 1)
                        v.wait_ge(S["sp"], n * 2 + X + 1)
                        ch.link(V.tensor_tensor(dl(n, X), dl(n, X), cv[:, X, :], ALU.add))
                        V.tensor_tensor(dl(n, X), dl(n, X), et[:, X, :], ALU.subtract).then_inc(S["dlt"], 1)
                if j == STEP_U:
                    for X in range(2):
                        v.wait_ge(S["dlt"], n * 2 + X + 1)
                        v.wait_ge(S["u"], n * 2 + X + 1)
                        ch.inc(V.scalar_tensor_tensor(ww(n, X), dl(n, X), 0.001, uu(n, X), ALU.mult, ALU.mult))
                    ch.wait()

            def y_out(c, X):
                v.wait_ge(S["y"], c * NTILE + (NA if X == 0 else NTILE))
                V.scalar_tensor_tensor(ysb[:, X, :], uu(c, X), par[:, X, 5:6], PS[:, 3, :],
                                       ALU.mult, ALU.add).then_inc(S["ye"], 1)

            def scan_tile(c, i):
                X = int(i >= NA)
                v.wait_ge(S["bb"], c * NTILE + i + 1)
                ch.link(V.tensor_tensor(PS[:, i % 2, :], ww(c, X), PS[:, i % 2, :], ALU.mult))
                v.wait_ge(S["da"], c * NTILE + i + 1)
                if reused(c, i):
                    v.wait_ge(S["g"], c * NTILE + i - 1)
                    v.wait_ge(S["st"], c * NTILE + i - 1)
                V.tensor_tensor_scan(hs[:, i % 2, :], dA[:, i % 2, :], PS[:, i % 2, :], state[:, i:i + 1],
                                     ALU.mult, ALU.add).then_inc(S["sc"], 1)
                if i == NA:
                    y_out(c, 0)

            def proj_slot(c, f, j):
                if j == 0:
                    y_out(f, 1)
                if (k := proj_in(c, j)) is not None:
                    bank = proj_bank(c, k)
                    v.wait_ge(S["o"], f * U + 2 * k + 2)
                    for u in (2 * k, 2 * k + 1):
                        ch.link(V.tensor_tensor(yb[:, u % 2, :], PS[:, bank, (u % 2) * D:(u % 2 + 1) * D],
                                                MODA[:, u // TPC, GA, :], ALU.mult))
                        V.tensor_tensor(Rt(f, u), Rt(f, u), yb[:, u % 2, :], ALU.add).then_inc(S["x1"], 1)
                if j == STATS:
                    v.wait_ge(S["x1"], f * U + U)
                    if there(f, -1):
                        v.wait_ge(S["n3"], f * U)
                    ch.met = S["holdv"]
                    v.sem_inc(S["holdv"], 1)
                    stats(Rt, 0, f, "rv3")
                    ch.met = None
                if j == STATS + 1:
                    mean_term(0, f, "sq3", "nm3")

            def ffn_slot(f, j):
                q = f * U
                if (u := tile_at(f, j, HID_HI)) is not None:
                    v.wait_ge(S["atv"], q + u + 1)
                    V.tensor_tensor(flat(aT[:, u % 2, 1, :, :]), PS[:, 6, :], flat(aT[:, u % 2, 0, :, :]),
                                    ALU.subtract).then_inc(S["atl"], 1)
                if (u := tile_at(f, j, IN_HI)) is not None:
                    v.wait_ge(S["htv"], q + u + 1)
                    V.tensor_tensor(flat(hT[:, u % 2, 1, :, :]), PS[:, 6, 0:D], flat(hT[:, u % 2, 0, :, :]),
                                    ALU.subtract).then_inc(S["htl"], 1)
                if (u := tile_at(f, j, HID)) is not None:
                    v.wait_ge(S["rt"], q + u + 1)
                    V.tensor_copy(flat(LG[:, bass.ds(tok(f, u), 1), :]), PS[:, 7, 0:E]).then_inc(S["lgc"], 1)
                    p = u % 2
                    v.wait_ge(S["gu"], q + u + 1)
                    v.wait_ge(S["sgs"], q + u + 1)
                    ch.link(V.scalar_tensor_tensor(av[:, p, :], sg[:, p, :], 1.0, PS[:, 5, :], ALU.add, ALU.mult))
                    V.tensor_tensor(av[:, p, :], av[:, p, :], PS[:, 4, :], ALU.mult).then_inc(S["a"], 1)
                if (u := tile_at(f, j, RES)) is not None:
                    v.wait_ge(S["y3"], q + u + 1)
                    ch.link(V.tensor_tensor(tmp[:, u % 2, :], PS[:, 7, D:2 * D], MODB[:, batch(u), GB - 3, :], ALU.mult))
                    V.tensor_tensor(Rt(f, u), Rt(f, u), tmp[:, u % 2, :], ALU.add).then_inc(S["r3"], 1)

            def low_parts(lo, hi, src, n, half):
                V.scalar_tensor_tensor(lo, src, 0.5 if half else 1.0, hi, ALU.mult, ALU.subtract).then_inc(S[n], 1)

            def split_expert(e):
                v.wait_ge(S["wh"], 2 * e + 2)
                if e >= E - 2:
                    v.wait_ge(S["wlg"], E - 2)
                lo, hi = e * EW + KD * 2 * FF, (e + 1) * EW
                low_parts(WRl[:, lo:hi], WRh[:, lo:hi], raw(e)[1][:, 0:KF * D], "wld", True)

            def slot(c, n, j):
                if scanned(c):
                    scan_tile(c, j)
                if n is not None:
                    pro_slot(c, n, j)
                if isinstance(c, int) and c == 0 and j < U * (NC - NC // 2):
                    late, u = NC // 2 + j // U, j % U
                    ch.link(V.tensor_tensor(yb[:, j % 2, :], Ht(late, u), MODA[:, u // TPC, GA, :], ALU.mult))
                    V.tensor_tensor(Rt(late, u), Rt(late, u), yb[:, j % 2, :], ALU.add).then_inc(S["r0l"], 1)
                if there(c - 1, 0):
                    proj_slot(c, c - 1, j)
                ffn_slot(c - 1, j)
                if (e := expert_at(c, j)) is not None:
                    split_expert(e)

            lead(pro_slot, 0)
            front(NC - 1)
            bound_gate(MODB[:, :, GB - 3, :])
            v.wait_ge(S["a0"], 2)
            ch.link(V.tensor_scalar(Apar[:, :], Apar[:, :], -0.001, None, ALU.mult))
            lead(pro_slot, 1)
            v.wait_ge(S["wsh"], 2)
            low_parts(WSl[:, 0:KD * 2 * FF], WSh[:, 0:KD * 2 * FF], STG[:, 0:KD * 2 * FF], "wsl", False)
            low_parts(WSl[:, KD * 2 * FF:EW], WSh[:, KD * 2 * FF:EW], STG[:, KD * 2 * FF:EW], "wsl", True)
            v.wait_ge(S["r0"], 1)
            lead(pro_slot, 2)
            v.wait_ge(S["wsl"], 2)
            walk(slot, 0, 1)
            walk(slot, 1, 2)
            b0 = ch.n
            per = (4 + 2 + 2 + 2) + NTILE + U + (2 * U + 1) + 2 * U
            with v.Fori(2, NC - 1) as c:
                ch.loop(b0, c - 2, per)
                walk(slot, c, c + 1)
            ch.end(b0, per, NC - 3)
            walk(slot, NC - 1, None)
            walk(slot, NC, None, LAST_SLOTS)

            v.wait_ge(S["a"], NT)
            v.wait_ge(S["r3"], NT)
            v.wait_ge(S["lgc"], NT)
            oh = flat(sg[:, :, :])[:, 0:NT * E].rearrange("p (t e) -> p t e", e=E)
            eq = flat(sg[:, :, :])[:, NT * E:2 * NT * E].rearrange("p (t e) -> p t e", e=E)
            rk = flat(av[:, :, :])[:, 0:NT * E].rearrange("p (t e) -> p t e", e=E)
            cum = flat(av[:, :, :])[:, NT * E:2 * NT * E].rearrange("p (e t) -> p e t", e=E)
            scr = h2s[:, :, :].rearrange("p a d -> p (a d)")
            seen = tmp[:, 0, 0:NT]
            nots = tmp[:, 1, 0:NT]
            ch.link(V.tensor_reduce(S1[:, :], LG[:, :, :], axis=AX.X, op=ALU.max))
            v.sem_inc(S["s1"], 1)
            mx = yb[:, 0, 0:NT]
            ch.link(V.tensor_reduce(mx, LG[:, :, :], axis=AX.X, op=ALU.max))
            ch.link(V.tensor_tensor(eq, LG[:, :, :], mx.unsqueeze(2).to_broadcast([P, NT, E]), ALU.is_ge))
            ch.link(V.memset(seen, 0.0))
            for e in range(E):
                ch.link(V.tensor_scalar(nots, seen, -1.0, 1.0, ALU.mult, ALU.add))
                ch.inc(V.tensor_tensor(oh[:, :, e], eq[:, :, e], nots, ALU.mult))
                ch.link(V.tensor_tensor(seen, seen, eq[:, :, e], ALU.max))
            ch.wait()
            v.sem_inc(S["oh"], 1)
            v.wait_ge(S["rk"], 1)
            ch.inc(V.tensor_copy(rk.rearrange("p t e -> p (t e)"), PS[:, 0, 0:NT * E]))
            ch.link(V.tensor_copy(cum, PS[:, 1, 0:NT * E].rearrange("p (t e) -> p e t", e=E)))
            inc_ = scr[:, 0:NT * E].rearrange("p (e t) -> p e t", e=E)
            ones_row = one[:, 0:NT]
            for e in range(E):
                ch.inc(V.tensor_tensor_scan(inc_[:, e, :], ones_row, cum[:, e, :], 0.0, ALU.mult, ALU.add))
            ch.wait()
            cmp_ = scr[:, NT * E:2 * NT * E].rearrange("p (e t) -> p e t", e=E)
            nti = yb[:, 0, 64:64 + E]
            ends = yb[:, 0, 80:80 + E]
            offs = yb[:, 0, 96:96 + E]
            ch.link(V.tensor_tensor(cmp_, inc_[:, :, NT - 1:NT].to_broadcast([P, E, NT]), jrow, ALU.is_gt))
            ch.link(V.tensor_reduce(nti, cmp_, axis=AX.X, op=ALU.add))
            ch.link(V.tensor_tensor_scan(ends, one[:, 0:E], nti, 0.0, ALU.mult, ALU.add))
            ch.link(V.tensor_tensor(offs, ends, nti, ALU.subtract))
            ch.link(V.tensor_scalar(offs, offs, float(P), None, ALU.mult))
            ch.link(V.tensor_tensor(inc_, inc_, cum, ALU.subtract))
            ch.link(V.tensor_tensor(inc_, inc_, offs.unsqueeze(2).to_broadcast([P, E, NT]), ALU.add))
            ch.link(V.tensor_tensor(rk, rk, inc_.rearrange("p e t -> p t e"), ALU.add))
            ch.link(V.tensor_tensor(rk, rk, oh, ALU.mult))
            ch.link(V.tensor_reduce(mx, rk, axis=AX.X, op=ALU.add))
            ch.link(V.tensor_copy(posi[:, :], mx))
            ef = yb[:, 1, 0:RT]
            et_ = yb[:, 1, 64:64 + RT]
            ch.link(V.tensor_scalar(ef, jtile, ends[:, 0:1], None, ALU.is_ge))
            for e in range(1, E - 1):
                ch.link(V.tensor_scalar(et_, jtile, ends[:, e:e + 1], None, ALU.is_ge))
                ch.link(V.tensor_tensor(ef, ef, et_, ALU.add))
            ch.link(V.tensor_copy(eidi[:, :], ef))
            v.sem_inc(S["pos"], 1)

            def step5(s, par_):
                if not isinstance(s, int) or s < RT:
                    v.wait_ge(S["htv5"], s + 1)
                    V.tensor_tensor(flat(hT[:, par_, 1, :, :]), PS[:, 2, 0:D], flat(hT[:, par_, 0, :, :]),
                                    ALU.subtract).then_inc(S["htl5"], 1)
                if not isinstance(s, int) or 1 <= s <= RT:
                    p = 1 - par_
                    v.wait_ge(S["sg5"], s)
                    ch.link(V.scalar_tensor_tensor(av[:, p, :], sg[:, p, :], 1.0, PS[:, 4 * p + 1, :], ALU.add, ALU.mult))
                    V.tensor_tensor(av[:, p, :], av[:, p, :], PS[:, 4 * p, :], ALU.mult).then_inc(S["a5"], 1)
                if not isinstance(s, int) or 2 <= s <= RT + 1:
                    v.wait_ge(S["atv5"], s - 1)
                    V.tensor_tensor(flat(aT[:, par_, 1, :, :]), PS[:, 6, :], flat(aT[:, par_, 0, :, :]),
                                    ALU.subtract).then_inc(S["atl5"], 1)
                if not isinstance(s, int) or s >= 3:
                    q = 1 - par_
                    v.wait_ge(S["y5"], s - 2)
                    if not isinstance(s, int) or s >= 5:
                        v.wait_ge(S[f"ysd{q}"], (s - 3) // 2 * 16 if isinstance(s, int) else ysw[0])
                    V.tensor_copy(yb[:, q, :], PS[:, 3, 0:D]).then_inc(S["yb5"], 1)

            ysw = [None]
            for s in range(5):
                step5(s, s % 2)
            b0 = ch.n
            with v.Fori(0, (RT - 5) // 2) as k:
                ch.loop(b0, k, 2)
                for s in range(2):
                    ysw[0] = k * 16 + 16
                    step5(k * 2 + (5 + s), (5 + s) % 2)
            ch.end(b0, 2, (RT - 5) // 2)
            for s in range(RT, RT + 3):
                step5(s, s % 2)
            v.wait_ge(S["rld"], 16 * B)
            b0 = ch.n
            for t in range(NT):
                v.wait_ge(S[f"gt{t % GS}"], 16 * (t // GS + 1))
                ch.link(V.tensor_tensor(H[:, t, :], H[:, t, :], MODB[:, t // (NT // B), GB - 3, :], ALU.mult))
                V.tensor_tensor(R[:, t, :], R[:, t, :], H[:, t, :], ALU.add).then_inc(S["fin"], 1)

        @block.tensor
        def _(pe):
            T = nc.tensor
            pe.wait_ge(S["cst"], 32)
            pe.wait_ge(S["b0"], 1)
            for b in range(B):
                for j in range(3):
                    for k in range(KD):
                        last = T.matmul(PS[:, 3 * b + j, :], cB[:, k, b, :], WM[:, k, j * CH:(j + 1) * CH],
                                        start=(k == 0), stop=(k == KD - 1))
            last.then_inc(S["m0"], 1)
            pe.wait_ge(S["mev"], 1)
            pe.wait_ge(S["sm"], SMALL[0])
            pe.wait_ge(S["z0"], 1)
            for m in range(3):
                for k in range(KD):
                    T.transpose(PS[:, m // 2, ((m % 2) * KD + k) * P:((m % 2) * KD + k + 1) * P],
                                inR[:, m, k * P:(k + 1) * P], ident)
            for m, n in ((0, SR), (1, SR), (2, B * RK)):
                for X in range(2):
                    j = 2 * m + X
                    T.transpose(PS[:, 2 + j // 4, (j % 4) * P:(j % 4) * P + n], xR[0:n, m, X, :], ident[0:n, 0:n])
            for X in range(2):
                T.transpose(PS[0:B * RK, 3, (2 + X) * P:(3 + X) * P], dtR[:, X, :], ident)
            for m in range(3):
                for k in range(KD):
                    T.transpose(PS[:, 4 + m // 2, ((m % 2) * KD + k) * P:((m % 2) * KD + k + 1) * P],
                                outR[:, k, m, :], ident)
            for k in range(KD):
                last = T.transpose(PS[:, 5, (2 + k) * P:(2 + k) * P + E], rR[0:E, k * P:(k + 1) * P], ident[0:E, 0:E])
            last.then_inc(S["t0"], 1)
            pe.wait_ge(S["e0"], 1)
            for X, ms in ((0, (0, 1)), (1, (2,))):
                j, n = 0, len(ms) * KD
                for m in ms:
                    for k in range(KD):
                        last = T.matmul(PS[:, 7, X:X + 1], winT[:, m, k, :], lnbc[:, k:k + 1],
                                        start=(j == 0), stop=(j == n - 1))
                        j += 1
            last.then_inc(S["w0"], 1)
            pe.wait_ge(S["m1"], 1)

            def front(c):
                for u in range(U):
                    b, i = u // TPC, u % TPC
                    pe.wait_ge(S["z1"], c * U + u + 1)
                    for k in range(KD):
                        last = T.transpose(PS[:, KD * b + k, i * P:(i + 1) * P], z[:, u, k * P:(k + 1) * P], ident)
                    last.then_inc(S["zt"], 1)
                pe.wait_ge(S["zev"], c * B + B)
                for X, ops in ((0, ((0, 0), (1, 1))), (1, ((2, 1),))):
                    j, n = 0, len(ops) * KD
                    for m, b in ops:
                        for k in range(KD):
                            last = T.matmul(PS[:, 4 + X, :], winT[:, m, k, :], zT[:, b, k, :],
                                            start=(j == 0), stop=(j == n - 1))
                            j += 1
                last.then_inc(S["xin"], 1)

            with pe.Fori(0, NC - 1) as c:
                front(c)

            def pro_slot(c, n, j):
                if (k := ITEM.get(j)) is None:
                    return
                if not isinstance(n, int) or n * ITEMS + k >= 1:
                    pe.wait_ge(S["pv"], n * ITEMS + k)
                if c is not None:
                    if (u := tile_at(c - 1, j - 1, HID)) is not None:
                        pe.wait_ge(S["a"], (c - 1) * U + u + 1)
                    if there(c - 1, 0) and j - 1 in PROJ:
                        pe.wait_ge(S["x1"], (c - 1) * U + 2 * PROJ[j - 1] + 2)
                if k < 3:
                    w, r = ((wxBT, SR), (wxCT, SR), (wxDT, B * RK))[k]
                    if k == 0:
                        pe.wait_ge(S["u"], n * 2 + 2)
                    for X in range(2):
                        last = T.matmul(PS[0:r, item_bank(c), :], w[:, X, :], uu(n, X), start=(X == 0), stop=(X == 1))
                else:
                    last = T.matmul(PS[:, item_bank(c), :], wdtT[0:B * RK, k - 3, :], dr[0:B * RK, :], start=True, stop=True)
                last.then_inc(S["pi"], 1)

            def bcast_B(c, i):
                if reused(c, i):
                    pe.wait_ge(S["sc"], c * NTILE + i - 1)
                T.matmul(PS[:, i % 2, :], sel[0:SR, i, :], flat(BsCs[0:SR, bass.ds(c, 1), 0, :]), start=True, stop=True) \
                    .then_inc(S["bb"], 1)

            def bcast_C(c, i):
                if not isinstance(c, int) or c + i >= 1:
                    pe.wait_ge(S["cs"], c * NTILE + i)
                T.matmul(PS[:, 2, :], sel[0:SR, i, :], flat(BsCs[0:SR, bass.ds(c, 1), 1, :]), start=True, stop=True) \
                    .then_inc(S["cb"], 1)

            def sum_states(c, i):
                pe.wait_ge(S["g"], c * NTILE + i + 1)
                if i == 0 and there(c - 1, 0):
                    pe.wait_ge(S["ye"], c * 2)
                if i == NA:
                    pe.wait_ge(S["ye"], c * 2 + 1)
                T.matmul(PS[:, 3, :], ident, g[:, i % 2, :],
                         start=(i in (0, NA)), stop=(i in (NA - 1, NTILE - 1))).then_inc(S["y"], 1)

            def scan_tile(c, n, i):
                if n is not None and i == NTILE - 2:
                    pe.wait_ge(S["bs"], n * 2 + 2)
                if i + 1 < NTILE:
                    bcast_C(c, i + 1)
                elif n is not None:
                    bcast_C(n, 0)
                if i + 2 < NTILE:
                    bcast_B(c, i + 2)
                elif n is not None:
                    bcast_B(n, i + 2 - NTILE)
                if i >= 1:
                    sum_states(c, i - 1)

            def proj_pair(c, f, k):
                bank = proj_bank(c, k)
                if k == 0:
                    pe.wait_ge(S["ye"], f * 2 + 2)
                for u in (2 * k, 2 * k + 1):
                    b, i = u // TPC, u % TPC
                    o = PS[:, bank, (u % 2) * D:(u % 2 + 1) * D]
                    if b == 0:
                        last = T.matmul(o, ysb[:, 0, i * P:(i + 1) * P], woutT[:, 0, :], start=True, stop=True)
                    else:
                        T.matmul(o, ysb[:, 0, i * P:(i + 1) * P], woutT[:, 1, :], start=True, stop=False)
                        last = T.matmul(o, ysb[:, 1, i * P:(i + 1) * P], woutT[:, 2, :], start=False, stop=True)
                    last.then_inc(S["o"], 1)

            def proj_slot(c, f, n, j):
                if (k := PROJ.get(j)) is not None:
                    if k == 0:
                        if n is not None:
                            pe.wait_ge(S["pv"], n * ITEMS)
                    elif n is not None:
                        pe.wait_ge(S["pv"], n * ITEMS + k)
                    else:
                        pe.wait_ge(S["x1"], f * U + 2 * k)
                    if (u := tile_at(f, j, HID)) is not None:
                        pe.wait_ge(S["a"], f * U + u + 1)
                    proj_pair(c, f, k)

            def transposes(bank, src, sname):
                for k in range(KD):
                    last = T.transpose(PS[:, bank, k * P:(k + 1) * P], src[:, k * P:(k + 1) * P], ident)
                last.then_inc(S[sname], 1)

            def product(o, n, lhs, wh, wl):
                for k in range(n):
                    T.matmul(o, lhs[:, 0, k, :], wh(k), start=(k == 0), stop=False)
                    T.matmul(o, lhs[:, 0, k, :], wl(k), start=False, stop=False)
                    last = T.matmul(o, lhs[:, 1, k, :], wh(k), start=False, stop=(k == n - 1))
                return last

            def a_transposes(p, sname):
                for k in range(KF):
                    last = T.transpose(PS[:, 6, k * P:(k + 1) * P], av[:, p, k * P:(k + 1) * P], ident)
                last.then_inc(S[sname], 1)

            def router(p):
                for m in range(KD * 4):
                    last = T.matmul(PS[:, 7, 0:E], hT[:, p, m // 2 % 2, m // 4, :], wrp[:, m % 2, m // 4, :],
                                    start=(m == 0), stop=(m == KD * 4 - 1))
                last.then_inc(S["rt"], 1)

            def ffn_slot(c, f, n, j):
                q = f * U
                if (u := tile_at(f, j, IN_T)) is not None:
                    pe.wait_ge(S["h2"], q + u + 1)
                    if there(f, u - 2):
                        pe.wait_ge(S["atl"], q + u - 1)
                    elif there(f, u - 1):
                        pe.wait_ge(S["htl"], q + u)
                    transposes(6, h2s[:, u % 2, :], "ht")
                if (u := tile_at(f, j, UP)) is not None:
                    if n is not None and j - 1 in ITEM:
                        pe.wait_ge(S["pv"], n * ITEMS + ITEM[j - 1] + 1)
                    elif scanned(c) and j - 2 in PROJ:
                        pe.wait_ge(S["x1"], f * U + 2 * PROJ[j - 2] + 2)
                    product(PS[:, 5, :], KD, hT[:, u % 2], lambda k: wgu(WSh, k, 1), lambda k: wgu(WSl, k, 1)) \
                        .then_inc(S["gu"], 1)
                    if there(f, u - 1):
                        pe.wait_ge(S["lgc"], q + u)
                    if there(f, u - 2):
                        pe.wait_ge(S["r3"], q + u - 1)
                    router(u % 2)
                if (u := tile_at(f, j, GATE)) is not None:
                    pe.wait_ge(S["htl"], q + u + 1)
                    if there(f, u - 1):
                        pe.wait_ge(S["a"], q + u)
                    product(PS[:, 4, :], KD, hT[:, u % 2], lambda k: wgu(WSh, k, 0), lambda k: wgu(WSl, k, 0)) \
                        .then_inc(S["gg"], 1)
                if (u := tile_at(f, j, HID_T)) is not None:
                    pe.wait_ge(S["a"], q + u + 1)
                    if there(f, u + 1):
                        pe.wait_ge(S["htl"], q + u + 2)
                    else:
                        pe.wait_ge(S["atl"], q + u)
                    a_transposes(u % 2, "atp")
                if (u := tile_at(f, j, DOWN)) is not None:
                    pe.wait_ge(S["atl"], q + u + 1)
                    if there(f, u + 1):
                        pe.wait_ge(S["lgc"], q + u + 2)
                    else:
                        pe.wait_ge(S["r3"], q + u)
                    product(PS[:, 7, D:2 * D], KF, aT[:, u % 2], lambda k: wdn(WSh, k), lambda k: wdn(WSl, k)) \
                        .then_inc(S["y3"], 1)

            def slot(c, n, j):
                if scanned(c):
                    scan_tile(c, n, j)
                if j == 0 and there(c - 1, 0):
                    sum_states(c - 1, NTILE - 1)
                if not scanned(c) and j < U // 2:
                    proj_pair(c, c - 1, j)
                ffn_slot(c, c - 1, n, j)
                if scanned(c) and there(c - 1, 0):
                    proj_slot(c, c - 1, n, j)
                if n is not None:
                    pro_slot(c, n, j)

            lead(pro_slot, 0)
            front(NC - 1)
            lead(pro_slot, 1)
            lead(pro_slot, 2)
            pe.wait_ge(S["bs"], 2)
            bcast_B(0, 0)
            bcast_B(0, 1)
            bcast_C(0, 0)
            walk(slot, 0, 1)
            pe.wait_ge(S["wsl"], 2)
            walk(slot, 1, 2)
            with pe.Fori(2, NC - 1) as c:
                walk(slot, c, c + 1)
            walk(slot, NC - 1, None)
            walk(slot, NC, None, LAST_SLOTS)
            pe.wait_ge(S["oh"], 1)
            oh = flat(sg[:, :, :])[:, 0:NT * E]
            T.matmul(PS[:, 0, 0:NT * E], ltri, oh, start=True, stop=True)
            T.matmul(PS[:, 1, 0:NT * E], one[:, :], oh, start=True, stop=True).then_inc(S["rk"], 1)
            pe.wait_ge(S["pos"], 1)
            pe.wait_ge(S["wlg"], E)
            pe.wait_ge(S["wld"], E)

            def part(W, e, lo, n):
                return W[:, bass.ds(e * EW + lo, n)]

            def step5(s, par_, k2):
                if not isinstance(s, int) or s < RT:
                    pe.wait_ge(S[f"xt{par_}"], k2 * 16 + 16)
                    if not isinstance(s, int) or s >= 1:
                        pe.wait_ge(S["htl5"], s)
                    transposes(2, tmp[:, par_, :], "ht5")
                if not isinstance(s, int) or 1 <= s <= RT:
                    p = 1 - par_
                    e = pe.value_load(eidi[0:1, bass.ds(s - 1, 1)], min_val=0, max_val=E - 1)
                    pe.wait_ge(S["htl5"], s)
                    if not isinstance(s, int) or s >= 3:
                        pe.wait_ge(S["a5"], s - 2)
                    for half in range(2):
                        last = product(PS[:, 4 * p + half, :], KD, hT[:, p],
                                       lambda k: part(WRh, e, k * 2 * FF + half * FF, FF),
                                       lambda k: part(WRl, e, k * 2 * FF + half * FF, FF))
                    last.then_inc(S["gu5"], 1)
                if not isinstance(s, int) or 2 <= s <= RT + 1:
                    pe.wait_ge(S["a5"], s - 1)
                    if not isinstance(s, int) or s >= 3:
                        pe.wait_ge(S["atl5"], s - 2)
                    a_transposes(par_, "at5")
                if not isinstance(s, int) or s >= 3:
                    e = pe.value_load(eidi[0:1, bass.ds(s - 3, 1)], min_val=0, max_val=E - 1)
                    pe.wait_ge(S["atl5"], s - 2)
                    if not isinstance(s, int) or s >= 4:
                        pe.wait_ge(S["yb5"], s - 3)
                    product(PS[:, 3, 0:D], KF, aT[:, 1 - par_], lambda k: part(WRh, e, KD * 2 * FF + k * D, D),
                            lambda k: part(WRl, e, KD * 2 * FF + k * D, D)).then_inc(S["y5"], 1)

            for s in range(4):
                step5(s, s % 2, s // 2)
            with pe.Fori(0, (RT - 5) // 2) as k:
                for s in range(2):
                    step5(k * 2 + (4 + s), s, k + 2)
            for s in range(RT - 1, RT + 3):
                step5(s, s % 2, s // 2)


_INS = ["L0_attn_feat_patch", "L0_attn_ln_w", "L0_attn_ln_b", "L0_attn_in_proj_W", "L0_attn_conv_w", "L0_attn_conv_b",
        "L0_attn_x_proj_W", "L0_attn_dt_proj_W", "L0_attn_dt_proj_b", "L0_attn_A_log", "L0_attn_D_param",
        "L0_attn_out_proj_W", "L0_ffn_router_w", "L0_ffn_gate_up_proj", "L0_ffn_down_proj", "L0_ffn_shared_gate_w",
        "L0_ffn_shared_up_w", "L0_ffn_shared_down_w", "L0_c", "L0_wmod"]


def _consts():
    import numpy as np
    ident = np.eye(P, dtype=np.float32)
    ltri = np.triu(np.ones((P, P), np.float32), 1)
    jrow = np.broadcast_to(np.tile(np.arange(NT, dtype=np.float32) * P, E), (P, E * NT))
    jtile = np.broadcast_to(np.arange(RT, dtype=np.float32), (P, RT))
    cst = np.concatenate([ident, ltri, jrow, jtile], 1)
    sel = np.zeros((3, B, NS, NTILE, P), np.float32)
    for n in range(NA):
        sel[:, 0, n, n, 0:DI] = 1
        sel[:, 1, n, n, DI:P] = 1
    for m in range(NB):
        sel[:, 1, m, NA + m, 0:D1B] = 1
        sel[:, 1, m + NB, NA + m, D1B:P] = 1
    return np.ascontiguousarray(cst), sel.reshape(SR, NTILE * P)


def kernel(**inputs):
    import numpy as np
    import concourse.bacc as bacc
    from concourse.bass_utils import run_bass_kernel_spmd
    nc = bacc.Bacc("TRN2", target_bir_lowering=False, num_devices=1)
    arrays = {f"in_{n}": np.ascontiguousarray(inputs[n]) for n in _INS}
    arrays["in_consts"], arrays["in_sel"] = _consts()
    args = [nc.dram_tensor(n, a.shape, mybir.dt.from_np(a.dtype), kind="ExternalInput").ap() for n, a in arrays.items()]
    o = nc.dram_tensor("out_0", (B, L, D), F32, kind="ExternalOutput").ap()
    adaln_block(nc, *args, o)
    r = run_bass_kernel_spmd(nc, [arrays], core_ids=[0])
    return r.results[0]["out_0"]
```

```python
import concourse.bass as bass
from concourse import mybir
from contextlib import ExitStack

F32 = mybir.dt.float32
BF16 = mybir.dt.bfloat16
I32 = mybir.dt.int32
ALU = mybir.AluOpType
ACT = mybir.ActivationFunctionType
AX = mybir.AxisListType

P = 128
B, L, D = 2, 2048, 256
DI, NS, RK = 96, 16, 6
E, FF = 8, 512
KD, KF = D // P, FF // P
CH = 512
NC = L // CH
TPC = CH // P
U = B * TPC
NT = B * L // P
D1A = P - DI
D1B = DI - D1A
NA, NB = NS, NS // 2
NTILE = NA + NB
RT = NT + E - 1
SR = 3 * B * NS
EW = KD * 2 * FF + KF * D
EPS = 1e-5
IN_T, IN_HI, GATE, UP, TANH, HID, HID_T, HID_HI, DOWN, RES = 0, 1, 2, 3, 3, 4, 5, 6, 7, 8
FIRST = 15
LAST_SLOTS = FIRST + 3 * (U - 1) + RES + 1
PROJ = {1 + 3 * k: k for k in range(U // 2)}
STATS = 12
CONV, SILU, SPLIT, ABS, LOG_IN, LOG, STEP, STEP_U = 0, 1, 4, 16, 17, 18, 19, 20
ITEM = {2 + 3 * k: k for k in range(5)}
ITEMS = 5
SPLIT_SLOTS = 3
PRO_SLOTS = STEP_U + 1
assert NTILE == 3 * U
EXPERTS_FROM, EXPERTS_EVERY = 5, 3
GT = 4
NG = NT // GT
ON_POOL = (1, 4)
SA, CA, GA, SB, CB, GB = range(6)


class Chain:

    def __init__(self, eng, sem):
        self.eng, self.sem, self.off, self.n = eng, sem, 0, 0
        self.met = None

    def inc(self, ins):
        ins.then_inc(self.sem, 1)
        self.n += 1
        return self.n

    def wait(self, n=None):
        self.eng.wait_ge(self.sem, self.off + (self.n if n is None else n))
        if self.met is not None:
            self.eng.sem_inc(self.met, 1)

    def link(self, ins):
        self.inc(ins)
        self.wait()

    def loop(self, base, it, per):
        self.off, self.n = base + it * per, 0

    def end(self, base, per, times):
        assert self.n == per, ("steps of the loop", self.n, per)
        self.off, self.n = 0, base + per * times


def flat(ap):
    return ap.rearrange("p a n -> p (a n)")


def adaln_block(nc, x, lnw, lnb, inW, convw, convb, xW, dtW, dtb, alog, dpar, outW, rW, guW, dnW,
                sgW, suW, sdW, cond, wmod, consts, selc, out):
    ctx = ExitStack()
    with ctx:
        def sb(name, shape, dt=F32):
            return ctx.enter_context(nc.sbuf_tensor(name, shape, dt))

        def sem(name):
            return ctx.enter_context(nc.semaphore(name))

        xs = nc.dram_tensor("xs", [NT * P, D], F32, kind="Internal").ap()
        ys = nc.dram_tensor("ys", [(NT + 1) * P, D], F32, kind="Internal").ap()

        R = sb("R", [P, NT, D])
        H = sb("H", [P, NT, D])
        WR = sb("WR", [P, E * EW])
        WRh = WR[:, 0:E * EW // 2].bitcast(BF16)
        WRl = WR[:, E * EW // 2:E * EW].bitcast(BF16)
        WSh = sb("WSh", [P, EW + KF * D], BF16)
        WSl = sb("WSl", [P, EW + KF * D], BF16)
        MODB = sb("MODB", [P, B, 3, D])
        CST = sb("CST", [P, 3 * P + E * NT + RT + NT + 2 + E])
        ident = CST[:, 0:P]
        ltri = CST[:, P:2 * P]
        jrow = CST[:, 2 * P:2 * P + E * NT].rearrange("p (e j) -> p e j", e=E)
        jtile = CST[:, 2 * P + E * NT:2 * P + E * NT + RT]
        CST2 = CST[:, 2 * P + E * NT + RT:]
        jcol = CST2[:, 0:P]
        jtok = CST2[:, P:P + NT]
        prow = CST2[:, P + NT:P + NT + 1]
        first = CST2[:, P + NT + 2:P + NT + 2 + E]
        trash = CST2[:, P + NT + 1:P + NT + 2]
        hT = sb("hT", [P, 2, 2, KD, P], BF16)
        sg = sb("sg", [P, 2, FF])
        av = sb("av", [P, 2, FF])
        aT = sb("aT", [P, 2, 2, KF, P], BF16)
        tmp = sb("tmp", [P, 2, D])
        yb = sb("yb", [P, 2, D])
        h2s = sb("h2s", [P, 2, D])
        st = sb("st", [P, U, 6])
        mv = sb("mv", [P, 2, U, 2])
        rs = sb("rs", [P, 2, U])
        nm = sb("nm", [P, 2, U])
        LG = sb("LG", [P, NT, E])
        wrT = sb("wrT", [P, KD, E])
        wrp = sb("wrp", [P, 2, KD, E], BF16)
        posi = sb("posi", [P, NT], I32)
        ptile = sb("ptile", [P, NT], I32)
        idin = sb("idin", [P, RT], I32)
        idout = sb("idout", [P, RT], I32)
        eidi = sb("eidi", [P, RT], I32)
        S1 = sb("S1", [P, NT])
        one = sb("one", [P, P])

        at = [0]

        def carve(*shape):
            n = 1
            for s in shape:
                n *= s
            ap = WR[:, at[0]:at[0] + n]
            at[0] += n
            if len(shape) == 1:
                return ap
            names = "abcd"[:len(shape)]
            return ap.rearrange(f"p ({' '.join(names)}) -> p {' '.join(names)}",
                                **{k: v for k, v in zip(names, shape)})

        XIN = carve(2, L + 2)
        MODA = carve(B, 3, D)
        winT = carve(3, KD, P)
        wxBT, wxCT = carve(2, SR), carve(2, SR)
        wxDT = carve(2, B * RK)
        wdtT = carve(2, P)
        woutT = carve(3, D)
        par = carve(2, 6)
        Apar = carve(NTILE)
        state = carve(NTILE)
        lnwc, lnbc = carve(KD), carve(KD)
        bia = carve(2)
        ysb = carve(2, CH)
        stx = carve(NT, 6)
        mvx = carve(NT, 2)
        rsx = carve(NT)
        nmx = carve(NT)
        sel = carve(NTILE * P // 2).bitcast(BF16).rearrange("p (t c) -> p t c", t=NTILE)
        BsCs = carve(NC * CH).bitcast(BF16).rearrange("p (m a c) -> p m a c", m=NC, a=2)
        cv = carve(2, CH)
        bc = carve(2, CH)
        vz = carve(2, CH)
        et = carve(2, CH)
        dr = carve(CH)
        spl = carve(2, CH)
        base_dyn = at[0]
        dA = carve(2, CH)
        cs = carve(2, CH)
        hs = carve(2, CH)
        g = carve(2, CH)
        assert at[0] <= E * EW
        at[0] = base_dyn
        STG = carve(EW)
        STG_gated = carve(B, KF * D)
        assert at[0] <= E * EW
        at[0] = base_dyn
        z = carve(U, D)
        zT = carve(B, KD, CH)
        cT, scT = carve(KD, B), carve(KD, B)
        cB = carve(KD, B, P)
        assert at[0] <= E * EW

        HF = H[:, TPC:NT // B, :].rearrange("p t d -> p (t d)")
        inR = HF[:, 0:3 * D].rearrange("p (k d) -> p k d", k=3)
        xR = HF[:, 768:768 + 6 * P].rearrange("p (m x d) -> p m x d", m=3, x=2)
        dtR = HF[:, 1536:1536 + 2 * B * RK].rearrange("p (x r) -> p x r", x=2)
        outR = HF[:, 1600:1600 + 3 * KD * P].rearrange("p (k m d) -> p k m d", k=KD, m=3)
        rR = HF[:, 2368:2368 + D]
        ROWS_END = 2368 + D

        PS = ctx.enter_context(nc.psum_tensor("PS", [P, 8, CH], F32))

        names = ("z0 wsg hp mp sp0 xsd ids hot tk finp r0l mev gates ex wl ab rt holda holdv holdp x sm wt wm cst ws wr xsz "
                 "d0 dch ach pch a0 t0 e0 w0 b0 m0 m1 "
                 "rv1 sq1 nm1 n1 h1 rv2 sq2 nm2 z1 zt zev xin xev "
                 "cv u dbc drr zz sp r1 dlt bs bb cb da cs sc g st y ye o x1 r0 "
                 "rv3 sq3 nm3 n3 h2 h3 ht htv gu sgs a atp atv y3 r3 lgc "
                 "oh rk pos s1 xr scd xt0 xt1 ht5 htv5 gu5 sg5 a5 at5 atv5 y5 yb5 ysd0 ysd1 fin od").split() + [f"gt{i}" for i in range(NG)] + "pi pv mx gg atl htl atl5 htl5 st00 st01 st10 st11 st20 st21 wh wlg wld wsh wsl spl rld".split()
        S = {n: sem("s_" + n) for n in names}
        WM = H[:, NT - KD * 3 * 2:NT, :].rearrange("p (k t) d -> p k (t d)", k=KD)
        SELF = WR[:, base_dyn:base_dyn + NTILE * P]

        block = ctx.enter_context(nc.Block())

        def tok(c, u):
            if u < 0:
                c, u = c - 1, u + U
            return (u // TPC) * (NT // B) + c * TPC + u % TPC

        def batch(u):
            return u % U // TPC

        def Rt(c, u):
            return flat(R[:, bass.ds(tok(c, u), 1), :])

        def Ht(c, u):
            return flat(H[:, bass.ds(tok(c, u), 1), :])


        def uu(c, X):
            return XIN[:, X, bass.ds(c * CH, CH)]

        def dl(c, X):
            return flat(H[:, bass.ds(c * TPC + X * TPC // 2, TPC // 2), :])

        def ww(c, X):
            return flat(H[:, bass.ds(NT // B + c * TPC + X * TPC // 2, TPC // 2), :])

        def parts(n, a, rows):
            return flat(BsCs[0:rows, bass.ds(n, 1), a, :])

        SLOT = [R[:, b * NT // B:b * NT // B + 2 * TPC, :].rearrange("p t d -> p (t d)") for b in range(B)]
        spill = [nc.dram_tensor(f"spill{b}", [P, 2 * TPC * D], F32, kind="Internal").ap() for b in range(B)]

        LATE = (E - 2) * EW // 2
        STAGES = ((SLOT[0], SLOT[1]),
                  (WR[:, LATE:LATE + KD * 2 * FF], WR[:, LATE + KD * 2 * FF:LATE + EW]),
                  (WR[:, E * EW // 2 + LATE:E * EW // 2 + LATE + KD * 2 * FF],
                   WR[:, E * EW // 2 + LATE + KD * 2 * FF:E * EW]))
        STAGE = [e % 3 for e in range(E - 2)] + [0, 0]

        def raw(e):
            return STAGES[STAGE[e]]

        def landed(e, part):
            return S[f"st{STAGE[e]}{part}"], 16 * STAGE[:e + 1].count(STAGE[e])

        hot_tile = WSl[:, 0:NT * 2 * RT].rearrange("p (t m r) -> p t m r", t=NT, m=2)
        IN_WSH = EW // P
        hot_rows = ((0, WSh[:, 0:EW].rearrange("p (t r) -> p t r", r=P)),
                    (IN_WSH, aT[:, :, :, :, :].rearrange("p a b k r -> p (a b k) r")[:, 0:NT - IN_WSH, :]))

        def wgu(W, k, half):
            return W[:, k * 2 * FF + half * FF:k * 2 * FF + (half + 1) * FF]

        def wdn(W, k, b):
            lo = KD * 2 * FF + (b * KF + k) * D
            return W[:, lo:lo + D]

        SMALL = [0]

        def walk(slot, c, n, slots=NTILE):
            for j in range(slots):
                slot(c, n, j)

        def lead(pro_slot, part):
            for j in range(*((0, 8), (8, 14), (14, PRO_SLOTS))[part]):
                pro_slot(None, 0, j)

        def item_bank(c):
            return 5 if c is not None else 6

        def last_sum(eng, ops, ch, groups, done):
            eng.wait_ge(S["rld"], 16 * B)
            for g in groups:
                eng.wait_ge(S[f"gt{g}"], 16)
                b, rows = g * GT * B // NT, slice(g * GT, (g + 1) * GT)
                gb = MODB[:, b:b + 1, GB - 3, :].to_broadcast([P, GT, D])
                ch.link(ops.tensor_tensor(H[:, rows, :], H[:, rows, :], gb, ALU.mult))
                ops.tensor_tensor(R[:, rows, :], R[:, rows, :], H[:, rows, :], ALU.add).then_inc(S[done], 1)

        def tile_at(f, j, after):
            u, r = divmod(j - FIRST - after, 3)
            if r != 0 or u >= U or not there(f, u):
                return None
            return u

        def reused(c, i):
            return not isinstance(c, int) or c >= 1 or i >= 2

        def scanned(c):
            return not isinstance(c, int) or c < NC

        def expert_at(c, j):
            e, r = divmod(j - EXPERTS_FROM, EXPERTS_EVERY)
            return e if isinstance(c, int) and c == NC and r == 0 and 0 <= e < E else None

        def proj_in(c, j):
            if scanned(c):
                return PROJ.get(j - 1)
            return j if j < U // 2 else None

        def proj_bank(c, k):
            return 5 if scanned(c) else k

        def there(f, u):
            return not isinstance(f, int) or 0 <= f * U + u < NT

        @block.sync
        def _(sp):
            def small(dst, src):
                sp.dma_start(dst, src).then_inc(S["sm"], 16)
                SMALL[0] += 16

            xv = x.rearrange("b (j p) d -> p b j d", p=P)
            for b in range(B):
                sp.dma_start(R[:, b * NT // B:(b + 1) * NT // B, :], xv[:, b]).then_inc(S["x"], 16)
            sp.dma_start(CST[:, :], consts).then_inc(S["cst"], 16)
            sp.dma_start(SELF[0:SR, :], selc).then_inc(S["cst"], 16)
            sp.dma_start(WM, wmod.rearrange("(k p) n -> p k n", p=P)).then_inc(S["wm"], 16)
            for k in range(KD):
                for b in range(B):
                    sp.dma_start(cT[:, k, b:b + 1], cond[b, k * P:(k + 1) * P].rearrange("(p a) -> p a", a=1)) \
                        .then_inc(S["wm"], 16)
            sp.wait_ge(S["z0"], 1)
            small(inR[0:DI, 0, :], inW)
            small(inR[DI:P, 1, :], inW[0:D1A, :])
            small(inR[0:D1B, 2, :], inW[D1A:DI, :])
            small(inR[D1B:P, 2, :], inW[D1A:DI, :])
            for m in range(2):
                r0 = RK + m * NS
                for rep in range(3):
                    q = rep * B * NS
                    small(xR[q:q + NS, m, 0, 0:DI], xW[r0:r0 + NS, :])
                    small(xR[q + NS:q + 2 * NS, m, 0, DI:P], xW[r0:r0 + NS, 0:D1A])
                    small(xR[q + NS:q + 2 * NS, m, 1, 0:D1B], xW[r0:r0 + NS, D1A:DI])
            small(xR[0:RK, 2, 0, 0:DI], xW[0:RK, :])
            small(xR[RK:2 * RK, 2, 0, DI:P], xW[0:RK, 0:D1A])
            small(xR[RK:2 * RK, 2, 1, 0:D1B], xW[0:RK, D1A:DI])
            small(dtR[0:DI, 0, 0:RK], dtW)
            small(dtR[DI:P, 0, RK:2 * RK], dtW[0:D1A, :])
            small(dtR[0:D1B, 1, RK:2 * RK], dtW[D1A:DI, :])
            small(dtR[D1B:P, 1, RK:2 * RK], dtW[D1A:DI, :])
            ov = outW.rearrange("(k p) d -> p k d", p=P)
            small(outR[:, :, 0, 0:DI], ov)
            small(outR[:, :, 1, DI:P], ov[:, :, 0:D1A])
            small(outR[:, :, 2, 0:D1B], ov[:, :, D1A:DI])
            small(outR[:, :, 2, D1B:P], ov[:, :, D1A:DI])
            small(rR[0:E, :], rW)
            for k in range(KD):
                small(lnwc[:, k:k + 1], lnw[k * P:(k + 1) * P].rearrange("(p a) -> p a", a=1))
                small(lnbc[:, k:k + 1], lnb[k * P:(k + 1) * P].rearrange("(p a) -> p a", a=1))

            def rows(x_, p0, p1, d0):
                n = p1 - p0
                small(par[p0:p1, x_, 0:3], convw[d0:d0 + n, 0, :])
                small(par[p0:p1, x_, 3:4], convb[d0:d0 + n].rearrange("(p a) -> p a", a=1))
                small(par[p0:p1, x_, 4:5], dtb[d0:d0 + n].rearrange("(p a) -> p a", a=1))
                if not (x_ == 1 and p0 > 0):
                    small(par[p0:p1, x_, 5:6], dpar[d0:d0 + n].rearrange("(p a) -> p a", a=1))

            rows(0, 0, DI, 0)
            rows(0, DI, P, 0)
            rows(1, 0, D1B, D1A)
            rows(1, D1B, P, D1A)
            small(Apar[0:DI, 0:NA], alog)
            small(Apar[DI:P, 0:NA], alog[0:D1A, :])
            small(Apar[0:D1B, NA:NTILE], alog[D1A:DI, 0:NB])
            small(Apar[D1B:P, NA:NTILE], alog[D1A:DI, NB:NS])

            sp.wait_ge(S["xev"], 2 * NC)
            for k in range(KD):
                sp.dma_start(wgu(STG, k, 0), sgW[k * P:(k + 1) * P, :]).then_inc(S["ws"], 16)
                sp.dma_start(wgu(STG, k, 1), suW[k * P:(k + 1) * P, :]).then_inc(S["ws"], 16)
            sp.dma_start(STG[:, KD * 2 * FF:EW].rearrange("p (k n) -> p k n", k=KF),
                         sdW.rearrange("(k p) n -> p k n", p=P)).then_inc(S["ws"], 16)
            sp.wait_ge(S["r3"], 2 * U)
            for b in range(B):
                sp.dma_start(spill[b], SLOT[b]).then_inc(S["spl"], 16)
            sp.wait_ge(S["spl"], 16 * B)
            sp.wait_ge(S["x1"], NT)
            sp.wait_ge(S["st"], NC * NTILE)
            for e in range(E):
                before = [d for d in range(e) if STAGE[d] == STAGE[e]]
                if before:
                    sp.wait_ge(S["wlg"], before[-1] + 1)
                sp.dma_start(raw(e)[0][:, 0:KD * 2 * FF].rearrange("p (k n) -> p k n", k=KD),
                             guW[e].rearrange("(k p) n -> p k n", p=P)).then_inc(landed(e, 0)[0], 16)
                if before:
                    sp.wait_ge(S["wld"], before[-1] + 1)
                sp.dma_start(raw(e)[1][:, 0:KF * D].rearrange("p (k n) -> p k n", k=KF),
                             dnW[e].rearrange("(k p) n -> p k n", p=P)).then_inc(landed(e, 1)[0], 16)
            sp.wait_ge(S["wlg"], E)
            sp.wait_ge(S["wld"], E)
            for b in range(B):
                sp.dma_start(SLOT[b], spill[b]).then_inc(S["rld"], 16)

            def group(dram, g):
                return dram[g * GT * P:(g + 1) * GT * P, :].rearrange("(t p) d -> p t d", p=P)

            for g in range(NG):
                sp.wait_ge(S["xr"], (g + 1) * GT)
                sp.dma_start(group(xs, g), H[:, g * GT:(g + 1) * GT, :]).then_inc(S["xsd"], 16)
            sp.wait_ge(S["xsd"], 16 * NG)
            sp.wait_ge(S["ysd0"], 16 * ((RT + 1) // 2))
            sp.wait_ge(S["ysd1"], 16 * (RT // 2))
            for g in range(NG):
                sp.dma_start(H[:, g * GT:(g + 1) * GT, :], group(ys, g)).then_inc(S[f"gt{g}"], 16)

        @block.gpsimd
        def _(gp):
            ch = Chain(gp, S["pch"])
            gp.wait_ge(S["gates"], 1)
            ch.met = S["holdp"]
            b0 = ch.n
            with gp.Fori(0, NC // 2) as c:
                ch.loop(b0, c, 2 * U)
                for u in range(U):
                    gp.wait_ge(S["h1"], c * U + u + 1)
                    gp.sem_inc(S["holdp"], 1)
                    ch.link(nc.gpsimd.tensor_tensor(tmp[:, u % 2, :], Ht(c, u),
                                                    MODA[:, u // TPC, GA, :], ALU.mult))
                    ch.link(nc.gpsimd.tensor_tensor(Rt(c, u), Rt(c, u), tmp[:, u % 2, :], ALU.add))
            ch.end(b0, 2 * U, NC // 2)
            gp.sem_inc(S["r0"], 1)

            def pro_slot(c, n, j):
                a, k = divmod(j - SPLIT, SPLIT_SLOTS)
                if a not in (0, 1) or k not in (0, 2):
                    return
                if k == 0:
                    gp.wait_ge(S["pv"], n * ITEMS + 1 + a)
                    gp.wait_ge(S["hp"], n * 2 + 1 + a)
                    gp.sem_inc(S["holdp"], 1)
                    nc.gpsimd.tensor_tensor(spl[0:SR, a, :], bc[0:SR, a, :], parts(n, a, SR), ALU.subtract) \
                        .then_inc(S["sp0"], 1)
                else:
                    gp.wait_ge(S["mp"], n * 2 + 1 + a)
                    gp.sem_inc(S["holdp"], 1)
                    nc.gpsimd.tensor_tensor(parts(n, a, B * NS), spl[0:B * NS, a, :], parts(n, a, B * NS),
                                            ALU.subtract).then_inc(S["bs"], 1)

            def scan_tile(c, i):
                gp.wait_ge(S["sc"], c * NTILE + i + 1)
                gp.wait_ge(S["cs"], c * NTILE + i + 1)
                if reused(c, i):
                    gp.wait_ge(S["y"], c * NTILE + i - 1)
                nc.gpsimd.tensor_tensor(g[:, i % 2, :], hs[:, i % 2, :], cs[:, i % 2, :], ALU.mult) \
                    .then_inc(S["g"], 1)
                nc.gpsimd.tensor_copy(state[:, i:i + 1], hs[:, i % 2, CH - 1:CH]).then_inc(S["st"], 1)

            def ffn_input(f, u):
                q = f * U
                gp.wait_ge(S["n3"], q + u + 1)
                gp.sem_inc(S["holdp"], 1)
                ch.link(nc.gpsimd.tensor_tensor(Ht(f, u), Ht(f, u), MODB[:, batch(u), CB - 3, :], ALU.mult))
                if there(f, u - 2):
                    gp.wait_ge(S["ht"], q + u - 1)
                    gp.sem_inc(S["holdp"], 1)
                nc.gpsimd.tensor_tensor(h2s[:, u % 2, :], Ht(f, u), MODB[:, batch(u), SB - 3, :], ALU.add) \
                    .then_inc(S["h2"], 1)
                gp.wait_ge(S["h2"], q + u + 1)
                gp.sem_inc(S["holdp"], 1)
                nc.gpsimd.tensor_tensor(Ht(f, u), Ht(f, u), MODB[:, batch(u), SB - 3, :], ALU.add) \
                    .then_inc(S["h3"], 1)

            def slot(c, n, j):
                if scanned(c):
                    scan_tile(c, j)
                if n is not None:
                    pro_slot(c, n, j)
                if (u := tile_at(c - 1, j, IN_T - 2)) is not None:
                    ffn_input(c - 1, u)
                if (e := expert_at(c, j)) is not None:
                    gp.wait_ge(S["wh"], 2 * e + 1)
                    if e >= E - 2:
                        gp.wait_ge(S["wld"], E - 2)
                    lo, hi = e * EW, e * EW + KD * 2 * FF
                    nc.gpsimd.tensor_tensor(WRl[:, lo:hi], raw(e)[0][:, 0:KD * 2 * FF], WRh[:, lo:hi], ALU.subtract) \
                        .then_inc(S["wlg"], 1)

            for part in range(3):
                lead(pro_slot, part)
            walk(slot, 0, 1)
            walk(slot, 1, 2)
            b0, per = ch.n, U
            with gp.Fori(2, NC - 1) as c:
                ch.loop(b0, c - 2, per)
                walk(slot, c, c + 1)
            ch.end(b0, per, NC - 3)
            walk(slot, NC - 1, None)
            walk(slot, NC, None, LAST_SLOTS)
            gp.wait_ge(S["ids"], 1)
            gp.wait_ge(S["xsd"], 16 * NG)

            def gather(t):
                gp.indirect_dma_start(out=tmp[:, t % 2, :], out_offset=None, in_=xs[:, :],
                                      in_offset=bass.IndirectOffsetOnAxis(ap=idin[:, t:t + 1], axis=0)) \
                    .then_inc(S[f"xt{t % 2}"], 16)

            def scatter(t):
                gp.wait_ge(S["yb5"], t + 1)
                if t >= 1:
                    gp.wait_ge(S[f"ysd{(t - 1) % 2}"], 16 * ((t - 1) // 2 + 1))
                gp.indirect_dma_start(out=ys[:, :], out_offset=bass.IndirectOffsetOnAxis(ap=idout[:, t:t + 1], axis=0),
                                      in_=yb[:, t % 2, :], in_offset=None).then_inc(S[f"ysd{t % 2}"], 16)

            for t in range(RT):
                if t >= 2:
                    gp.wait_ge(S["ht5"], t - 1)
                gather(t)
                if t >= 5:
                    scatter(t - 5)
            for t in range(RT - 5, RT):
                scatter(t)
            last_sum(gp, nc.gpsimd, ch, ON_POOL, "finp")

        @block.scalar
        def _(act):
            act.wait_ge(S["wm"], 16 * 5)
            nc.scalar.activation(scT[:, :, :], cT[:, :, :], ACT.Silu).then_inc(S["a0"], 1)
            def root(c, which, rvs, sqs):
                act.wait_ge(S[rvs], c + 1)
                nc.scalar.activation(rs[:, which, :], rs[:, which, :], ACT.Sqrt).then_inc(S[sqs], 1)

            def normed(c, nms):
                act.wait_ge(S[nms], c + 1)
                act.sem_inc(S["holda"], 1)

            def normalise_x(c):
                act.wait_ge(S["nm1"], c * 2 + 2)
                act.sem_inc(S["holda"], 1)
                for u in range(U):
                    nc.scalar.activation(Ht(c, u), Rt(c, u), ACT.Identity, bias=nm[:, 0, u:u + 1],
                                         scale=rs[:, 0, u:u + 1]).then_inc(S["n1"], 1)

            def normalise_h(c):
                root(c, 1, "rv2", "sq2")
                normed(c, "nm2")
                for u in range(U):
                    nc.scalar.activation(z[:, u, :], Ht(c, u), ACT.Identity, bias=nm[:, 1, u:u + 1],
                                         scale=rs[:, 1, u:u + 1]).then_inc(S["z1"], 1)

            def front(c):
                normalise_h(c)
                for b in range(B):
                    act.wait_ge(S["zt"], c * U + (b + 1) * TPC)
                    nc.scalar.activation(flat(zT[:, b, :, :]), flat(PS[:, KD * b:KD * b + KD, :]), ACT.Copy) \
                        .then_inc(S["zev"], 1)
                if not isinstance(c, int) or c + 2 < NC:
                    normalise_x(c + 2)
                act.wait_ge(S["xin"], c + 1)
                act.sem_inc(S["holda"], 1)
                for X in range(2):
                    nc.scalar.activation(XIN[:, X, bass.ds(c * CH + 1, CH)], PS[:, 4 + X, :], ACT.Identity,
                                         bias=bia[:, X:X + 1]).then_inc(S["xev"], 1)

            act.wait_ge(S["rv1"], 1)
            nc.scalar.activation(rsx[:, :], rsx[:, :], ACT.Sqrt).then_inc(S["sq1"], 1)
            normalise_x(0)
            act.wait_ge(S["sm"], SMALL[0])
            nc.scalar.activation(Apar[:, :], Apar[:, :], ACT.Exp).then_inc(S["a0"], 1)
            act.wait_ge(S["m0"], 1)
            act.wait_ge(S["t0"], 1)
            normalise_x(1)
            act.wait_ge(S["m1"], 1)
            with act.Fori(0, NC - 2) as c:
                front(c)
            front(NC - 2)

            def pro_slot(c, n, j):
                if j == SILU:
                    for X in range(2):
                        act.wait_ge(S["cv"], n * 2 + X + 1)
                        act.sem_inc(S["holda"], 1)
                        nc.scalar.activation(uu(n, X), cv[:, X, :], ACT.Silu, bias=par[:, X, 3:4]).then_inc(S["u"], 1)
                if (k := ITEM.get(j - 1)) is not None:
                    act.wait_ge(S["pi"], n * ITEMS + k + 1)
                    if k < 2:
                        nc.scalar.activation(parts(n, k, SR), PS[0:SR, item_bank(c), :], ACT.Copy).then_inc(S["hp"], 1)
                        nc.scalar.activation(bc[0:SR, k, :], PS[0:SR, item_bank(c), :], ACT.Copy).then_inc(S["pv"], 1)
                    elif k == 2:
                        nc.scalar.activation(dr[0:B * RK, :], PS[0:B * RK, item_bank(c), :], ACT.Copy).then_inc(S["pv"], 1)
                    else:
                        nc.scalar.activation(vz[:, k - 3, :], PS[:, item_bank(c), :], ACT.Identity, bias=par[:, k - 3, 4:5]) \
                            .then_inc(S["pv"], 1)
                a, k = divmod(j - SPLIT, SPLIT_SLOTS)
                if a in (0, 1) and k == 1:
                    act.wait_ge(S["sp0"], n * 2 + 1 + a)
                    act.sem_inc(S["holda"], 1)
                    nc.scalar.activation(parts(n, a, 2 * B * NS), spl[0:2 * B * NS, a, :], ACT.Copy).then_inc(S["mp"], 1)
                if j == ABS:
                    act.wait_ge(S["pv"], n * ITEMS + ITEMS)
                    for X in range(2):
                        nc.scalar.activation(et[:, X, :], vz[:, X, :], ACT.Abs).then_inc(S["ab"], 1)
                    for X in range(2):
                        act.wait_ge(S["ab"], n * 2 + X + 1)
                        nc.scalar.activation(et[:, X, :], et[:, X, :], ACT.Exp, scale=-1.0).then_inc(S["ex"], 1)
                if j == LOG:
                    for X in range(2):
                        act.wait_ge(S["wl"], n * 2 + X + 1)
                        nc.scalar.activation(cv[:, X, :], cv[:, X, :], ACT.Ln).then_inc(S["sp"], 1)

            def decays(c, i):
                X = int(i >= NA)
                if i == 0 or i == NA:
                    act.wait_ge(S["dlt"], c * 2 + X + 1)
                if reused(c, i):
                    act.wait_ge(S["sc"], c * NTILE + i - 1)
                act.sem_inc(S["holda"], 1)
                nc.scalar.activation(dA[:, i % 2, :], dl(c, X), ACT.Exp, scale=Apar[:, i:i + 1]) \
                    .then_inc(S["da"], 1)

            def scan_tile(c, n, i):
                if i + 1 < NTILE:
                    decays(c, i + 1)
                elif n is not None:
                    decays(n, 0)
                act.wait_ge(S["cb"], c * NTILE + i + 1)
                if reused(c, i):
                    act.wait_ge(S["g"], c * NTILE + i - 1)
                nc.scalar.activation(cs[:, i % 2, :], PS[:, 2, :], ACT.Copy).then_inc(S["cs"], 1)

            def rows_in(f, u):
                nc.scalar.activation(Ht(f, u), Rt(f, u), ACT.Identity, bias=nm[:, 0, u % U:u % U + 1],
                                     scale=rs[:, 0, u % U:u % U + 1]).then_inc(S["n3"], 1)

            def ffn_slot(f, j):
                q = f * U
                if (u := tile_at(f, j, HID_HI)) is not None:
                    act.wait_ge(S["atp"], q + u + 1)
                    nc.scalar.activation(flat(aT[:, u % 2, 0, :, :]), PS[:, 6, :], ACT.Copy).then_inc(S["atv"], 1)
                if (u := tile_at(f, j, IN_HI)) is not None:
                    act.wait_ge(S["ht"], q + u + 1)
                    nc.scalar.activation(flat(hT[:, u % 2, 0, :, :]), PS[:, 6, 0:D], ACT.Copy).then_inc(S["htv"], 1)
                if (u := tile_at(f, j, TANH)) is not None:
                    act.wait_ge(S["gg"], q + u + 1)
                    nc.scalar.activation(sg[:, u % 2, :], PS[:, 4, :], ACT.Tanh, scale=0.5).then_inc(S["sgs"], 1)
                if there(f, 0) and j == STATS:
                    root(f, 0, "rv3", "sq3")
                if there(f, 0) and j == STATS + 1:
                    normed(f, "nm3")
                    rows_in(f, 0)
                    rows_in(f, 1)
                if (u := tile_at(f, j, IN_T - 4)) is not None and not 0 <= u < 2:
                    rows_in(f, u)

            def high_parts(hi, src, n, half):
                nc.scalar.activation(hi, src, ACT.Copy, scale=0.5 if half else 1.0).then_inc(S[n], 1)

            def split_expert(e):
                if e >= E - 2:
                    act.wait_ge(S["wlg"], E - 2)
                    act.wait_ge(S["wld"], E - 2)
                for m, (lo, n) in enumerate(((0, KD * 2 * FF), (KD * 2 * FF, KF * D))):
                    act.wait_ge(*landed(e, m))
                    high_parts(WRh[:, e * EW + lo:e * EW + lo + n], raw(e)[m][:, 0:n], "wh", m == 1)

            def slot(c, n, j):
                if scanned(c):
                    scan_tile(c, n, j)
                if n is not None:
                    pro_slot(c, n, j)
                ffn_slot(c - 1, j)
                if (e := expert_at(c, j)) is not None:
                    split_expert(e)

            lead(pro_slot, 0)
            front(NC - 1)
            lead(pro_slot, 1)
            act.wait_ge(S["ws"], 16 * (2 * KD + 1))
            high_parts(WSh[:, 0:KD * 2 * FF], STG[:, 0:KD * 2 * FF], "wsh", False)
            act.wait_ge(S["wsg"], B)
            high_parts(WSh[:, KD * 2 * FF:], flat(STG_gated), "wsh", True)
            lead(pro_slot, 2)
            act.wait_ge(S["wsl"], 2)
            decays(0, 0)
            walk(slot, 0, 1)
            walk(slot, 1, 2)
            with act.Fori(2, NC - 1) as c:
                walk(slot, c, c + 1)
            walk(slot, NC - 1, None)
            walk(slot, NC, None, LAST_SLOTS)
            act.wait_ge(S["s1"], 1)
            nc.scalar.activation(S1[:, :], S1[:, :], ACT.Sigmoid).then_inc(S["a0"], 1)
            act.wait_ge(S["a0"], 3)
            act.wait_ge(S["h3"], NT)
            for t in range(NT):
                nc.scalar.activation(H[:, t, :], H[:, t, :], ACT.Copy, scale=S1[:, t:t + 1]).then_inc(S["xr"], 1)

            def step5(s, par_):
                if not isinstance(s, int) or s < RT:
                    act.wait_ge(S["ht5"], s + 1)
                    nc.scalar.activation(flat(hT[:, par_, 0, :, :]), PS[:, 2, 0:D], ACT.Copy).then_inc(S["htv5"], 1)
                if not isinstance(s, int) or 1 <= s <= RT:
                    act.wait_ge(S["gu5"], s)
                    nc.scalar.activation(sg[:, 1 - par_, :], PS[:, 4 * (1 - par_), :], ACT.Tanh, scale=0.5) \
                        .then_inc(S["sg5"], 1)
                if not isinstance(s, int) or 2 <= s <= RT + 1:
                    act.wait_ge(S["at5"], s - 1)
                    nc.scalar.activation(flat(aT[:, par_, 0, :, :]), PS[:, 6, :], ACT.Copy).then_inc(S["atv5"], 1)

            for s in range(3):
                step5(s, s % 2)
            with act.Fori(0, (RT - 3) // 2) as k:
                for s in range(2):
                    step5(k * 2 + (3 + s), (3 + s) % 2)
            for s in range(RT, RT + 3):
                step5(s, s % 2)
            for g in range(NG):
                on_pool = sum(h in ON_POOL for h in range(g + 1))
                if g in ON_POOL:
                    act.wait_ge(S["finp"], on_pool)
                else:
                    act.wait_ge(S["fin"], g + 1 - on_pool)
                b, l = divmod(g * GT * P, L)
                act.dma_start(out[b, l:l + GT * P, :].rearrange("(t p) d -> p t d", p=P),
                              R[:, g * GT:(g + 1) * GT, :]).then_inc(S["od"], 16)
            act.wait_ge(S["od"], 16 * NG)

        @block.vector
        def _(v):
            V = nc.vector
            ch = Chain(v, S["dch"])
            ch.link(V.memset(HF[:, 0:ROWS_END], 0.0))
            ch.link(V.memset(XIN[:, :, :], 0.0))
            ch.inc(V.memset(state[:, :], 0.0))
            ch.inc(V.memset(one[:, :], 1.0))
            ch.link(V.memset(par[:, :, :], 0.0))
            v.sem_inc(S["z0"], 1)
            v.wait_ge(S["x"], 16 * B)
            n0 = ch.n
            for t in range(NT):
                ch.inc(V.bn_stats(stx[:, t, :], R[:, tok(t // U, t % U), :]))
            v.wait_ge(S["a0"], 1)
            V.tensor_copy(cB[:, :, :, :], scT[:, :, :].unsqueeze(3).to_broadcast([P, KD, B, P])).then_inc(S["b0"], 1)
            for t in range(NT):
                ch.wait(n0 + t + 1)
                ch.inc(V.bn_aggr(mvx[:, t, :], stx[:, t, :]))
            ch.wait()
            ch.link(V.tensor_scalar(rsx[:, :], mvx[:, :, 1], EPS, None, ALU.add))
            V.reciprocal(rsx[:, :], rsx[:, :]).then_inc(S["rv1"], 1)
            v.wait_ge(S["cst"], 32)
            ch.link(V.tensor_copy(sel[0:SR, :, :].rearrange("p t c -> p (t c)"), SELF[0:SR, :]))
            v.wait_ge(S["sq1"], 1)
            ch.link(V.scalar_tensor_tensor(nmx[:, :], mvx[:, :, 0], -1.0, rsx[:, :], ALU.mult, ALU.mult))
            def aggregate(which, rvs):
                for u in range(U):
                    ch.inc(V.bn_aggr(mv[:, which, u, :], st[:, u, :]))
                ch.wait()
                ch.link(V.tensor_scalar(rs[:, which, :], mv[:, which, :, 1], EPS, None, ALU.add))
                V.reciprocal(rs[:, which, :], rs[:, which, :]).then_inc(S[rvs], 1)

            def mean_term(which, c, sqs, nms):
                v.wait_ge(S[sqs], c + 1)
                V.scalar_tensor_tensor(nm[:, which, :], mv[:, which, :, 0], -1.0, rs[:, which, :], ALU.mult, ALU.mult) \
                    .then_inc(S[nms], 1)

            def norm_in(c):
                V.tensor_copy(rs[:, 0, :], rsx[:, bass.ds(c * U, U)]).then_inc(S["nm1"], 1)
                V.tensor_copy(nm[:, 0, :], nmx[:, bass.ds(c * U, U)]).then_inc(S["nm1"], 1)

            def modulate(c):
                n0 = ch.n
                for u in range(U):
                    v.wait_ge(S["n1"], c * U + u + 1)
                    ch.inc(V.tensor_tensor(Ht(c, u), Ht(c, u), MODA[:, u // TPC, CA, :], ALU.mult))
                for u in range(U):
                    ch.wait(n0 + u + 1)
                    V.tensor_tensor(Ht(c, u), Ht(c, u), MODA[:, u // TPC, SA, :], ALU.add).then_inc(S["h1"], 1)

            def stats_h(c):
                if not isinstance(c, int) or c >= 1:
                    v.wait_ge(S["z1"], c * U)
                v.wait_ge(S["h1"], c * U + U)
                if ch.met is not None:
                    v.sem_inc(S["holdv"], 1)
                for u in range(U):
                    ch.inc(V.bn_stats(st[:, u, :], Ht(c, u)))
                ch.wait()
                aggregate(1, "rv2")

            def front(c):
                mean_term(1, c, "sq2", "nm2")
                if not isinstance(c, int) or c + 1 < NC:
                    modulate(c + 1)
                if not isinstance(c, int) or c + 2 < NC:
                    norm_in(c + 2)
                if not isinstance(c, int) or c + 1 < NC:
                    stats_h(c + 1)

            norm_in(0)
            v.wait_ge(S["m0"], 1)
            for b in range(B):
                for j in range(3):
                    for hf in range(2):
                        m = 2 * j + hf
                        dst = (MODA if m < 3 else MODB)[:, b, m % 3, :]
                        src = PS[:, 3 * b + j, hf * D:(hf + 1) * D]
                        if m in (CA, CB):
                            ch.inc(V.tensor_scalar(dst, src, 1.0, None, ALU.add))
                        else:
                            ch.inc(V.tensor_copy(dst, src))
            ch.wait()
            v.sem_inc(S["mev"], 1)
            modulate(0)
            norm_in(1)
            v.wait_ge(S["t0"], 1)
            for m in range(3):
                for k in range(KD):
                    ch.inc(V.tensor_copy(winT[:, m, k, :], PS[:, m // 2, ((m % 2) * KD + k) * P:((m % 2) * KD + k + 1) * P]))
            for m, dst, n in ((0, wxBT, SR), (1, wxCT, SR), (2, wxDT, B * RK)):
                for X in range(2):
                    ch.inc(V.tensor_copy(dst[:, X, :], PS[:, 2 + (2 * m + X) // 4, ((2 * m + X) % 4) * P:((2 * m + X) % 4) * P + n]))
            for X in range(2):
                ch.inc(V.tensor_copy(wdtT[0:B * RK, X, :], PS[0:B * RK, 3, (2 + X) * P:(3 + X) * P]))
            for m in range(3):
                for k in range(KD):
                    ch.inc(V.tensor_copy(woutT[:, m, k * P:(k + 1) * P], PS[:, 4 + m // 2, ((m % 2) * KD + k) * P:((m % 2) * KD + k + 1) * P]))
            for k in range(KD):
                ch.inc(V.tensor_copy(wrT[:, k, :], PS[:, 5, (2 + k) * P:(2 + k) * P + E]))
            ch.wait()
            ch.link(V.tensor_copy(wrp[:, 0, :, :], wrT[:, :, :]))
            ch.link(V.tensor_tensor(wrp[:, 1, :, :], wrT[:, :, :], wrp[:, 0, :, :], ALU.subtract))
            v.sem_inc(S["e0"], 1)
            v.wait_ge(S["w0"], 1)
            ch.inc(V.tensor_copy(bia[:, :], PS[:, 7, 0:2]))
            for m in range(3):
                for k in range(KD):
                    ch.inc(V.tensor_scalar(winT[:, m, k, :], winT[:, m, k, :], lnwc[:, k:k + 1], None, ALU.mult))
            ch.wait()
            v.sem_inc(S["m1"], 1)
            def bound_gate(gate):
                sgn = h2s[:, :, :]
                mag = yb[:, :, :]
                ch.inc(V.tensor_scalar(sgn, gate, 0.0, None, ALU.is_ge))
                ch.link(V.tensor_scalar(mag, gate, -1.0, None, ALU.mult))
                ch.inc(V.tensor_scalar(sgn, sgn, 2.0, -1.0, ALU.mult, ALU.add))
                ch.link(V.tensor_tensor(mag, mag, gate, ALU.max))
                ch.link(V.tensor_scalar(mag, mag, 0.25, None, ALU.max))
                ch.link(V.tensor_tensor(gate, sgn, mag, ALU.mult))

            bound_gate(MODA[:, :, GA, :])
            for m in range(3):
                ch.inc(V.tensor_tensor(woutT[:, m, :], woutT[:, m, :], MODA[:, int(m > 0), GA, :], ALU.mult))
            ch.wait()
            v.sem_inc(S["gates"], 1)
            stats_h(0)
            ch.met = S["holdv"]
            b0, per = ch.n, 2 * U + 1 + U
            with v.Fori(0, NC - 2) as c:
                ch.loop(b0, c, per)
                front(c)
            ch.end(b0, per, NC - 2)
            ch.met = None
            front(NC - 2)
            v.wait_ge(S["xev"], 4)

            def pro_slot(c, n, j):
                if j in (CONV, CONV + 1):
                    X = j - CONV
                    ch.link(V.tensor_scalar(cv[:, X, :], XIN[:, X, bass.ds(n * CH, CH)], par[:, X, 0:1], None, ALU.mult))
                    ch.link(V.scalar_tensor_tensor(cv[:, X, :], XIN[:, X, bass.ds(n * CH + 1, CH)], par[:, X, 1:2],
                                                   cv[:, X, :], ALU.mult, ALU.add))
                    V.scalar_tensor_tensor(cv[:, X, :], XIN[:, X, bass.ds(n * CH + 2, CH)], par[:, X, 2:3],
                                           cv[:, X, :], ALU.mult, ALU.add).then_inc(S["cv"], 1)
                if j == ABS:
                    v.wait_ge(S["pv"], n * ITEMS + ITEMS)
                    for X in range(2):
                        V.tensor_scalar(dl(n, X), vz[:, X, :], 0.0, None, ALU.max).then_inc(S["mx"], 1)
                if j == LOG_IN:
                    for X in range(2):
                        v.wait_ge(S["ex"], n * 2 + X + 1)
                        ch.link(V.tensor_scalar(cv[:, X, :], et[:, X, :], 1.0, None, ALU.add))
                        V.scalar_tensor_tensor(et[:, X, :], cv[:, X, :], -1.0, et[:, X, :], ALU.add, ALU.subtract) \
                            .then_inc(S["wl"], 1)
                if j == STEP:
                    for X in range(2):
                        v.wait_ge(S["mx"], n * 2 + X + 1)
                        v.wait_ge(S["sp"], n * 2 + X + 1)
                        ch.link(V.tensor_tensor(dl(n, X), dl(n, X), cv[:, X, :], ALU.add))
                        V.tensor_tensor(dl(n, X), dl(n, X), et[:, X, :], ALU.subtract).then_inc(S["dlt"], 1)
                if j == STEP_U:
                    for X in range(2):
                        v.wait_ge(S["dlt"], n * 2 + X + 1)
                        v.wait_ge(S["u"], n * 2 + X + 1)
                        ch.inc(V.scalar_tensor_tensor(ww(n, X), dl(n, X), 0.001, uu(n, X), ALU.mult, ALU.mult))
                    ch.wait()

            def y_out(c, X):
                v.wait_ge(S["y"], c * NTILE + (NA if X == 0 else NTILE))
                V.scalar_tensor_tensor(ysb[:, X, :], uu(c, X), par[:, X, 5:6], PS[:, 3, :],
                                       ALU.mult, ALU.add).then_inc(S["ye"], 1)

            def scan_tile(c, i):
                X = int(i >= NA)
                v.wait_ge(S["bb"], c * NTILE + i + 1)
                ch.link(V.tensor_tensor(PS[:, i % 2, :], ww(c, X), PS[:, i % 2, :], ALU.mult))
                v.wait_ge(S["da"], c * NTILE + i + 1)
                if reused(c, i):
                    v.wait_ge(S["g"], c * NTILE + i - 1)
                    v.wait_ge(S["st"], c * NTILE + i - 1)
                V.tensor_tensor_scan(hs[:, i % 2, :], dA[:, i % 2, :], PS[:, i % 2, :], state[:, i:i + 1],
                                     ALU.mult, ALU.add).then_inc(S["sc"], 1)
            def proj_slot(c, f, j):
                if j == 0:
                    y_out(f, 1)
                if (k := proj_in(c, j)) is not None:
                    bank = proj_bank(c, k)
                    v.wait_ge(S["o"], f * U + 2 * k + 2)
                    for u in (2 * k, 2 * k + 1):
                        V.tensor_tensor(Rt(f, u), Rt(f, u), PS[:, bank, (u % 2) * D:(u % 2 + 1) * D], ALU.add) \
                            .then_inc(S["x1"], 1)
                    v.wait_ge(S["x1"], f * U + 2 * k + 2)
                    v.sem_inc(S["holdv"], 1)
                    for u in (2 * k, 2 * k + 1):
                        ch.inc(V.bn_stats(st[:, u, :], Rt(f, u)))
                if j == STATS:
                    if there(f, -1):
                        v.wait_ge(S["n3"], f * U)
                    ch.met = S["holdv"]
                    ch.wait()
                    aggregate(0, "rv3")
                    ch.met = None
                if j == STATS + 1:
                    mean_term(0, f, "sq3", "nm3")

            def ffn_slot(f, j):
                q = f * U
                if (u := tile_at(f, j, HID_HI)) is not None:
                    v.wait_ge(S["atv"], q + u + 1)
                    V.tensor_tensor(flat(aT[:, u % 2, 1, :, :]), PS[:, 6, :], flat(aT[:, u % 2, 0, :, :]),
                                    ALU.subtract).then_inc(S["atl"], 1)
                if (u := tile_at(f, j, IN_HI)) is not None:
                    v.wait_ge(S["htv"], q + u + 1)
                    V.tensor_tensor(flat(hT[:, u % 2, 1, :, :]), PS[:, 6, 0:D], flat(hT[:, u % 2, 0, :, :]),
                                    ALU.subtract).then_inc(S["htl"], 1)
                if (u := tile_at(f, j, HID)) is not None:
                    v.wait_ge(S["rt"], q + u + 1)
                    V.tensor_copy(flat(LG[:, bass.ds(tok(f, u), 1), :]), PS[:, 7, 0:E]).then_inc(S["lgc"], 1)
                    p = u % 2
                    v.wait_ge(S["gu"], q + u + 1)
                    v.wait_ge(S["sgs"], q + u + 1)
                    ch.link(V.scalar_tensor_tensor(av[:, p, :], sg[:, p, :], 1.0, PS[:, 5, :], ALU.add, ALU.mult))
                    V.tensor_tensor(av[:, p, :], av[:, p, :], PS[:, 4, :], ALU.mult).then_inc(S["a"], 1)
                if (u := tile_at(f, j, RES)) is not None:
                    v.wait_ge(S["y3"], q + u + 1)
                    V.tensor_tensor(Rt(f, u), Rt(f, u), PS[:, 7, D:2 * D], ALU.add).then_inc(S["r3"], 1)

            def low_parts(lo, hi, src, n, half):
                V.scalar_tensor_tensor(lo, src, 0.5 if half else 1.0, hi, ALU.mult, ALU.subtract).then_inc(S[n], 1)

            def split_expert(e):
                v.wait_ge(S["wh"], 2 * e + 2)
                if e >= E - 2:
                    v.wait_ge(S["wlg"], E - 2)
                lo, hi = e * EW + KD * 2 * FF, (e + 1) * EW
                low_parts(WRl[:, lo:hi], WRh[:, lo:hi], raw(e)[1][:, 0:KF * D], "wld", True)

            def slot(c, n, j):
                if scanned(c):
                    scan_tile(c, j)
                if n is not None:
                    pro_slot(c, n, j)
                if isinstance(c, int) and c == 0 and j < U * (NC - NC // 2):
                    late, u = NC // 2 + j // U, j % U
                    ch.link(V.tensor_tensor(yb[:, j % 2, :], Ht(late, u), MODA[:, u // TPC, GA, :], ALU.mult))
                    V.tensor_tensor(Rt(late, u), Rt(late, u), yb[:, j % 2, :], ALU.add).then_inc(S["r0l"], 1)
                if there(c - 1, 0):
                    proj_slot(c, c - 1, j)
                ffn_slot(c - 1, j)
                if scanned(c) and j == NA:
                    y_out(c, 0)
                if (e := expert_at(c, j)) is not None:
                    split_expert(e)

            lead(pro_slot, 0)
            front(NC - 1)
            bound_gate(MODB[:, :, GB - 3, :])
            v.wait_ge(S["a0"], 2)
            ch.link(V.tensor_scalar(Apar[:, :], Apar[:, :], -0.001, None, ALU.mult))
            lead(pro_slot, 1)
            v.wait_ge(S["ws"], 16 * (2 * KD + 1))
            for b in range(B):
                V.tensor_tensor(STG_gated[:, b, :].rearrange("p (k d) -> p k d", d=D),
                                STG[:, KD * 2 * FF:EW].rearrange("p (k d) -> p k d", d=D),
                                MODB[:, b:b + 1, GB - 3, :].to_broadcast([P, KF, D]), ALU.mult).then_inc(S["wsg"], 1)
            v.wait_ge(S["wsh"], 2)
            low_parts(WSl[:, 0:KD * 2 * FF], WSh[:, 0:KD * 2 * FF], STG[:, 0:KD * 2 * FF], "wsl", False)
            low_parts(WSl[:, KD * 2 * FF:], WSh[:, KD * 2 * FF:], flat(STG_gated), "wsl", True)
            v.wait_ge(S["r0"], 1)
            lead(pro_slot, 2)
            v.wait_ge(S["wsl"], 2)
            walk(slot, 0, 1)
            walk(slot, 1, 2)
            b0 = ch.n
            per = (4 + 2 + 2 + 2) + NTILE + (2 * U + 1) + U
            with v.Fori(2, NC - 1) as c:
                ch.loop(b0, c - 2, per)
                walk(slot, c, c + 1)
            ch.end(b0, per, NC - 3)
            walk(slot, NC - 1, None)
            walk(slot, NC, None, LAST_SLOTS)

            v.wait_ge(S["a"], NT)
            v.wait_ge(S["r3"], NT)
            v.wait_ge(S["lgc"], NT)
            oh = flat(sg[:, :, :])[:, 0:NT * E].rearrange("p (t e) -> p t e", e=E)
            eq = flat(sg[:, :, :])[:, NT * E:2 * NT * E].rearrange("p (t e) -> p t e", e=E)
            rk = flat(av[:, :, :])[:, 0:NT * E].rearrange("p (t e) -> p t e", e=E)
            cum = flat(av[:, :, :])[:, NT * E:2 * NT * E].rearrange("p (e t) -> p e t", e=E)
            scr = h2s[:, :, :].rearrange("p a d -> p (a d)")
            ch.link(V.tensor_reduce(S1[:, :], LG[:, :, :], axis=AX.X, op=ALU.max))
            v.sem_inc(S["s1"], 1)
            mx = yb[:, 0, 0:NT]
            ch.link(V.tensor_reduce(mx, LG[:, :, :], axis=AX.X, op=ALU.max))
            ch.link(V.tensor_tensor(eq, LG[:, :, :], mx.unsqueeze(2).to_broadcast([P, NT, E]), ALU.is_ge))
            ch.link(V.tensor_tensor(eq, eq, first.unsqueeze(1).to_broadcast([P, NT, E]), ALU.mult))
            ch.link(V.tensor_reduce(mx, eq, axis=AX.X, op=ALU.max))
            ch.link(V.tensor_tensor(oh, eq, mx.unsqueeze(2).to_broadcast([P, NT, E]), ALU.is_equal))
            v.sem_inc(S["oh"], 1)
            v.wait_ge(S["rk"], 1)
            ch.inc(V.tensor_copy(rk.rearrange("p t e -> p (t e)"), PS[:, 0, 0:NT * E]))
            ch.link(V.tensor_copy(cum, PS[:, 1, 0:NT * E].rearrange("p (t e) -> p e t", e=E)))
            inc_ = scr[:, 0:NT * E].rearrange("p (e t) -> p e t", e=E)
            ones_row = one[:, 0:NT]
            for e in range(E):
                ch.inc(V.tensor_tensor_scan(inc_[:, e, :], ones_row, cum[:, e, :], 0.0, ALU.mult, ALU.add))
            ch.wait()
            cmp_ = scr[:, NT * E:2 * NT * E].rearrange("p (e t) -> p e t", e=E)
            nti = yb[:, 0, 64:64 + E]
            ends = yb[:, 0, 80:80 + E]
            offs = yb[:, 0, 96:96 + E]
            ch.link(V.tensor_tensor(cmp_, inc_[:, :, NT - 1:NT].to_broadcast([P, E, NT]), jrow, ALU.is_gt))
            ch.link(V.tensor_reduce(nti, cmp_, axis=AX.X, op=ALU.add))
            ch.link(V.tensor_tensor_scan(ends, one[:, 0:E], nti, 0.0, ALU.mult, ALU.add))
            ch.link(V.tensor_tensor(offs, ends, nti, ALU.subtract))
            ch.link(V.tensor_scalar(offs, offs, float(P), None, ALU.mult))
            ch.link(V.tensor_tensor(inc_, inc_, cum, ALU.subtract))
            ch.link(V.tensor_tensor(inc_, inc_, offs.unsqueeze(2).to_broadcast([P, E, NT]), ALU.add))
            ch.link(V.tensor_tensor(rk, rk, inc_.rearrange("p e t -> p t e"), ALU.add))
            ch.link(V.tensor_tensor(rk, rk, oh, ALU.mult))
            ch.link(V.tensor_reduce(mx, rk, axis=AX.X, op=ALU.add))
            ch.link(V.tensor_copy(posi[:, :], mx))
            ch.link(V.tensor_scalar(ptile[:, :], posi[:, :], 7, None, ALU.logical_shift_right))
            ch.link(V.tensor_scalar(posi[:, :], posi[:, :], P - 1, None, ALU.bitwise_and))
            tl, row = tmp[:, 0, 0:NT], tmp[:, 1, 0:NT]
            ch.inc(V.tensor_copy(tl, ptile[:, :]))
            ch.link(V.tensor_copy(row, posi[:, :]))
            ch.link(V.tensor_tensor(hot_tile[:, :, 1, :], tl.unsqueeze(2).to_broadcast([P, NT, RT]),
                                    jtile.unsqueeze(1).to_broadcast([P, NT, RT]), ALU.is_equal))
            ch.link(V.tensor_tensor(hot_tile[:, :, 0, :], hot_tile[:, :, 1, :],
                                    jtok.unsqueeze(2).to_broadcast([P, NT, RT]), ALU.mult))
            ch.link(V.tensor_scalar(hot_tile[:, :, 1, :], hot_tile[:, :, 1, :], prow, None, ALU.mult))
            for t0, hot in hot_rows:
                n = hot.shape[1]
                V.tensor_tensor(hot, row[:, t0:t0 + n].unsqueeze(2).to_broadcast([P, n, P]),
                                jcol.unsqueeze(1).to_broadcast([P, n, P]), ALU.is_equal).then_inc(S["hot"], 1)
            v.wait_ge(S["tk"], 1)
            who, flag, place = scr[:, 0:2 * RT], scr[:, 128:128 + RT], scr[:, 192:192 + RT]
            ch.link(V.tensor_copy(who, PS[:, 2, 0:2 * RT]))
            ch.inc(V.tensor_scalar(flag, who[:, 0:RT], 0.0, trash, ALU.is_equal, ALU.mult))
            ch.link(V.scalar_tensor_tensor(place, who[:, 0:RT], float(P), who[:, RT:2 * RT], ALU.mult, ALU.add))
            ch.inc(V.scalar_tensor_tensor(flag, place, float(-P), flag, ALU.add, ALU.add))
            ch.link(V.tensor_scalar(place, place, float(-P), 0.0, ALU.add, ALU.max))
            ch.inc(V.tensor_copy(idin[:, :], place))
            ch.link(V.tensor_copy(idout[:, :], flag))
            v.sem_inc(S["ids"], 1)
            ended = flat(av[:, :, :])[:, 2 * NT * E:2 * NT * E + RT * (E - 1)].rearrange("p (r e) -> p r e", e=E - 1)
            ef = yb[:, 1, 0:RT]
            ch.link(V.tensor_tensor(ended, jtile.unsqueeze(2).to_broadcast([P, RT, E - 1]),
                                    ends[:, 0:E - 1].unsqueeze(1).to_broadcast([P, RT, E - 1]), ALU.is_ge))
            ch.link(V.tensor_reduce(ef, ended, axis=AX.X, op=ALU.add))
            ch.link(V.tensor_copy(eidi[:, :], ef))
            v.sem_inc(S["pos"], 1)

            def step5(s, par_):
                if not isinstance(s, int) or s < RT:
                    v.wait_ge(S["htv5"], s + 1)
                    V.tensor_tensor(flat(hT[:, par_, 1, :, :]), PS[:, 2, 0:D], flat(hT[:, par_, 0, :, :]),
                                    ALU.subtract).then_inc(S["htl5"], 1)
                if not isinstance(s, int) or 1 <= s <= RT:
                    p = 1 - par_
                    v.wait_ge(S["sg5"], s)
                    ch.link(V.scalar_tensor_tensor(av[:, p, :], sg[:, p, :], 1.0, PS[:, 4 * p + 1, :], ALU.add, ALU.mult))
                    V.tensor_tensor(av[:, p, :], av[:, p, :], PS[:, 4 * p, :], ALU.mult).then_inc(S["a5"], 1)
                if not isinstance(s, int) or 2 <= s <= RT + 1:
                    v.wait_ge(S["atv5"], s - 1)
                    V.tensor_tensor(flat(aT[:, par_, 1, :, :]), PS[:, 6, :], flat(aT[:, par_, 0, :, :]),
                                    ALU.subtract).then_inc(S["atl5"], 1)
                if not isinstance(s, int) or s >= 3:
                    q = 1 - par_
                    v.wait_ge(S["y5"], s - 2)
                    if not isinstance(s, int) or s >= 5:
                        v.wait_ge(S[f"ysd{q}"], (s - 3) // 2 * 16 if isinstance(s, int) else ysw[0])
                    V.tensor_copy(yb[:, q, :], PS[:, 3, 0:D]).then_inc(S["yb5"], 1)

            ysw = [None]
            for s in range(5):
                step5(s, s % 2)
            b0 = ch.n
            with v.Fori(0, (RT - 5) // 2) as k:
                ch.loop(b0, k, 2)
                for s in range(2):
                    ysw[0] = k * 16 + 16
                    step5(k * 2 + (5 + s), (5 + s) % 2)
            ch.end(b0, 2, (RT - 5) // 2)
            for s in range(RT, RT + 3):
                step5(s, s % 2)
            last_sum(v, V, ch, [k for k in range(NG) if k not in ON_POOL], "fin")

        @block.tensor
        def _(pe):
            T = nc.tensor
            pe.wait_ge(S["cst"], 32)
            pe.wait_ge(S["b0"], 1)
            for b in range(B):
                for j in range(3):
                    for k in range(KD):
                        last = T.matmul(PS[:, 3 * b + j, :], cB[:, k, b, :], WM[:, k, j * CH:(j + 1) * CH],
                                        start=(k == 0), stop=(k == KD - 1))
            last.then_inc(S["m0"], 1)
            pe.wait_ge(S["mev"], 1)
            pe.wait_ge(S["sm"], SMALL[0])
            pe.wait_ge(S["z0"], 1)
            for m in range(3):
                for k in range(KD):
                    T.transpose(PS[:, m // 2, ((m % 2) * KD + k) * P:((m % 2) * KD + k + 1) * P],
                                inR[:, m, k * P:(k + 1) * P], ident)
            for m, n in ((0, SR), (1, SR), (2, B * RK)):
                for X in range(2):
                    j = 2 * m + X
                    T.transpose(PS[:, 2 + j // 4, (j % 4) * P:(j % 4) * P + n], xR[0:n, m, X, :], ident[0:n, 0:n])
            for X in range(2):
                T.transpose(PS[0:B * RK, 3, (2 + X) * P:(3 + X) * P], dtR[:, X, :], ident)
            for m in range(3):
                for k in range(KD):
                    T.transpose(PS[:, 4 + m // 2, ((m % 2) * KD + k) * P:((m % 2) * KD + k + 1) * P],
                                outR[:, k, m, :], ident)
            for k in range(KD):
                last = T.transpose(PS[:, 5, (2 + k) * P:(2 + k) * P + E], rR[0:E, k * P:(k + 1) * P], ident[0:E, 0:E])
            last.then_inc(S["t0"], 1)
            pe.wait_ge(S["e0"], 1)
            for X, ms in ((0, (0, 1)), (1, (2,))):
                j, n = 0, len(ms) * KD
                for m in ms:
                    for k in range(KD):
                        last = T.matmul(PS[:, 7, X:X + 1], winT[:, m, k, :], lnbc[:, k:k + 1],
                                        start=(j == 0), stop=(j == n - 1))
                        j += 1
            last.then_inc(S["w0"], 1)
            pe.wait_ge(S["m1"], 1)

            def front(c):
                for u in range(U):
                    b, i = u // TPC, u % TPC
                    pe.wait_ge(S["z1"], c * U + u + 1)
                    for k in range(KD):
                        last = T.transpose(PS[:, KD * b + k, i * P:(i + 1) * P], z[:, u, k * P:(k + 1) * P], ident)
                    last.then_inc(S["zt"], 1)
                pe.wait_ge(S["zev"], c * B + B)
                for X, ops in ((0, ((0, 0), (1, 1))), (1, ((2, 1),))):
                    j, n = 0, len(ops) * KD
                    for m, b in ops:
                        for k in range(KD):
                            last = T.matmul(PS[:, 4 + X, :], winT[:, m, k, :], zT[:, b, k, :],
                                            start=(j == 0), stop=(j == n - 1))
                            j += 1
                last.then_inc(S["xin"], 1)

            with pe.Fori(0, NC - 1) as c:
                front(c)

            def pro_slot(c, n, j):
                if (k := ITEM.get(j)) is None:
                    return
                if not isinstance(n, int) or n * ITEMS + k >= 1:
                    pe.wait_ge(S["pv"], n * ITEMS + k)
                if c is not None:
                    if (u := tile_at(c - 1, j - 1, HID)) is not None:
                        pe.wait_ge(S["a"], (c - 1) * U + u + 1)
                    if there(c - 1, 0) and j - 1 in PROJ:
                        pe.wait_ge(S["x1"], (c - 1) * U + 2 * PROJ[j - 1] + 2)
                if k < 3:
                    w, r = ((wxBT, SR), (wxCT, SR), (wxDT, B * RK))[k]
                    if k == 0:
                        pe.wait_ge(S["u"], n * 2 + 2)
                    for X in range(2):
                        last = T.matmul(PS[0:r, item_bank(c), :], w[:, X, :], uu(n, X), start=(X == 0), stop=(X == 1))
                else:
                    last = T.matmul(PS[:, item_bank(c), :], wdtT[0:B * RK, k - 3, :], dr[0:B * RK, :], start=True, stop=True)
                last.then_inc(S["pi"], 1)

            def bcast_B(c, i):
                if reused(c, i):
                    pe.wait_ge(S["sc"], c * NTILE + i - 1)
                T.matmul(PS[:, i % 2, :], sel[0:SR, i, :], flat(BsCs[0:SR, bass.ds(c, 1), 0, :]), start=True, stop=True) \
                    .then_inc(S["bb"], 1)

            def bcast_C(c, i):
                if not isinstance(c, int) or c + i >= 1:
                    pe.wait_ge(S["cs"], c * NTILE + i)
                T.matmul(PS[:, 2, :], sel[0:SR, i, :], flat(BsCs[0:SR, bass.ds(c, 1), 1, :]), start=True, stop=True) \
                    .then_inc(S["cb"], 1)

            def sum_states(c, i):
                pe.wait_ge(S["g"], c * NTILE + i + 1)
                if i == 0 and there(c - 1, 0):
                    pe.wait_ge(S["ye"], c * 2)
                if i == NA:
                    pe.wait_ge(S["ye"], c * 2 + 1)
                T.matmul(PS[:, 3, :], ident, g[:, i % 2, :],
                         start=(i in (0, NA)), stop=(i in (NA - 1, NTILE - 1))).then_inc(S["y"], 1)

            def scan_tile(c, n, i):
                if n is not None and i == NTILE - 2:
                    pe.wait_ge(S["bs"], n * 2 + 2)
                if i + 1 < NTILE:
                    bcast_C(c, i + 1)
                elif n is not None:
                    bcast_C(n, 0)
                if i + 2 < NTILE:
                    bcast_B(c, i + 2)
                elif n is not None:
                    bcast_B(n, i + 2 - NTILE)
                if i >= 1:
                    sum_states(c, i - 1)

            def proj_pair(c, f, k):
                bank = proj_bank(c, k)
                if k == 0:
                    pe.wait_ge(S["ye"], f * 2 + 2)
                for u in (2 * k, 2 * k + 1):
                    b, i = u // TPC, u % TPC
                    o = PS[:, bank, (u % 2) * D:(u % 2 + 1) * D]
                    if b == 0:
                        last = T.matmul(o, ysb[:, 0, i * P:(i + 1) * P], woutT[:, 0, :], start=True, stop=True)
                    else:
                        T.matmul(o, ysb[:, 0, i * P:(i + 1) * P], woutT[:, 1, :], start=True, stop=False)
                        last = T.matmul(o, ysb[:, 1, i * P:(i + 1) * P], woutT[:, 2, :], start=False, stop=True)
                    last.then_inc(S["o"], 1)

            def proj_slot(c, f, n, j):
                if (k := PROJ.get(j)) is not None:
                    if k == 0:
                        if n is not None:
                            pe.wait_ge(S["pv"], n * ITEMS)
                    elif n is not None:
                        pe.wait_ge(S["pv"], n * ITEMS + k)
                    else:
                        pe.wait_ge(S["x1"], f * U + 2 * k)
                    if (u := tile_at(f, j, HID)) is not None:
                        pe.wait_ge(S["a"], f * U + u + 1)
                    proj_pair(c, f, k)

            def transposes(bank, src, sname):
                for k in range(KD):
                    last = T.transpose(PS[:, bank, k * P:(k + 1) * P], src[:, k * P:(k + 1) * P], ident)
                last.then_inc(S[sname], 1)

            def product(o, n, lhs, wh, wl):
                for k in range(n):
                    T.matmul(o, lhs[:, 0, k, :], wh(k), start=(k == 0), stop=False)
                    T.matmul(o, lhs[:, 0, k, :], wl(k), start=False, stop=False)
                    last = T.matmul(o, lhs[:, 1, k, :], wh(k), start=False, stop=(k == n - 1))
                return last

            def a_transposes(p, sname):
                for k in range(KF):
                    last = T.transpose(PS[:, 6, k * P:(k + 1) * P], av[:, p, k * P:(k + 1) * P], ident)
                last.then_inc(S[sname], 1)

            def router(p):
                for m in range(KD * 4):
                    last = T.matmul(PS[:, 7, 0:E], hT[:, p, m // 2 % 2, m // 4, :], wrp[:, m % 2, m // 4, :],
                                    start=(m == 0), stop=(m == KD * 4 - 1))
                last.then_inc(S["rt"], 1)

            def ffn_slot(c, f, n, j):
                q = f * U
                if (u := tile_at(f, j, IN_T)) is not None:
                    pe.wait_ge(S["h2"], q + u + 1)
                    if there(f, u - 2):
                        pe.wait_ge(S["atl"], q + u - 1)
                    elif there(f, u - 1):
                        pe.wait_ge(S["htl"], q + u)
                    transposes(6, h2s[:, u % 2, :], "ht")
                if (u := tile_at(f, j, UP)) is not None:
                    if n is not None and j - 1 in ITEM:
                        pe.wait_ge(S["pv"], n * ITEMS + ITEM[j - 1] + 1)
                    elif scanned(c) and j - 2 in PROJ:
                        pe.wait_ge(S["x1"], f * U + 2 * PROJ[j - 2] + 2)
                    product(PS[:, 5, :], KD, hT[:, u % 2], lambda k: wgu(WSh, k, 1), lambda k: wgu(WSl, k, 1)) \
                        .then_inc(S["gu"], 1)
                    if there(f, u - 1):
                        pe.wait_ge(S["lgc"], q + u)
                    if there(f, u - 2):
                        pe.wait_ge(S["r3"], q + u - 1)
                    router(u % 2)
                if (u := tile_at(f, j, GATE)) is not None:
                    pe.wait_ge(S["htl"], q + u + 1)
                    if there(f, u - 1):
                        pe.wait_ge(S["a"], q + u)
                    product(PS[:, 4, :], KD, hT[:, u % 2], lambda k: wgu(WSh, k, 0), lambda k: wgu(WSl, k, 0)) \
                        .then_inc(S["gg"], 1)
                if (u := tile_at(f, j, HID_T)) is not None:
                    pe.wait_ge(S["a"], q + u + 1)
                    if there(f, u + 1):
                        pe.wait_ge(S["htl"], q + u + 2)
                    else:
                        pe.wait_ge(S["atl"], q + u)
                    a_transposes(u % 2, "atp")
                if (u := tile_at(f, j, DOWN)) is not None:
                    pe.wait_ge(S["atl"], q + u + 1)
                    if there(f, u + 1):
                        pe.wait_ge(S["lgc"], q + u + 2)
                    else:
                        pe.wait_ge(S["r3"], q + u)
                    product(PS[:, 7, D:2 * D], KF, aT[:, u % 2], lambda k: wdn(WSh, k, batch(u)),
                            lambda k: wdn(WSl, k, batch(u))) \
                        .then_inc(S["y3"], 1)

            def slot(c, n, j):
                if scanned(c):
                    scan_tile(c, n, j)
                if j == 0 and there(c - 1, 0):
                    sum_states(c - 1, NTILE - 1)
                if not scanned(c) and j < U // 2:
                    proj_pair(c, c - 1, j)
                ffn_slot(c, c - 1, n, j)
                if scanned(c) and there(c - 1, 0):
                    proj_slot(c, c - 1, n, j)
                if n is not None:
                    pro_slot(c, n, j)

            lead(pro_slot, 0)
            front(NC - 1)
            lead(pro_slot, 1)
            lead(pro_slot, 2)
            pe.wait_ge(S["bs"], 2)
            bcast_B(0, 0)
            bcast_B(0, 1)
            bcast_C(0, 0)
            walk(slot, 0, 1)
            pe.wait_ge(S["wsl"], 2)
            walk(slot, 1, 2)
            with pe.Fori(2, NC - 1) as c:
                walk(slot, c, c + 1)
            walk(slot, NC - 1, None)
            walk(slot, NC, None, LAST_SLOTS)
            pe.wait_ge(S["oh"], 1)
            oh = flat(sg[:, :, :])[:, 0:NT * E]
            T.matmul(PS[:, 0, 0:NT * E], ltri, oh, start=True, stop=True)
            T.matmul(PS[:, 1, 0:NT * E], one[:, :], oh, start=True, stop=True).then_inc(S["rk"], 1)
            for t0, hot in hot_rows:
                pe.wait_ge(S["hot"], 1 + (t0 > 0))
                for i in range(hot.shape[1]):
                    t = t0 + i
                    last = T.matmul(PS[:, 2, 0:2 * RT], hot[:, i, :], hot_tile[:, t, :, :].rearrange("p m r -> p (m r)"),
                                    start=(t == 0), stop=(t == NT - 1))
            last.then_inc(S["tk"], 1)
            pe.wait_ge(S["pos"], 1)
            pe.wait_ge(S["wlg"], E)
            pe.wait_ge(S["wld"], E)

            def part(W, e, lo, n):
                return W[:, bass.ds(e * EW + lo, n)]

            def step5(s, par_, k2):
                if not isinstance(s, int) or s < RT:
                    pe.wait_ge(S[f"xt{par_}"], k2 * 16 + 16)
                    if not isinstance(s, int) or s >= 1:
                        pe.wait_ge(S["htl5"], s)
                    transposes(2, tmp[:, par_, :], "ht5")
                if not isinstance(s, int) or 1 <= s <= RT:
                    p = 1 - par_
                    e = pe.value_load(eidi[0:1, bass.ds(s - 1, 1)], min_val=0, max_val=E - 1)
                    pe.wait_ge(S["htl5"], s)
                    if not isinstance(s, int) or s >= 3:
                        pe.wait_ge(S["a5"], s - 2)
                    for half in range(2):
                        last = product(PS[:, 4 * p + half, :], KD, hT[:, p],
                                       lambda k: part(WRh, e, k * 2 * FF + half * FF, FF),
                                       lambda k: part(WRl, e, k * 2 * FF + half * FF, FF))
                    last.then_inc(S["gu5"], 1)
                if not isinstance(s, int) or 2 <= s <= RT + 1:
                    pe.wait_ge(S["a5"], s - 1)
                    if not isinstance(s, int) or s >= 3:
                        pe.wait_ge(S["atl5"], s - 2)
                    a_transposes(par_, "at5")
                if not isinstance(s, int) or s >= 3:
                    e = pe.value_load(eidi[0:1, bass.ds(s - 3, 1)], min_val=0, max_val=E - 1)
                    pe.wait_ge(S["atl5"], s - 2)
                    if not isinstance(s, int) or s >= 4:
                        pe.wait_ge(S["yb5"], s - 3)
                    product(PS[:, 3, 0:D], KF, aT[:, 1 - par_], lambda k: part(WRh, e, KD * 2 * FF + k * D, D),
                            lambda k: part(WRl, e, KD * 2 * FF + k * D, D)).then_inc(S["y5"], 1)

            for s in range(4):
                step5(s, s % 2, s // 2)
            with pe.Fori(0, (RT - 5) // 2) as k:
                for s in range(2):
                    step5(k * 2 + (4 + s), s, k + 2)
            for s in range(RT - 1, RT + 3):
                step5(s, s % 2, s // 2)


_INS = ["L0_attn_feat_patch", "L0_attn_ln_w", "L0_attn_ln_b", "L0_attn_in_proj_W", "L0_attn_conv_w", "L0_attn_conv_b",
        "L0_attn_x_proj_W", "L0_attn_dt_proj_W", "L0_attn_dt_proj_b", "L0_attn_A_log", "L0_attn_D_param",
        "L0_attn_out_proj_W", "L0_ffn_router_w", "L0_ffn_gate_up_proj", "L0_ffn_down_proj", "L0_ffn_shared_gate_w",
        "L0_ffn_shared_up_w", "L0_ffn_shared_down_w", "L0_c", "L0_wmod"]


def _consts():
    import numpy as np
    ident = np.eye(P, dtype=np.float32)
    ltri = np.triu(np.ones((P, P), np.float32), 1)
    jrow = np.broadcast_to(np.tile(np.arange(NT, dtype=np.float32) * P, E), (P, E * NT))
    jtile = np.broadcast_to(np.arange(RT, dtype=np.float32), (P, RT))
    jcol = np.broadcast_to(np.arange(P, dtype=np.float32), (P, P))
    jtok = np.broadcast_to(np.arange(1, NT + 1, dtype=np.float32), (P, NT))
    prow = np.arange(P, dtype=np.float32).reshape(P, 1)
    cst = np.concatenate([ident, ltri, jrow, jtile, jcol, jtok, prow, prow + NT * P + P,
                          np.broadcast_to(np.arange(E, 0, -1, dtype=np.float32), (P, E))], 1)
    sel = np.zeros((3, B, NS, NTILE, P), np.float32)
    for n in range(NA):
        sel[:, 0, n, n, 0:DI] = 1
        sel[:, 1, n, n, DI:P] = 1
    for m in range(NB):
        sel[:, 1, m, NA + m, 0:D1B] = 1
        sel[:, 1, m + NB, NA + m, D1B:P] = 1
    return np.ascontiguousarray(cst), sel.reshape(SR, NTILE * P)


def kernel(**inputs):
    import numpy as np
    import concourse.bacc as bacc
    from concourse.bass_utils import run_bass_kernel_spmd
    nc = bacc.Bacc("TRN2", target_bir_lowering=False, num_devices=1)
    arrays = {f"in_{n}": np.ascontiguousarray(inputs[n]) for n in _INS}
    arrays["in_consts"], arrays["in_sel"] = _consts()
    args = [nc.dram_tensor(n, a.shape, mybir.dt.from_np(a.dtype), kind="ExternalInput").ap() for n, a in arrays.items()]
    o = nc.dram_tensor("out_0", (B, L, D), F32, kind="ExternalOutput").ap()
    adaln_block(nc, *args, o)
    r = run_bass_kernel_spmd(nc, [arrays], core_ids=[0])
    return r.results[0]["out_0"]
```
